# Optimizing a Trainium2 kernel written in Bass

```python
import numpy as np
import jax
import jax.numpy as jnp

def _softmax(x, axis=-1):
    return jax.nn.softmax(x, axis=axis)

def _gelu(x):
    return jax.nn.gelu(x, approximate=True)

def _silu(x):
    return jax.nn.silu(x)

def _sigmoid(x):
    return jax.nn.sigmoid(x)

def _layernorm(x, axis=-1, eps=1e-05):
    m = jnp.mean(x, axis=axis, keepdims=True)
    v = jnp.var(x, axis=axis, keepdims=True)
    return (x - m) / jnp.sqrt(v + eps)

def _scatter_add(tgt, idx, src, axis=0):
    return tgt.at[idx].add(src)

def _segment_sum(src, seg, n):
    return jax.ops.segment_sum(src, seg, n)
kernel_name = 'mk_vit_tower_cls_d1_tok_img256_r4_0359fe'

def setup_inputs(seed: int=0):
    np.random.seed(seed)
    _w = jnp.asarray

    def _rec_inputs():
        import jax
        import jax.numpy as jnp
        _rk = jax.random.key(seed)
        x = -7.10856e-05 + 0.999911 * jax.random.normal(jax.random.fold_in(_rk, 1), (64, 1, 96, 96), jnp.float32)
        cls_tok = 0.02 * jax.random.normal(jax.random.fold_in(_rk, 5), (1, 1, 64), jnp.float32)
        return (x, cls_tok)
    x, cls_tok = _rec_inputs()

    def _L0_tok_setup():
        import jax, jax.numpy as jnp
        import numpy as np
        INV_SQRT2 = 0.7071067811865476

        def haar_dwt2(x):
            lo = (x[..., ::2] + x[..., 1::2]) * INV_SQRT2
            hi = (x[..., ::2] - x[..., 1::2]) * INV_SQRT2
            cA = (lo[..., ::2, :] + lo[..., 1::2, :]) * INV_SQRT2
            cH = (lo[..., ::2, :] - lo[..., 1::2, :]) * INV_SQRT2
            cV = (hi[..., ::2, :] + hi[..., 1::2, :]) * INV_SQRT2
            cD = (hi[..., ::2, :] - hi[..., 1::2, :]) * INV_SQRT2
            return (cA, (cH, cV, cD))

        def wavedec2_maps(x, levels):
            a = x
            details = []
            for _ in range(levels):
                a, d = haar_dwt2(a)
                details.append(d)
            maps = [a]
            for d in reversed(details):
                maps.extend(d)
            return maps
        key = jax.random.key(seed)
        k1, k2 = jax.random.split(key)
        B, H, W_img = (64, 256, 256)
        x = jax.random.normal(k1, (B, 1, H, W_img), dtype=jnp.float32)
        n_maps = 1 + 3 * 2
        W = jax.random.normal(k2, (n_maps, 64), dtype=jnp.float32) * (1.0 / np.sqrt(n_maps))
        b = jnp.zeros((64,), dtype=jnp.float32)
        return {'x': x, 'W': W, 'b': b}
    _L0_tok_all = _L0_tok_setup()
    _L0_tok_in = {k: v for k, v in _L0_tok_all.items() if k in ('W', 'b')}
    del _L0_tok_all

    def _L0_attn_setup():
        import jax, jax.numpy as jnp
        import numpy as np
        B_SZ, T, H, N, L = (4, 128, 64, 64, 4)
        EPS = 1e-05

        def _hippo(n):
            i = np.arange(n)[:, None]
            j = np.arange(n)[None, :]
            A = np.where(i >= j, (-1.0) ** (i - j) * np.sqrt((2 * i + 1.0) * (2 * j + 1.0)), 0.0)
            A = A / (1.1 * np.linalg.norm(A, 2))
            return A.astype(np.float32)

        def _xavier(key, shape):
            fan_in, fan_out = (shape[1], shape[0])
            a = float(np.sqrt(6.0 / (fan_in + fan_out)))
            return jax.random.uniform(key, shape, jnp.float32, -a, a)

        def _ln(x):
            m = jnp.mean(x, -1, keepdims=True)
            v = jnp.mean((x - m) ** 2, -1, keepdims=True)
            return (x - m) / jnp.sqrt(v + EPS)

        def _ssm_layer(h, A, B, C, D):
            Cbar = C.mean(0)
            BT = B.T
            DT = D.T

            def step(state, u):
                y = jnp.einsum('bnh,n->bh', state, Cbar) + u @ DT
                new_state = jnp.einsum('nm,bmh->bnh', A, state) + (u @ BT)[:, :, None]
                return (new_state, y)
            state0 = jnp.zeros((h.shape[0], A.shape[0], h.shape[2]), h.dtype)
            _, ys = jax.lax.scan(step, state0, jnp.swapaxes(h, 0, 1))
            y = jnp.swapaxes(ys, 0, 1)
            y = jax.nn.gelu(y, approximate=False) + h
            return _ln(y)
        key = jax.random.key(seed)
        ks = jax.random.split(key, 8)
        x = jax.random.normal(ks[0], (B_SZ, T, H), jnp.float32)
        A = jnp.broadcast_to(jnp.asarray(_hippo(N)), (L, N, N))
        Bm = jnp.stack([_xavier(jax.random.fold_in(ks[1], l), (N, H)) for l in range(L)])
        Cm = jnp.stack([_xavier(jax.random.fold_in(ks[2], l), (H, N)) for l in range(L)])
        Dm = jnp.stack([_xavier(jax.random.fold_in(ks[3], l), (H, H)) for l in range(L)])
        Win = _xavier(ks[4], (H, H))
        bin_ = jnp.zeros((H,), jnp.float32)
        Wout = _xavier(ks[5], (H, H))
        bout = jnp.zeros((H,), jnp.float32)
        return {'x': x, 'Win': Win, 'bin_': bin_, 'Wout': Wout, 'bout': bout, 'A': A, 'Bm': Bm, 'Cm': Cm, 'Dm': Dm}
    _L0_attn_all = _L0_attn_setup()
    _L0_attn_in = {k: v for k, v in _L0_attn_all.items() if k in ('Win', 'bin_', 'Wout', 'bout', 'A', 'Bm', 'Cm', 'Dm')}
    del _L0_attn_all

    def _L0_ffn_setup():
        import jax, jax.numpy as jnp
        import numpy as np
        B, N, D = (16, 1024, 64)
        NUM_EXPERTS, TOP_K, HEADS = (4, 2, 4)
        N_EDGES = 262144
        LN_EPS = 1e-05

        def _layernorm(x, g, b):
            mu = x.mean(-1, keepdims=True)
            var = ((x - mu) ** 2).mean(-1, keepdims=True)
            return (x - mu) * jax.lax.rsqrt(var + LN_EPS) * g + b

        def _forward(x, edge_index, W_gat, att_src, att_dst, b_gat, ln_gamma, ln_beta, W1, b1, W2, b2):
            Bc, Nc, Dc = x.shape
            M = Bc * Nc
            x_flat = x.reshape(M, Dc)
            h = (x_flat @ W_gat).reshape(M, HEADS, NUM_EXPERTS)
            loops = jnp.arange(M, dtype=edge_index.dtype)
            src = jnp.concatenate([edge_index[0], loops])
            dst = jnp.concatenate([edge_index[1], loops])
            a_src = (h * att_src).sum(-1)
            a_dst = (h * att_dst).sum(-1)
            e = jax.nn.leaky_relu(a_src[src] + a_dst[dst], negative_slope=0.2)
            e_max = jax.ops.segment_max(e, dst, num_segments=M)
            ee = jnp.exp(e - e_max[dst])
            denom = jax.ops.segment_sum(ee, dst, num_segments=M)
            alpha = ee / (denom[dst] + 1e-16)
            msg = h[src] * alpha[:, :, None]
            agg = jax.ops.segment_sum(msg, dst, num_segments=M).reshape(M, HEADS * NUM_EXPERTS) + b_gat
            scores = _layernorm(agg, ln_gamma, ln_beta).reshape(M, HEADS, NUM_EXPERTS).mean(1)
            scores = scores.reshape(Bc, Nc, NUM_EXPERTS)
            topk_s, topk_i = jax.lax.top_k(scores, TOP_K)
            w = jax.nn.softmax(topk_s, axis=-1)
            out = jnp.zeros_like(x)
            for ei in range(NUM_EXPERTS):
                g = jnp.where(topk_i == ei, w, 0.0).sum(-1)
                hh = jax.nn.gelu(x @ W1[ei] + b1[ei], approximate=False)
                out = out + g[..., None] * (hh @ W2[ei] + b2[ei])
            return out
        key = jax.random.key(seed)
        ks = jax.random.split(key, 8)
        s = 0.05
        return {'x': jax.random.normal(ks[0], (B, N, D), jnp.float32), 'W_gat': jax.random.normal(ks[1], (D, HEADS * NUM_EXPERTS), jnp.float32) * s, 'att_src': jax.random.normal(ks[2], (HEADS, NUM_EXPERTS), jnp.float32) * s, 'att_dst': jax.random.normal(ks[3], (HEADS, NUM_EXPERTS), jnp.float32) * s, 'b_gat': jnp.zeros((HEADS * NUM_EXPERTS,), jnp.float32), 'ln_gamma': jnp.ones((HEADS * NUM_EXPERTS,), jnp.float32), 'ln_beta': jnp.zeros((HEADS * NUM_EXPERTS,), jnp.float32), 'W1': jax.random.normal(ks[4], (NUM_EXPERTS, D, 2 * D), jnp.float32) * s, 'b1': jnp.zeros((NUM_EXPERTS, 2 * D), jnp.float32), 'W2': jax.random.normal(ks[5], (NUM_EXPERTS, 2 * D, D), jnp.float32) * s, 'b2': jnp.zeros((NUM_EXPERTS, D), jnp.float32), 'edge_index': jax.random.randint(ks[6], (2, N_EDGES), 0, B * N, jnp.int32)}
    _L0_ffn_all = _L0_ffn_setup()
    _L0_ffn_in = {k: v for k, v in _L0_ffn_all.items() if k in ('W_gat', 'att_src', 'att_dst', 'b_gat', 'ln_gamma', 'ln_beta', 'W1', 'b1', 'W2', 'b2', 'edge_index')}
    del _L0_ffn_all
    return {'x': x, 'cls_tok': cls_tok, 'L0_tok_W': _L0_tok_in['W'], 'L0_tok_b': _L0_tok_in['b'], 'L0_attn_Win': _L0_attn_in['Win'], 'L0_attn_bin_': _L0_attn_in['bin_'], 'L0_attn_Wout': _L0_attn_in['Wout'], 'L0_attn_bout': _L0_attn_in['bout'], 'L0_attn_A': _L0_attn_in['A'], 'L0_attn_Bm': _L0_attn_in['Bm'], 'L0_attn_Cm': _L0_attn_in['Cm'], 'L0_attn_Dm': _L0_attn_in['Dm'], 'L0_ffn_W_gat': _L0_ffn_in['W_gat'], 'L0_ffn_att_src': _L0_ffn_in['att_src'], 'L0_ffn_att_dst': _L0_ffn_in['att_dst'], 'L0_ffn_b_gat': _L0_ffn_in['b_gat'], 'L0_ffn_ln_gamma': _L0_ffn_in['ln_gamma'], 'L0_ffn_ln_beta': _L0_ffn_in['ln_beta'], 'L0_ffn_W1': _L0_ffn_in['W1'], 'L0_ffn_b1': _L0_ffn_in['b1'], 'L0_ffn_W2': _L0_ffn_in['W2'], 'L0_ffn_b2': _L0_ffn_in['b2'], 'L0_ffn_edge_index': _L0_ffn_in['edge_index']}

def reference(x, cls_tok, L0_tok_W, L0_tok_b, L0_attn_Win, L0_attn_bin_, L0_attn_Wout, L0_attn_bout, L0_attn_A, L0_attn_Bm, L0_attn_Cm, L0_attn_Dm, L0_ffn_W_gat, L0_ffn_att_src, L0_ffn_att_dst, L0_ffn_b_gat, L0_ffn_ln_gamma, L0_ffn_ln_beta, L0_ffn_W1, L0_ffn_b1, L0_ffn_W2, L0_ffn_b2, L0_ffn_edge_index):
    import jax
    import jax.numpy as jnp

    def _L0_tok_ref(x, W, b):
        import jax, jax.numpy as jnp
        import numpy as np
        INV_SQRT2 = 0.7071067811865476

        def haar_dwt2(x):
            lo = (x[..., ::2] + x[..., 1::2]) * INV_SQRT2
            hi = (x[..., ::2] - x[..., 1::2]) * INV_SQRT2
            cA = (lo[..., ::2, :] + lo[..., 1::2, :]) * INV_SQRT2
            cH = (lo[..., ::2, :] - lo[..., 1::2, :]) * INV_SQRT2
            cV = (hi[..., ::2, :] + hi[..., 1::2, :]) * INV_SQRT2
            cD = (hi[..., ::2, :] - hi[..., 1::2, :]) * INV_SQRT2
            return (cA, (cH, cV, cD))

        def wavedec2_maps(x, levels):
            a = x
            details = []
            for _ in range(levels):
                a, d = haar_dwt2(a)
                details.append(d)
            maps = [a]
            for d in reversed(details):
                maps.extend(d)
            return maps
        imgs = x[:, 0]
        B = imgs.shape[0]
        maps = wavedec2_maps(imgs, 2)
        proc = [jax.image.resize(m, (B, 8, 8), method='bilinear') for m in maps]
        feat = jnp.stack(proc, axis=1)
        feat = feat.reshape(B, feat.shape[1], 64).transpose(0, 2, 1)
        return feat @ W + b

    def _L0_attn_ref(x, Win, bin_, Wout, bout, A, Bm, Cm, Dm):
        import jax, jax.numpy as jnp
        import numpy as np
        B_SZ, T, H, N, L = (4, 128, 64, 64, 4)
        EPS = 1e-05

        def _hippo(n):
            i = np.arange(n)[:, None]
            j = np.arange(n)[None, :]
            A = np.where(i >= j, (-1.0) ** (i - j) * np.sqrt((2 * i + 1.0) * (2 * j + 1.0)), 0.0)
            A = A / (1.1 * np.linalg.norm(A, 2))
            return A.astype(np.float32)

        def _xavier(key, shape):
            fan_in, fan_out = (shape[1], shape[0])
            a = float(np.sqrt(6.0 / (fan_in + fan_out)))
            return jax.random.uniform(key, shape, jnp.float32, -a, a)

        def _ln(x):
            m = jnp.mean(x, -1, keepdims=True)
            v = jnp.mean((x - m) ** 2, -1, keepdims=True)
            return (x - m) / jnp.sqrt(v + EPS)

        def _ssm_layer(h, A, B, C, D):
            Cbar = C.mean(0)
            BT = B.T
            DT = D.T

            def step(state, u):
                y = jnp.einsum('bnh,n->bh', state, Cbar) + u @ DT
                new_state = jnp.einsum('nm,bmh->bnh', A, state) + (u @ BT)[:, :, None]
                return (new_state, y)
            state0 = jnp.zeros((h.shape[0], A.shape[0], h.shape[2]), h.dtype)
            _, ys = jax.lax.scan(step, state0, jnp.swapaxes(h, 0, 1))
            y = jnp.swapaxes(ys, 0, 1)
            y = jax.nn.gelu(y, approximate=False) + h
            return _ln(y)
        h = x @ Win.T + bin_
        for l in range(L):
            h = _ssm_layer(h, A[l], Bm[l], Cm[l], Dm[l])
        h = _ln(h)
        return h @ Wout.T + bout

    def _L0_ffn_ref(x, W_gat, att_src, att_dst, b_gat, ln_gamma, ln_beta, W1, b1, W2, b2, edge_index):
        import jax, jax.numpy as jnp
        import numpy as np
        B, N, D = (16, 1024, 64)
        NUM_EXPERTS, TOP_K, HEADS = (4, 2, 4)
        N_EDGES = 262144
        LN_EPS = 1e-05

        def _layernorm(x, g, b):
            mu = x.mean(-1, keepdims=True)
            var = ((x - mu) ** 2).mean(-1, keepdims=True)
            return (x - mu) * jax.lax.rsqrt(var + LN_EPS) * g + b

        def _forward(x, edge_index, W_gat, att_src, att_dst, b_gat, ln_gamma, ln_beta, W1, b1, W2, b2):
            Bc, Nc, Dc = x.shape
            M = Bc * Nc
            x_flat = x.reshape(M, Dc)
            h = (x_flat @ W_gat).reshape(M, HEADS, NUM_EXPERTS)
            loops = jnp.arange(M, dtype=edge_index.dtype)
            src = jnp.concatenate([edge_index[0], loops])
            dst = jnp.concatenate([edge_index[1], loops])
            a_src = (h * att_src).sum(-1)
            a_dst = (h * att_dst).sum(-1)
            e = jax.nn.leaky_relu(a_src[src] + a_dst[dst], negative_slope=0.2)
            e_max = jax.ops.segment_max(e, dst, num_segments=M)
            ee = jnp.exp(e - e_max[dst])
            denom = jax.ops.segment_sum(ee, dst, num_segments=M)
            alpha = ee / (denom[dst] + 1e-16)
            msg = h[src] * alpha[:, :, None]
            agg = jax.ops.segment_sum(msg, dst, num_segments=M).reshape(M, HEADS * NUM_EXPERTS) + b_gat
            scores = _layernorm(agg, ln_gamma, ln_beta).reshape(M, HEADS, NUM_EXPERTS).mean(1)
            scores = scores.reshape(Bc, Nc, NUM_EXPERTS)
            topk_s, topk_i = jax.lax.top_k(scores, TOP_K)
            w = jax.nn.softmax(topk_s, axis=-1)
            out = jnp.zeros_like(x)
            for ei in range(NUM_EXPERTS):
                g = jnp.where(topk_i == ei, w, 0.0).sum(-1)
                hh = jax.nn.gelu(x @ W1[ei] + b1[ei], approximate=False)
                out = out + g[..., None] * (hh @ W2[ei] + b2[ei])
            return out
        return _forward(x, edge_index, W_gat, att_src, att_dst, b_gat, ln_gamma, ln_beta, W1, b1, W2, b2)
    h = _L0_tok_ref(x, L0_tok_W, L0_tok_b)
    h = jnp.concatenate([jnp.broadcast_to(cls_tok, (h.shape[0], 1, h.shape[2])), h], axis=1)
    h = h + _L0_attn_ref(_layernorm(h, axis=-1), L0_attn_Win, L0_attn_bin_, L0_attn_Wout, L0_attn_bout, L0_attn_A, L0_attn_Bm, L0_attn_Cm, L0_attn_Dm)
    h = h + _L0_ffn_ref(_layernorm(h, axis=-1), L0_ffn_W_gat, L0_ffn_att_src, L0_ffn_att_dst, L0_ffn_b_gat, L0_ffn_ln_gamma, L0_ffn_ln_beta, L0_ffn_W1, L0_ffn_b1, L0_ffn_W2, L0_ffn_b2, L0_ffn_edge_index)
    return h

_drawn_inputs = setup_inputs


def setup_inputs(seed=0):
    import zlib

    import numpy as np

    out = dict(_drawn_inputs(seed))
    spreads = {'L0_tok_b': (0.0, 0.1),
     'L0_attn_bin_': (0.0, 0.1),
     'L0_attn_bout': (0.0, 0.1),
     'L0_ffn_b_gat': (0.0, 0.8),
     'L0_ffn_ln_gamma': (1.0, 0.6),
     'L0_ffn_ln_beta': (0.0, 0.8),
     'L0_ffn_b1': (0.0, 0.333),
     'L0_ffn_b2': (0.0, 0.1)}
    factors = {'L0_ffn_att_src': 64.0, 'L0_ffn_att_dst': 64.0}
    for name, (base, spread) in spreads.items():
        noise = np.random.default_rng([zlib.crc32(name.encode()), seed]).standard_normal(out[name].shape)
        drawn = base * np.exp(spread * noise) if base else spread * noise
        out[name] = jnp.asarray(drawn.astype(out[name].dtype))
    for name, factor in factors.items():
        out[name] = (out[name] * factor).astype(out[name].dtype)
    return out
```

```python
from contextlib import ExitStack

import numpy as np
import concourse.bass as bass
from concourse import mybir

F32 = mybir.dt.float32
BF16 = mybir.dt.bfloat16
I32 = mybir.dt.int32
U32 = mybir.dt.uint32
ALU = mybir.AluOpType
ACT = mybir.ActivationFunctionType
X = mybir.AxisListType.X

P = 128
IMAGES, SIDE = 64, 96
TOK, H = 65, 64
NODES = IMAGES * TOK
SLOTS = 33
PAIRS = 17
LAYERS = 4
HEADS, EXPERTS, HE = 4, 4, 16
HID = 128
EDGES = 262144
ECOL = EDGES // P
EPS = 1e-5
NF = 24
NODE_ROWS = P * SLOTS
BLK = 16
KEY0 = NODES // 2
DEAD = -4.0e9
LIVE = -1.0e8
ROW = 64
CROWS = 3
CW = CROWS * ROW
LIST_ROWS = EDGES // ROW + P + 8
LAST_ROW = LIST_ROWS - 1
FAR = 1.0e6
DHI, DLO = 65, 64


def wavelet_operator():
    def resize(n):
        s = n / 8.0
        at = (np.arange(8) + 0.5) * s - 0.5
        w = np.maximum(0.0, 1.0 - np.abs(at[:, None] - np.arange(n)[None, :]) / s)
        return w / w.sum(1, keepdims=True)

    def haar(n, sign):
        m = np.zeros((n // 2, n))
        m[np.arange(n // 2), 2 * np.arange(n // 2)] = 0.7071067811865476
        m[np.arange(n // 2), 2 * np.arange(n // 2) + 1] = sign * 0.7071067811865476
        return m

    lo1, hi1, lo2, hi2 = haar(96, 1), haar(96, -1), haar(48, 1), haar(48, -1)
    rows = [resize(24) @ lo2 @ lo1, resize(24) @ hi2 @ lo1, resize(48) @ lo1, resize(48) @ hi1]
    return np.ascontiguousarray(np.concatenate(rows).T.astype(np.float32))


MAPS = [(0, 0), (1, 0), (0, 1), (1, 1), (3, 2), (2, 3), (3, 3)]


def constants():
    eye = np.eye(P, dtype=np.float32)
    before = np.triu(np.ones((P, P), np.float32), 1)
    pick = np.zeros((32, 8), np.float32)
    pick[np.arange(32), np.arange(32) % 8] = 1
    wave = wavelet_operator()
    order = [8 * g + 4 * q + i for g in range(4) for i in range(4) for q in range(2)]
    return {"c_eye": eye, "c_before": before, "c_pick": pick, "c_wave": wave,
            "c_waver": np.ascontiguousarray(wave[:, order])}


def tower(nc, x, cls_tok, tok_W, tok_b, Win, bin_, Wout, bout, A, Bm, Cm, Dm, W_gat, att_src, att_dst,
          b_gat, ln_gamma, ln_beta, W1, b1, W2, b2, edge_index, c_eye, c_before, c_pick, c_wave, c_waver, out,
          dbg=None):
    with ExitStack() as ctx:
        def sb(name, shape, dt=F32):
            return ctx.enter_context(nc.sbuf_tensor(name, shape, dt))

        def ps(name, shape, dt=F32):
            return ctx.enter_context(nc.psum_tensor(name, shape, dt))

        def sem(name):
            return ctx.enter_context(nc.semaphore(name))

        def rep(ap, n):
            return ap.rearrange("(a f) -> a f", a=1).broadcast_to([n, ap.shape[0]])

        def cut(flat):
            at = [0]

            def take(parts, *shape):
                n = int(np.prod(shape))
                ap = flat[0:parts, at[0]:at[0] + n]
                at[0] += n
                assert at[0] <= flat.shape[1]
                names = "abcd"[:len(shape)]
                if len(shape) == 1:
                    return ap
                return ap.rearrange(f"p ({' '.join(names)}) -> p {' '.join(names)}",
                                    **dict(zip(names[1:], shape[1:])))
            return take

        node_tab = nc.dram_tensor("node_tab", [NODE_ROWS, NF], F32).ap()
        edge_list = nc.dram_tensor("edge_list", [LIST_ROWS * ROW, 1], F32).ap()
        edge_rows = edge_list.rearrange("(r c) a -> r (c a)", c=ROW)
        scan_tab = nc.dram_tensor("scan_tab", [P * CW, NF], F32).ap()
        last_tab = nc.dram_tensor("last_tab", [NODE_ROWS], F32).ap()
        gate_tab = nc.dram_tensor("gate_tab", [NODE_ROWS, EXPERTS], F32).ap()

        eye = sb("eye", [P, P])
        before = sb("before", [P, P])
        pick = sb("pick", [32, 8])
        wave = sb("wave", [SIDE, 32])
        waver = sb("waver", [SIDE, 32])
        tokb = sb("tokb", [P, H])
        wlin = sb("wlin", [P, 6, P])
        binr = sb("binr", [P, H])
        boutr = sb("boutr", [P, H])
        mean64 = sb("mean64", [H, 1])
        conv = sb("conv", [P, LAYERS, 132])
        early = sb("early", [P, IMAGES * (SIDE + 32) + 2048])
        xs = early[0:SIDE, 0:IMAGES * SIDE].rearrange("p (b c) -> p b c", c=SIDE)
        y1 = early[0:SIDE, IMAGES * SIDE:IMAGES * (SIDE + 32)].rearrange("p (b m) -> p b m", m=32)
        y2 = early[0:32, IMAGES * (SIDE + 32):].rearrange("p (m b) -> p m b", b=IMAGES)
        place_f = early[:, 0:SLOTS * CW]
        place_m = early[:, SLOTS * CW:SLOTS * CW * 3 // 2].bitcast(BF16)
        scans = early[:, 0:CW * NF].rearrange("p (l f) -> p l f", f=NF)
        ye = sb("ye", [P, EXPERTS, SLOTS, H])
        prep_room = cut(ye[:, :, :, :].rearrange("p e s h -> p (e s h)"))
        tokwd = prep_room(32, 4, 8, H)
        win2 = prep_room(P, 6, P)
        a_pow = prep_room(H, 2, LAYERS, H)
        a_powT = prep_room(H, 2, LAYERS, H)
        bm = prep_room(H, LAYERS, 2, H)
        cm = prep_room(H, LAYERS, H)
        vee = prep_room(H, LAYERS, H)
        zeros = prep_room(P, 529)
        tokw = prep_room(32, 4, H)
        rows64r = prep_room(P, P)
        before64 = prep_room(P, P)
        h0 = sb("h0", [P, SLOTS, H])
        u = sb("u", [P, SLOTS, H])
        xc = sb("xc", [P, SLOTS, H])
        sq = sb("sq", [P, SLOTS, H])
        s1 = sb("s1", [P, SLOTS])
        s2 = sb("s2", [P, SLOTS])
        s3 = sb("s3", [P, SLOTS])
        uT = sb("uT", [P, PAIRS, P])
        yrow = sb("yrow", [P, 32])
        yfar = sb("yfar", [P, 32])
        late = sb("late", [P, 4 * ECOL])
        raw = late[:, 0:2 * ECOL].bitcast(I32).rearrange("p (a e) -> p a e", a=2)
        srcf = late[:, 2 * ECOL:3 * ECOL]
        etmp = late[:, 3 * ECOL:4 * ECOL]
        gath = late[:, 0:CW * NF].rearrange("p (l f) -> p l f", f=NF)
        key = sb("key", [P, ECOL])
        hcode = sb("hcode", [P, 2, ECOL], BF16)
        cls_tab = sb("cls_tab", [P, ECOL])
        rank_tab = cls_tab[:, :].bitcast(U32)
        lkey_tab = sb("lkey_tab", [P, ECOL])
        late_room = cut(late[:, CW * NF:])
        adst, eh, mh, rh = (late_room(P, HEADS, CW) for _ in range(4))
        tabs_c, tabs_l = cut(cls_tab[:, :]), cut(lkey_tab[:, :])
        xh_a, xh_b = tabs_c(P, HE // 2, CW), tabs_l(P, HE // 2, CW)
        wh = cut(early[:, CW * NF:])(P, HEADS, CW)
        key_room = cut(key[:, :])
        chunk, skey, place, keep, ctmp = (key_room(P, CW) for _ in range(5))
        seg = key_room(P, SLOTS, NF)
        xc_room = cut(xc[:, :, :].rearrange("p s h -> p (s h)"))
        nn, st = xc_room(P, SLOTS, NF), xc_room(P, SLOTS, NF)
        sq_room = cut(sq[:, :, :].rearrange("p s h -> p (s h)"))
        n16, nt = sq_room(P, 2, SLOTS, HE), sq_room(P, SLOTS, NF)
        u_room = cut(u[:, :, :].rearrange("p s h -> p (s h)"))
        n4, gates, gtok = u_room(P, 8, SLOTS, HEADS), u_room(P, SLOTS, EXPERTS), u_room(P, SLOTS, EXPERTS)
        lastc = u_room(P, SLOTS)
        iota = sb("iota", [P, CW])
        iota_b = sb("iota_b", [P, P], BF16)
        top = sb("top", [P, BLK])
        cw = sb("cw", [P, 6, BLK])
        oh = sb("oh", [P, BLK, P], BF16)
        hidT = oh[:, :, :].rearrange("p j c -> p (j c)").bitcast(F32).rearrange("p (b n) -> p b n", b=2)
        hoh = sb("hoh", [P, 2, BLK, DHI + DLO], BF16)
        ones_b = sb("ones_b", [P, 1], BF16)
        zero_b = sb("zero_b", [P, 1], BF16)
        before_b = sb("before_b", [P, P], BF16)
        after_b = sb("after_b", [P, P], BF16)
        junk = sb("junk", [P, P])
        ecnt = sb("ecnt", [P, 8])
        ctl = sb("ctl", [1, 4], I32)
        rows64 = sb("rows64", [P, 1], I32)
        ring_i = sb("ring_i", [P, 2, BLK // 2], U32)
        ring_k = sb("ring_k", [P, 2, BLK // 2])
        wg2 = sb("wg2", [P, 2, HE])
        att = sb("att", [P, 2, HE])
        lastr = sb("lastr", [P, NF])
        hsum = sb("hsum", [DHI, DLO])
        rowi = sb("rowi", [P, CROWS], U32)
        rowf = sb("rowf", [P, CROWS])
        srci = sb("srci", [P, CW], U32)
        ends = sb("ends", [P, SLOTS + 1])
        endi = sb("endi", [P, SLOTS], U32)
        has = sb("has", [P, SLOTS])
        gamr = sb("gamr", [P, 3, HE])
        w1 = sb("w1", [P, EXPERTS, HID])
        w2 = sb("w2", [HID, EXPERTS, H])
        b1c = sb("b1c", [HID, EXPERTS])
        b2r = sb("b2r", [P, EXPERTS, H])

        wide = ps("wide", [P, 5 * 512])
        bank5 = ps("bank5", [P, 512])
        bank6 = ps("bank6", [P, 512])
        bank7 = ps("bank7", [P, 512])
        wtok = wide[:, 0:SLOTS * H].rearrange("p (s h) -> p s h", h=H)

        c_in = sem("const_loaded")
        w_in = sem("weights_loaded")
        x_in = [sem(f"x_loaded{i}") for i in range(4)]
        zero_ok = sem("weight_tiles_zeroed")
        tokwd_ok = sem("token_weights_spread")
        x_rows = sem("rows_mapped")
        x_rows_out = sem("rows_evacuated")
        x_cols = sem("columns_mapped")
        x_cols_out = sem("columns_evacuated")
        tok_mm = sem("tokens_multiplied")
        tok_out = sem("tokens_evacuated")
        prep_mm = sem("prep_products")
        prep_ev = sem("prep_evacuated")
        u_ok = sem("normed_ready")
        t_mm = sem("transposed")
        t_ev = sem("transposed_evacuated")
        y_mm = sem("mixed")
        y_ok = sem("mixed_summed")
        g_ok = sem("gelu_done")
        var_ok = sem("variance_ready")
        rt_ok = sem("root_ready")
        d_out = sem("output_stored")
        e_in = sem("edges_loaded")
        pool_passed = sem("pool_passed_a_wait")
        pool_c = sem("pool_constants_ready")
        nblk_ok = sem("block_count_ready")
        ctl_mm = sem("counts_transposed")
        oh_ok = sem("classes_spread")
        oh_used = sem("classes_counted")
        cnt_ev = sem("counts_read")
        start_mm = sem("list_starts_ready")
        roh_ok = sem("rank_classes_spread")
        acc_ok = sem("rank_sums_ready")
        acc_read = sem("rank_sums_read")
        roh_used = sem("rank_classes_used")
        rank_ok = sem("ranks_ready")
        chunk_ok = sem("chunk_count_ready")
        scat = [sem("scattered0"), sem("scattered1")]
        list_zero = sem("list_zeroed")
        h_ok = [sem("last_spread0"), sem("last_spread1")]
        h_used = [sem("last_counted0"), sem("last_counted1")]
        hsum_ok = sem("last_count_ready")
        hsum_st = sem("last_count_stored")
        hsum_in = sem("last_count_loaded")
        nt_ok = sem("node_rows_ready")
        nt_st = sem("node_rows_stored")
        nn_in = sem("node_rows_loaded")
        rowi_ok = sem("chunk_rows_known")
        chunk_in = sem("chunk_loaded")
        src_ok = sem("chunk_sources_known")
        gath_in = sem("source_rows_gathered")
        a_req = sem("exponents_ready")
        a_done = sem("exponentials_done")
        scan_ok = sem("scans_ready")
        scan_st = sem("scans_stored")
        endi_ok = sem("segment_ends_known")
        seg_in = sem("segment_ends_gathered")
        seg_used = sem("segments_merged")
        hid_mm = sem("hidden_multiplied")
        hid_ok = sem("hidden_activated")
        ye_mm = sem("expert_multiplied")
        ye_ev = sem("expert_evacuated")
        gate_ok = sem("gates_ready")
        gate_st = sem("gates_stored")
        gate_in = sem("gates_loaded")
        done_dve = sem("result_ready")

        block = ctx.enter_context(nc.Block())
        DVE, PE, SC, PL = nc.vector, nc.tensor, nc.scalar, nc.gpsimd

        def bc(ap2, n):
            return ap2.unsqueeze(2).broadcast_to([ap2.shape[0], ap2.shape[1], n])

        def mid(ap2, n):
            return ap2.unsqueeze(1).broadcast_to([ap2.shape[0], n, ap2.shape[1]])

        LIN_IN, LIN_OUT = 0, 5
        X_PARTS = 4
        NX = IMAGES // X_PARTS
        MAX_BLK = ECOL // BLK
        MAX_CHUNKS = EDGES // CW + 1
        MAGIC = 12582912.0
        H_BUFS = 2
        H_GROUPS = MAX_BLK // H_BUFS
        H_ROUND = 3
        H_EARLY = H_ROUND * (LAYERS + 3)
        AS, AD, HF = slice(0, 4), slice(4, 8), slice(8, 24)
        MX, DN, NM = slice(0, 4), slice(4, 8), slice(8, 24)

        def store_tokens(eng, table, tile, width, s):
            rows = table[0:NODES].rearrange("(b t) h -> b t h", t=TOK)
            for half in range(2):
                eng.dma_start(rows[:, 1 + 32 * half:33 + 32 * half, :],
                              tile[64 * half:64 * half + 64, 0:32, 0:width]).then_inc(s, 16)
            eng.dma_start(rows[:, 0, :], tile[0:64, 32, 0:width]).then_inc(s, 16)

        weight_dmas = []
        for m, (g, gc) in enumerate(MAPS):
            weight_dmas.append((tokw[gc * 8:gc * 8 + 8, g, :], rep(tok_W[m], 8)))
        for i, w in enumerate([Win] + [Dm[l] for l in range(LAYERS)] + [Wout]):
            for q in range(2):
                weight_dmas.append((win2[64 * q:64 * q + 64, i, 64 * q:64 * q + 64], w))
        weight_dmas += [
            (tokb[:, :], rep(tok_b, P)), (binr[:, :], rep(bin_, P)), (boutr[:, :], rep(bout, P)),
            (a_pow[:, 0, :, :], A.rearrange("l n m -> n l m")),
            (bm[:, :, 0, :], Bm.rearrange("l n h -> n l h")),
            (cm[:, :, :], Cm.rearrange("l a n -> a l n")),
            (h0[0:64, 32, :], cls_tok[0, 0:1, :].broadcast_to([64, H])),
            (wg2[0:64, 0, :], W_gat), (wg2[64:128, 1, :], W_gat),
            (att[:, 0, :], rep(att_src.rearrange("a b -> (a b)"), P)),
            (att[:, 1, :], rep(att_dst.rearrange("a b -> (a b)"), P)),
            (gamr[:, 0, :], rep(b_gat, P)), (gamr[:, 1, :], rep(ln_gamma, P)), (gamr[:, 2, :], rep(ln_beta, P)),
            (w1[0:64, :, :], W1.rearrange("e h f -> h e f")), (w1[64:128, :, :], W1.rearrange("e h f -> h e f")),
            (w2[:, :, :], W2.rearrange("e f h -> f e h")), 
            (b2r[:, :, :].rearrange("p e h -> p (e h)"), rep(b2.rearrange("e h -> (e h)"), P)),
        ]

        def count_last_dve(v, g):
            for b in range(H_BUFS):
                c = (g * H_BUFS + b) * BLK
                if not (isinstance(g, int) and g == 0):
                    v.wait_ge(h_used[b], g)
                v.tensor_tensor(hoh[:, b, :, 0:DHI], bc(hcode[:, 0, bass.ds(c, BLK)], DHI),
                                mid(iota_b[:, 0:DHI], BLK), ALU.is_equal)
                v.tensor_tensor(hoh[:, b, :, DHI:], bc(hcode[:, 1, bass.ds(c, BLK)], DLO),
                                mid(iota_b[:, 0:DLO], BLK), ALU.is_equal)
                v.drain().then_inc(h_ok[b], 1)

        def count_last_pe(pe, g, last_group=False):
            for b in range(H_BUFS):
                pe.wait_ge(h_ok[b], g + 1)
                for j in range(BLK):
                    first = isinstance(g, int) and g == 0 and b == 0 and j == 0
                    end = last_group and b == H_BUFS - 1 and j == BLK - 1
                    m = pe.matmul(bank7[0:DHI, 0:DLO], hoh[:, b, j, 0:DHI], hoh[:, b, j, DHI:],
                                  start=first, stop=end, skip_group_check=True)
                m.then_inc(h_used[b], 1)


        def evacuate_T(act, r):
            for k in range(5):
                act.wait_ge(t_mm, 5 * r + k + 1)
                if k < 4:
                    act.activation(uT[:, 4 * k:4 * k + 4, :],
                                   wide[:, 512 * k:512 * k + 512].rearrange("p (s f) -> p s f", f=P),
                                   ACT.Copy).then_inc(t_ev, 1)
                else:
                    act.activation(uT[0:64, 16, :], wide[0:64, 2048:2048 + P], ACT.Copy).then_inc(t_ev, 1)

        def ye_slots(k):
            e, t = divmod(k, 9)
            if t == 8:
                return ye[:, e, 32:33, :]
            q, s2 = t // 2, t % 2
            return ye[:, e, 8 * q:8 * q + 8, :].rearrange("p (r s) h -> p s r h", s=2)[:, s2]

        def ye_evacuate(act, k):
            n = 4 if k % 9 < 8 else 1
            act.wait_ge(ye_mm, k + 1)
            act.activation(ye_slots(k), wide[:, (2 + k % 2) * 512:(2 + k % 2) * 512 + n * H].rearrange(
                "p (r h) -> p r h", h=H), ACT.Copy).then_inc(ye_ev, 1)

        def root(act, n):
            act.wait_ge(var_ok, n)
            act.activation(s3[:, :], s2[:, :], ACT.Sqrt).then_inc(rt_ok, 1)

        def transposes(pe, r):
            for k in range(5):
                for i in range(4 * k, min(4 * k + 4, PAIRS)):
                    last = (pe.transpose(wide[:, 128 * i:128 * i + 128], u[:, 2 * i:2 * i + 2, :], eye[:, :])
                            if i < 16 else
                            pe.transpose(wide[0:64, 2048:2048 + P], u[:, 32, :], eye[:, :]))
                last.then_inc(t_mm, 1)

        def linear(pe, w):
            for i in range(PAIRS):
                last = (pe.matmul(wide[:, 128 * i:128 * i + 128], uT[:, i, :], wlin[:, w, :], start=True, stop=True)
                        if i < 16 else
                        pe.matmul(wide[:, 2048:2048 + H], uT[0:64, 16, :], wlin[0:64, w, 0:64], start=True, stop=True))
            last.then_inc(y_mm, 1)

        def edges_pe(pe):
            pe.wait_ge(ctl_mm, 1)
            pe.transpose(bank6[0:1, 0:P], ecnt[:, 0:1], eye[:, :]).then_inc(ctl_mm, 1)
            pe.wait_ge(nblk_ok, 1)
            nblk = nc.tensor.value_load(ctl[0:1, 0:1], min_val=2, max_val=MAX_BLK)
            pe.matmul(bank6[:, 256:257], before_b[:, :], zero_b[:, :], start=True, stop=False,
                      skip_group_check=True).then_inc(oh_used, 1)
            with pe.Fori(0, nblk) as i:
                pe.wait_ge(oh_ok, i + 1)
                for j in range(BLK):
                    m = pe.matmul(bank6[:, 256:257], oh[:, j, :], ones_b[:, :], start=False, stop=False,
                                  skip_group_check=True)
                m.then_inc(oh_used, 1)
            pe.matmul(bank6[:, 256:257], before_b[:, :], zero_b[:, :], start=False, stop=True,
                      skip_group_check=True).then_inc(cnt_ev, 1)
            pe.wait_ge(cnt_ev, 3)
            pe.transpose(bank6[0:1, 0:P], ecnt[:, 1:2], eye[:, :])
            pe.matmul(bank6[:, 128:129], before[:, :], ecnt[:, 2:3], start=True, stop=True)
            pe.matmul(bank5[:, 0:P], rows64r[:, :], before64[:, :], start=True, stop=False,
                      skip_group_check=True).then_inc(start_mm, 1)
            pe.matmul(bank5[:, 0:1], before_b[:, :], zero_b[:, :], start=False, stop=False,
                      skip_group_check=True).then_inc(roh_used, 1)
            with pe.Fori(0, nblk) as i:
                pe.wait_ge(roh_ok, i + 1)
                for j in range(BLK):
                    pe.matmul(bank5[:, 0:P], before_b[:, :], oh[:, j, :], start=False, stop=False,
                              skip_group_check=True).then_inc(acc_ok, 1)
                    pe.wait_ge(acc_read, i * BLK + (j + 1))
                    m = pe.matmul(bank5[:, 0:P], after_b[:, :], oh[:, j, :], start=False, stop=False,
                                  skip_group_check=True)
                m.then_inc(roh_used, 1)
            pe.matmul(bank5[:, 0:1], before_b[:, :], zero_b[:, :], start=False, stop=True, skip_group_check=True)

        def prep(pe):
            n = 0
            pe.wait_ge(w_in, 16 * (len(weight_dmas) + 1))
            for i in range(6):
                b = [bank5, bank6, bank7][i % 3]
                if i >= 3:
                    pe.wait_ge(prep_ev, i - 2)
                pe.transpose(b[:, 0:P], win2[:, i, :], eye[:, :]).then_inc(prep_mm, 1)
            pe.wait_ge(prep_ev, 6)
            for l in range(LAYERS):
                pe.transpose(bank5[0:64, 64 * l:64 * l + 64], a_pow[:, 0, l, :], eye[0:64, 0:64])
                last = pe.matmul(bank6[0:64, l:l + 1], cm[:, l, :], mean64[:, :], start=True, stop=True)
            last.then_inc(prep_mm, 1)
            n = 7
            for d in range(6):
                pe.wait_ge(prep_ev, n)
                c, w = d % 2, 1 << d
                for l in range(LAYERS):
                    last = pe.matmul(bank6[0:64, 64 * l:64 * l + w], a_pow[:, c, l, :], vee[:, l, 0:w],
                                     start=True, stop=True)
                    if d < 5:
                        pe.matmul(bank5[0:64, 64 * l:64 * l + 64], a_powT[:, c, l, :], a_pow[:, c, l, :],
                                  start=True, stop=True)
                        last = pe.matmul(bank7[0:64, 64 * l:64 * l + 64], a_pow[:, c, l, :], a_powT[:, c, l, :],
                                         start=True, stop=True)
                last.then_inc(prep_mm, 1)
                n += 1
            pe.wait_ge(prep_ev, n)
            for l in range(LAYERS):
                last = pe.matmul(bank5[:, 64 * l:64 * l + 64], bm[:, l, :, :], vee[:, l, :], start=True, stop=True)
            last.then_inc(prep_mm, 1)
            pe.wait_ge(prep_ev, n + 1)

        def dve_prep(v):
            v.wait_ge(c_in, 16 * 5)
            v.wait_ge(w_in, 16 * (len(weight_dmas) + 1))
            for g in range(4):
                v.tensor_tensor(tokwd[:, g, :, :], mid(tokw[:, g, :], 8), bc(pick[:, :], H), ALU.mult)
            v.tensor_copy(bm[:, :, 1, :], bm[:, :, 0, :])
            v.drain().then_inc(tokwd_ok, 1)

        def dve_kernels(v):
            for i in range(6):
                v.wait_ge(prep_mm, i + 1)
                v.tensor_copy(wlin[:, i, :], [bank5, bank6, bank7][i % 3][:, 0:P]).then_inc(prep_ev, 1)
            v.wait_ge(prep_mm, 7)
            v.tensor_copy(a_powT[:, 0, :, :], bank5[0:64, 0:256].rearrange("p (l m) -> p l m", l=LAYERS))
            v.tensor_copy(vee[:, :, 0:1], bank6[0:64, 0:LAYERS].unsqueeze(2)).then_inc(prep_ev, 1)
            for d in range(6):
                v.wait_ge(prep_mm, 8 + d)
                c, w = 1 - d % 2, 1 << d
                if d < 5:
                    v.tensor_copy(a_pow[:, c, :, :], bank5[0:64, 0:256].rearrange("p (l m) -> p l m", l=LAYERS))
                    v.tensor_copy(a_powT[:, c, :, :], bank7[0:64, 0:256].rearrange("p (l m) -> p l m", l=LAYERS))
                v.tensor_copy(vee[:, :, w:2 * w],
                              bank6[0:64, 0:256].rearrange("p (l m) -> p l m", l=LAYERS)[:, :, 0:w])
                v.drain().then_inc(prep_ev, 1)
            v.wait_ge(prep_mm, 14)
            w = bank5[:, 0:256].rearrange("p (l m) -> p l m", l=LAYERS)
            v.tensor_copy(conv[0:64, :, 65:129], w[0:64])
            v.tensor_copy(conv[64:128, :, 66:130], w[64:128])
            v.drain().then_inc(prep_ev, 1)

        def layer_norm(v, n, src, dst):
            v.reduce_sum(s1[:, :], src, axis=X)
            v.drain()
            v.tensor_scalar(s1[:, :], s1[:, :], 1.0 / H, None, ALU.mult)
            v.drain()
            v.tensor_tensor(xc[:, :, :], src, bc(s1[:, :], H), ALU.subtract)
            v.drain()
            v.tensor_tensor(sq[:, :, :], xc[:, :, :], xc[:, :, :], ALU.mult)
            v.drain()
            v.reduce_sum(s2[:, :], sq[:, :, :], axis=X)
            v.drain()
            v.tensor_scalar(s2[:, :], s2[:, :], 1.0 / H, EPS, ALU.mult, ALU.add).then_inc(var_ok, 1)
            v.wait_ge(rt_ok, n)
            v.reciprocal(s1[:, :], s3[:, :])
            v.drain()
            v.tensor_tensor(dst, xc[:, :, :], bc(s1[:, :], H), ALU.mult)
            v.drain()

        def await_then_pass(pool, s, value):
            pool.wait_ge(s, value)
            pool.sem_inc(pool_passed, 1)

        def scatter_block(pool, i):
            for h in range(2):
                c = i * BLK + h * (BLK // 2)
                if not (isinstance(i, int) and i == 0):
                    pool.wait_ge(scat[h], i * (8 * BLK))
                pool.tensor_copy(ring_i[:, h, :], rank_tab[:, bass.ds(c, BLK // 2)])
                pool.tensor_copy(ring_k[:, h, :], lkey_tab[:, bass.ds(c, BLK // 2)])
                pool.drain()
                for j in range(BLK // 2):
                    pool.indirect_dma_start(
                        edge_list, bass.IndirectOffsetOnAxis(ap=ring_i[:, h, j:j + 1], axis=0),
                        ring_k[:, h, j:j + 1], None, bounds_check=LIST_ROWS * ROW - 1,
                        oob_is_err=False).then_inc(scat[h], 16)

        def round_to(v, ap):
            v.tensor_scalar(ap, ap, MAGIC, MAGIC, ALU.add, ALU.subtract)
            v.drain()

        def edges_dve(v):
            v.wait_ge(e_in, 32)
            v.tensor_copy(key[:, :], raw[:, 1, :])
            v.tensor_scalar(srcf, raw[:, 0, :], float(NODES - 1), None, ALU.min)
            v.drain()
            v.tensor_scalar(etmp, key[:, :], float(NODES), DEAD, ALU.is_ge, ALU.mult)
            v.drain()
            v.tensor_scalar(key[:, :], key[:, :], float(-KEY0), float(NODES), ALU.add, ALU.mult)
            v.drain()
            v.tensor_tensor(key[:, :], key[:, :], srcf, ALU.add)
            v.drain()
            v.tensor_tensor(key[:, :], key[:, :], etmp, ALU.add)
            v.drain()
            v.tensor_scalar(etmp, srcf, float(NODES - 1), DEAD, ALU.is_ge, ALU.mult)
            v.drain()
            v.tensor_tensor(key[:, :], key[:, :], etmp, ALU.add)
            v.drain()
            v.tensor_scalar(etmp, key[:, :], LIVE, 0.0, ALU.is_ge, ALU.add, accum_out=ecnt[:, 0:1])
            v.drain()
            v.tensor_scalar(srcf, srcf, float(NODES - 1), 1024.0, ALU.is_lt, ALU.mult)
            v.tensor_scalar(etmp.bitcast(I32), raw[:, 1, :], 6, None, ALU.logical_shift_right)
            v.drain()
            v.tensor_tensor(hcode[:, 0, :], etmp.bitcast(I32), srcf, ALU.add)
            v.drain()
            v.tensor_scalar(etmp.bitcast(I32), raw[:, 1, :], DLO - 1, None, ALU.bitwise_and)
            v.drain()
            v.tensor_copy(hcode[:, 1, :], etmp.bitcast(I32))
            v.wait_ge(c_in, 16 * 5)
            v.wait_ge(pool_c, 1)
            v.tensor_copy(before_b[:, :], before[:, :])
            v.tensor_scalar(after_b[:, :], before[:, :], -1.0, 1.0, ALU.mult, ALU.add)
            v.tensor_scalar(before64[:, :], before[:, :], float(ROW), None, ALU.mult)
            v.drain().then_inc(ctl_mm, 1)
            v.wait_ge(ctl_mm, 2)
            v.reduce_max(junk[0:1, 0:1], bank6[0:1, 0:P], axis=X)
            v.drain()
            to_blocks(v, ctl[0:1, 0:1], junk[0:1, 0:1], BLK - 1, 4, 2)
            v.drain().then_inc(nblk_ok, 1)
            nblk = nc.vector.value_load(ctl[0:1, 0:1], min_val=2, max_val=MAX_BLK)
            with v.Fori(0, nblk) as i:
                for q in range(BLK // 8):
                    v.max(top[:, 8 * q:8 * q + 8], key[:, :])
                    v.drain()
                    v.match_replace(key[:, :], top[:, 8 * q:8 * q + 8], key[:, :], 4 * DEAD)
                    v.drain()
                q_, r_, t_, c_ = cw[:, 0, :], cw[:, 1, :], cw[:, 2, :], cw[:, 3, :]
                v.tensor_scalar(q_, top[:, :], -0.5 * (NODES - 1), 1.0 / NODES, ALU.add, ALU.mult)
                v.drain()
                round_to(v, q_)
                v.scalar_tensor_tensor(r_, q_, float(-NODES), top[:, :], ALU.mult, ALU.add)
                v.drain()
                v.tensor_scalar(t_, r_, 0.0, None, ALU.is_lt)
                v.tensor_scalar(c_, r_, float(NODES), None, ALU.is_ge)
                v.drain()
                v.tensor_tensor(q_, q_, t_, ALU.subtract)
                v.drain()
                v.tensor_tensor(q_, q_, c_, ALU.add)
                v.drain()
                v.tensor_scalar(c_, q_, float(KEY0 - SLOTS // 2), 1.0 / SLOTS, ALU.add, ALU.mult)
                v.drain()
                round_to(v, c_)
                v.tensor_scalar(t_, c_, float(SLOTS * NODES), float(KEY0 * NODES), ALU.mult, ALU.subtract)
                v.drain()
                v.tensor_tensor(t_, top[:, :], t_, ALU.subtract)
                v.drain()
                v.tensor_scalar(lkey_tab[:, bass.ds(i * BLK, BLK)], t_, 1.0, None, ALU.add)
                v.tensor_copy(cls_tab[:, bass.ds(i * BLK, BLK)], c_)
                v.wait_ge(oh_used, i + 1)
                v.tensor_tensor(oh[:, :, :], bc(c_, P), mid(iota_b[:, :], BLK), ALU.is_equal)
                v.drain().then_inc(oh_ok, 1)
            v.wait_ge(oh_used, nblk + 1)
            v.wait_ge(cnt_ev, 1)
            v.tensor_copy(ecnt[:, 1:2], bank6[:, 256:257])
            v.drain()
            to_blocks(v, rows64[:, :], ecnt[:, 1:2], ROW - 1, 6, 0)
            v.drain()
            v.tensor_copy(ecnt[:, 2:3], rows64[:, :])
            v.drain()
            v.tensor_copy(rows64r[:, :], ecnt[:, 2:3].broadcast_to([P, P]))
            v.drain().then_inc(cnt_ev, 2)
            v.wait_ge(start_mm, 1)
            v.tensor_copy(ecnt[:, 3:4], bank6[:, 128:129])
            v.reduce_max(junk[0:1, 0:1], bank6[0:1, 0:P], axis=X)
            v.drain()
            v.tensor_scalar(junk[0:1, 0:1], junk[0:1, 0:1], 0.5 * (CW - 1), 1.0 / CW, ALU.add, ALU.mult)
            v.drain()
            round_to(v, junk[0:1, 0:1])
            v.tensor_scalar(junk[0:1, 0:1], junk[0:1, 0:1], 1.0, None, ALU.max)
            v.drain()
            v.tensor_copy(ctl[0:1, 1:2], junk[0:1, 0:1])
            v.drain().then_inc(chunk_ok, 1)
            with v.Fori(0, nblk) as i:
                v.wait_ge(roh_used, i + 1)
                v.tensor_tensor(oh[:, :, :], bc(cls_tab[:, bass.ds(i * BLK, BLK)], P),
                                mid(iota_b[:, :], BLK), ALU.is_equal)
                v.tensor_scalar(cw[:, 1, :], cls_tab[:, bass.ds(i * BLK, BLK)], 0.0, FAR, ALU.is_lt, ALU.mult)
                v.drain().then_inc(roh_ok, 1)
                for j in range(BLK):
                    v.wait_ge(acc_ok, i * BLK + (j + 1))
                    v.tensor_tensor_reduce(out=junk[:, :], in0=bank5[:, 0:P], in1=oh[:, j, :], scale=1.0,
                                           scalar=0.0, op0=ALU.mult, op1=ALU.add,
                                           accum_out=cw[:, 0, j:j + 1]).then_inc(acc_read, 1)
                v.drain()
                v.tensor_tensor(rank_tab[:, bass.ds(i * BLK, BLK)], cw[:, 0, :], cw[:, 1, :], ALU.add)
                v.drain().then_inc(rank_ok, 1)

        def count_round(v, r):
            for g in range(H_ROUND * r, H_ROUND * r + H_ROUND):
                count_last_dve(v, g)

        def to_blocks(v, out_i, in_f, less_one, shift, least):
            v.tensor_scalar(out_i, in_f, float(less_one), None, ALU.add)
            v.drain()
            v.tensor_scalar(out_i, out_i, shift, None, ALU.logical_shift_right)
            if least:
                v.drain()
                v.tensor_scalar(out_i, out_i, float(least), None, ALU.max)

        def chunk_rows(v, t):
            if t is None:
                for r in range(CROWS):
                    v.tensor_scalar(rowf[:, r:r + 1], ecnt[:, 3:4], float(r), float(LAST_ROW), ALU.add, ALU.min)
                v.tensor_copy(ecnt[:, 4:5], ecnt[:, 1:2])
                v.drain()
                v.tensor_copy(rowi[:, :], rowf[:, :])
                v.drain().then_inc(rowi_ok, 1)
            else:
                v.tensor_scalar(rowf[:, :], rowf[:, :], float(CROWS), float(LAST_ROW), ALU.add, ALU.min)
                v.tensor_scalar(ecnt[:, 4:5], ecnt[:, 4:5], float(CW), None, ALU.subtract)
                v.drain()
                v.tensor_copy(rowi[:, :], rowf[:, :])
                v.drain().then_inc(rowi_ok, 1)

        def leaky(v, out, z, tmp):
            v.tensor_scalar(tmp, z, 0.2, None, ALU.mult)
            v.drain()
            v.tensor_tensor(out, z, tmp, ALU.max)
            v.drain()

        def graph_start(v):
            v.wait_ge(nn_in, 32)
            v.wait_ge(hsum_in, 16)
            own, last, t4, lcb = n4[:, 0], n4[:, 1], n4[:, 2], n4[:, 3]
            v.tensor_tensor(t4, nn[:, :, AS], nn[:, :, AD], ALU.add)
            v.drain()
            leaky(v, own, t4, lcb)
            v.tensor_tensor(t4, mid(lastr[:, AS], SLOTS), nn[:, :, AD], ALU.add)
            v.drain()
            leaky(v, last, t4, lcb)
            v.tensor_copy(lcb, bc(lastc[:, :], HEADS))
            v.drain()
            v.tensor_scalar(t4, lcb, 0.5, -1.0e30, ALU.is_lt, ALU.mult)
            v.drain()
            v.tensor_tensor(t4, last, t4, ALU.add)
            v.drain()
            v.tensor_tensor(st[:, :, MX], own, t4, ALU.max)
            v.drain()
            v.tensor_tensor(own, own, st[:, :, MX], ALU.subtract)
            v.tensor_tensor(last, last, st[:, :, MX], ALU.subtract)
            v.drain()
            v.tensor_scalar(last, last, 0.0, None, ALU.min)
            v.drain().then_inc(a_req, 1)
            v.wait_ge(a_done, 1)
            v.tensor_tensor(last, last, lcb, ALU.mult)
            v.drain()
            v.tensor_tensor(st[:, :, DN], own, last, ALU.add)
            v.tensor_tensor(heads(n16[:, 0]), heads(nn[:, :, HF]), bc4(own), ALU.mult)
            v.tensor_tensor(heads(n16[:, 1]), heads(mid(lastr[:, HF], SLOTS)), bc4(last), ALU.mult)
            v.drain()
            v.tensor_tensor(st[:, :, NM], n16[:, 0], n16[:, 1], ALU.add)
            v.drain()

        def heads(ap):
            return ap.rearrange("p s (a b) -> p s a b", a=HEADS)

        def bc4(ap):
            return ap.unsqueeze(3).broadcast_to([P, SLOTS, HEADS, EXPERTS])

        def graph_chunk(v, t):
            v.wait_ge(chunk_in, t * (16 * CROWS) + 16 * CROWS)
            v.tensor_scalar(ctmp[:, :], iota[:, :], ecnt[:, 4:5], None, ALU.is_lt)
            v.drain()
            v.tensor_tensor(chunk[:, :], chunk[:, :], ctmp[:, :], ALU.mult)
            v.drain()
            for k in range(CW // 8):
                v.max(skey[:, 8 * k:8 * k + 8], chunk[:, :])
                v.drain()
                if k < CW // 8 - 1:
                    v.match_replace(chunk[:, :], skey[:, 8 * k:8 * k + 8], chunk[:, :], -1.0)
                    v.drain()
            v.tensor_scalar(place[:, :], skey[:, :], -1.0 - 0.5 * (NODES - 1), 1.0 / NODES, ALU.add, ALU.mult)
            v.drain()
            round_to(v, place[:, :])
            v.scalar_tensor_tensor(ctmp[:, :], place[:, :], float(-NODES), skey[:, :], ALU.mult, ALU.add)
            v.drain()
            v.tensor_scalar(srci[:, :], ctmp[:, :], -1.0, None, ALU.add)
            v.drain().then_inc(src_ok, 1)
            v.memset(keep[:, 0:1], 0.0)
            v.tensor_tensor(keep[:, 1:CW], place[:, 1:CW], place[:, 0:CW - 1], ALU.is_equal)
            v.drain()
            v.tensor_scalar(ctmp[:, :], keep[:, :], -1.0, 1.0e30, ALU.add, ALU.mult)
            pm = place_m.rearrange("p (l s) -> p l s", s=SLOTS)
            pf = place_f.rearrange("p (l s) -> p l s", s=SLOTS)
            v.tensor_tensor(pm, bc(place[:, :], SLOTS), mid(iota[:, 0:SLOTS], CW), ALU.is_equal)
            v.drain()
            for h in range(HEADS):
                v.tensor_tensor(pf, pm, mid(nn[:, :, 4 + h], CW), ALU.mult)
                v.drain()
                v.reduce_sum(adst[:, h, :], pf, axis=X)
                v.drain()
            v.tensor_tensor(pm.rearrange("p l s -> p (l s)").rearrange("p (s l) -> p s l", l=CW),
                            mid(place[:, :], SLOTS), bc(iota[:, 0:SLOTS], CW), ALU.is_ge)
            v.memset(ends[:, SLOTS:SLOTS + 1], 0.0)
            v.drain()
            v.reduce_sum(ends[:, 0:SLOTS], pm.rearrange("p l s -> p (l s)").rearrange("p (s l) -> p s l", l=CW),
                         axis=X)
            v.drain()
            v.tensor_tensor(has[:, :], ends[:, 0:SLOTS], ends[:, 1:SLOTS + 1], ALU.is_gt)
            v.drain()
            v.tensor_scalar(ends[:, 0:SLOTS], ends[:, 0:SLOTS], -1.0, 0.0, ALU.add, ALU.max)
            v.drain()
            v.tensor_scalar(ecnt[:, 5:6], ecnt[:, 7:8], float(CW), None, ALU.mult)
            v.drain()
            v.tensor_scalar(ends[:, 0:SLOTS], ends[:, 0:SLOTS], ecnt[:, 5:6], None, ALU.add)
            v.drain()
            v.tensor_copy(endi[:, :], ends[:, 0:SLOTS])
            v.drain().then_inc(endi_ok, 1)
            v.wait_ge(gath_in, t * (16 * CW) + 16 * CW)
            v.tensor_tensor(adst[:, :, :], adst[:, :, :], gath[:, :, AS].rearrange("p l a -> p a l"), ALU.add)
            v.drain()
            leaky(v, eh[:, :, :], adst[:, :, :], mh[:, :, :])
            for h in range(HEADS):
                v.tensor_tensor_scan(mh[:, h, :], ctmp[:, :], eh[:, h, :], 0.0, ALU.add, ALU.max)
            v.drain()
            v.memset(rh[:, :, 0:1], 0.0)
            v.tensor_tensor(rh[:, :, 1:CW], mh[:, :, 0:CW - 1], mh[:, :, 1:CW], ALU.subtract)
            v.tensor_tensor(wh[:, :, :], eh[:, :, :], mh[:, :, :], ALU.subtract)
            v.drain()
            v.tensor_scalar(rh[:, :, :], rh[:, :, :], 0.0, None, ALU.min)
            v.drain().then_inc(a_req, 1)
            v.wait_ge(a_done, 2 + 2 * t)
            v.tensor_tensor(rh[:, :, :], rh[:, :, :], mid(keep[:, :], HEADS), ALU.mult)
            for h in range(HEADS):
                xh = xh_a if h < 2 else xh_b
                v.tensor_tensor(xh[:, 4 * (h % 2):4 * (h % 2) + 4, :],
                                gath[:, :, 8 + 4 * h:12 + 4 * h].rearrange("p l a -> p a l"),
                                mid(wh[:, h, :], EXPERTS), ALU.mult)
            v.tensor_copy(scans[:, :, MX], mh[:, :, :].rearrange("p a l -> p l a"))
            v.drain()
            for h in range(HEADS):
                v.tensor_tensor_scan(scans[:, :, 4 + h], rh[:, h, :], wh[:, h, :], 0.0, ALU.mult, ALU.add)
            for f in range(HE):
                v.tensor_tensor_scan(scans[:, :, 8 + f], rh[:, f // 4, :], (xh_a if f < 8 else xh_b)[:, f % 8, :], 0.0, ALU.mult, ALU.add)
            v.drain().then_inc(scan_ok, 1)
            v.wait_ge(seg_in, t * (16 * SLOTS) + 16 * SLOTS)
            hb, mc, old, new, dn = n4[:, 0], n4[:, 1], n4[:, 2], n4[:, 3], n4[:, 4]
            v.tensor_copy(hb, bc(has[:, :], HEADS))
            v.drain()
            v.tensor_scalar(mc, hb, -1.0, 1.0e30, ALU.add, ALU.mult)
            v.drain()
            v.tensor_tensor(mc, mc, seg[:, :, MX], ALU.add)
            v.drain()
            v.tensor_tensor(mc, mc, st[:, :, MX], ALU.max)
            v.drain()
            v.tensor_tensor(old, st[:, :, MX], mc, ALU.subtract)
            v.tensor_tensor(new, seg[:, :, MX], mc, ALU.subtract)
            v.drain()
            v.tensor_scalar(new, new, 0.0, None, ALU.min)
            v.tensor_copy(st[:, :, MX], mc)
            v.drain().then_inc(a_req, 1)
            v.wait_ge(a_done, 3 + 2 * t)
            v.tensor_tensor(new, new, hb, ALU.mult)
            v.drain()
            v.tensor_tensor(st[:, :, DN], st[:, :, DN], old, ALU.mult)
            v.tensor_tensor(dn, seg[:, :, DN], new, ALU.mult)
            v.tensor_tensor(heads(n16[:, 0]), heads(st[:, :, NM]), bc4(old), ALU.mult)
            v.tensor_tensor(heads(n16[:, 1]), heads(seg[:, :, NM]), bc4(new), ALU.mult)
            v.drain()
            v.tensor_tensor(st[:, :, DN], st[:, :, DN], dn, ALU.add)
            v.tensor_tensor(st[:, :, NM], n16[:, 0], n16[:, 1], ALU.add)
            v.drain()
            chunk_rows(v, t)

        def graph_end(v, n):
            inv, agg, x2 = n4[:, 0], n16[:, 0], n16[:, 1]
            v.tensor_scalar(inv, st[:, :, DN], 1e-16, None, ALU.add)
            v.drain()
            v.reciprocal(inv, inv)
            v.drain()
            v.tensor_tensor(heads(agg), heads(st[:, :, NM]), bc4(inv), ALU.mult)
            v.drain()
            v.tensor_tensor(agg, agg, mid(gamr[:, 0, :], SLOTS), ALU.add)
            v.drain()
            v.reduce_sum(s1[:, :], agg, axis=X)
            v.drain()
            v.tensor_scalar(s1[:, :], s1[:, :], 1.0 / HE, None, ALU.mult)
            v.drain()
            v.tensor_tensor(agg, agg, bc(s1[:, :], HE), ALU.subtract)
            v.drain()
            v.tensor_tensor(x2, agg, agg, ALU.mult)
            v.drain()
            v.reduce_sum(s2[:, :], x2, axis=X)
            v.drain()
            v.tensor_scalar(s2[:, :], s2[:, :], 1.0 / HE, EPS, ALU.mult, ALU.add).then_inc(var_ok, 1)
            v.wait_ge(rt_ok, LAYERS + 4)
            v.reciprocal(s1[:, :], s3[:, :])
            v.drain()
            v.tensor_tensor(agg, agg, bc(s1[:, :], HE), ALU.mult)
            v.drain()
            v.tensor_tensor(agg, agg, mid(gamr[:, 1, :], SLOTS), ALU.mult)
            v.drain()
            v.tensor_tensor(agg, agg, mid(gamr[:, 2, :], SLOTS), ALU.add)
            v.drain()
            sc, ex, sel = n4[:, 0], n4[:, 1], n4[:, 2]
            v.reduce_sum(sc, agg.rearrange("p s (a b) -> p s b a", a=HEADS), axis=X)
            v.drain()
            v.tensor_scalar(sc, sc, 1.0 / HEADS, None, ALU.mult)
            v.drain()
            for e in range(EXPERTS):
                for o in range(EXPERTS):
                    if o != e:
                        v.tensor_tensor(n4[:, 3 + e, :, o], sc[:, :, o], sc[:, :, e],
                                        ALU.is_ge if o < e else ALU.is_gt)
                    else:
                        v.memset(n4[:, 3 + e, :, o], 0.0)
            v.drain()
            for e in range(EXPERTS):
                v.reduce_sum(sel[:, :, e], n4[:, 3 + e], axis=X)
            v.reduce_max(s1[:, :], sc, axis=X)
            v.drain()
            v.tensor_scalar(sel, sel, 1.5, None, ALU.is_lt)
            v.tensor_tensor(ex, sc, bc(s1[:, :], EXPERTS), ALU.subtract)
            v.drain().then_inc(a_req, 1)
            v.wait_ge(a_done, n * 2 + 2)
            v.tensor_tensor(ex, ex, sel, ALU.mult)
            v.drain()
            v.reduce_sum(s1[:, :], ex, axis=X)
            v.drain()
            v.reciprocal(s1[:, :], s1[:, :])
            v.drain()
            v.memset(gtok[:, :, :], 0.0)
            v.tensor_tensor(gates[:, :, :], ex, bc(s1[:, :], EXPERTS), ALU.mult)
            v.drain().then_inc(gate_ok, 1)

        @block.sync
        def _(sp):
            ev = edge_index.rearrange("a (p e) -> p a e", p=P)
            sp.dma_start(raw[:, 1, :], ev[:, 1, :]).then_inc(e_in, 16)
            sp.dma_start(raw[:, 0, :], ev[:, 0, :]).then_inc(e_in, 16)
            sp.dma_start(waver[:, :], c_waver).then_inc(c_in, 16)
            sp.dma_start(wave[:, :], c_wave).then_inc(c_in, 16)
            for i in range(X_PARTS):
                sp.dma_start(xs[:, i * NX:(i + 1) * NX, :],
                             x[i * NX:(i + 1) * NX, 0].rearrange("b r c -> r b c")).then_inc(x_in[i], 16)
            sp.dma_start(eye[:, :], c_eye).then_inc(c_in, 16)
            sp.dma_start(before[:, :], c_before).then_inc(c_in, 16)
            sp.dma_start(pick[:, :], c_pick).then_inc(c_in, 16)
            sp.wait_ge(pool_c, 1)
            lz = edge_list.rearrange("(k p f) a -> k p (f a)", p=P, f=529)
            for k in range(4):
                sp.dma_start(lz[k], zeros[:, :]).then_inc(list_zero, 16)
            pad = NODE_ROWS - NODES
            sp.dma_start(node_tab[NODES:NODE_ROWS, :], zeros[0:pad, 0:NF]).then_inc(nt_st, 16)
            sp.dma_start(last_tab[NODES:NODE_ROWS].rearrange("(a b) -> a b", a=1),
                         zeros[0:1, 0:pad]).then_inc(hsum_st, 16)
            sp.wait_ge(nt_ok, 1)
            store_tokens(sp, node_tab, nt, NF, nt_st)
            sp.wait_ge(nt_st, 16 * 4)
            sp.dma_start(nn[:, :, :], node_tab.rearrange("(p s) f -> p s f", s=SLOTS)).then_inc(nn_in, 16)
            sp.dma_start(lastr[:, :], node_tab[NODES - 1:NODES, :].broadcast_to([P, NF])).then_inc(nn_in, 16)
            sp.wait_ge(hsum_ok, 1)
            sp.dma_start(last_tab[0:NODES].rearrange("(a b) -> a b", b=DLO), hsum[:, :]).then_inc(hsum_st, 16)
            sp.wait_ge(hsum_st, 32)
            sp.dma_start(lastc[:, :], last_tab.rearrange("(p s) -> p s", s=SLOTS)).then_inc(hsum_in, 16)
            sp.wait_ge(chunk_ok, 1)
            n = nc.sync.value_load(ctl[0:1, 1:2], min_val=1, max_val=MAX_CHUNKS)
            with sp.Fori(0, n) as t:
                sp.wait_ge(scan_ok, t + 1)
                sp.dma_start(scan_tab.rearrange("(p l) f -> p l f", l=CW), scans).then_inc(scan_st, 16)
            sp.wait_ge(gate_ok, 1)
            sp.dma_start(gate_tab.rearrange("(p s) f -> p s f", s=SLOTS), gates[:, :, :]).then_inc(gate_st, 16)
            sp.wait_ge(gate_st, 16)
            grow = gate_tab[0:NODES].rearrange("(b t) f -> b t f", t=TOK)
            for half in range(2):
                sp.dma_start(gtok[64 * half:64 * half + 64, 0:32, :],
                             grow[:, 1 + 32 * half:33 + 32 * half, :]).then_inc(gate_in, 16)
            sp.dma_start(gtok[0:64, 32, :], grow[:, 0, :]).then_inc(gate_in, 16)
            sp.wait_ge(done_dve, 1)
            store_tokens(sp, out.rearrange("b t h -> (b t) h"), h0, H, d_out)
            sp.wait_ge(d_out, 16 * 3)

        @block.scalar
        def _(act):
            act.wait_ge(zero_ok, 1)
            for dst, src in weight_dmas:
                act.dma_start(dst, src).then_inc(w_in, 16)
            act.dma_start(b1c[:, :], b1.rearrange("e f -> f e"), allow_slow_non_contiguous=True).then_inc(w_in, 16)
            for i in range(16):
                act.wait_ge(x_rows, i + 1)
                act.activation(y1[:, 4 * i:4 * i + 4, :],
                               wide[0:SIDE, (i % 4) * 512:(i % 4) * 512 + 128].rearrange("p (b m) -> p b m", b=4),
                               ACT.Copy).then_inc(x_rows_out, 1)
            for i in range(4):
                act.wait_ge(x_cols, i + 1)
                act.activation(y2[:, :, 16 * i:16 * i + 16].rearrange("n m b -> n b m"),
                               wide[0:32, i * 512:i * 512 + 512].rearrange("n (b m) -> n b m", m=32),
                               ACT.Copy).then_inc(x_cols_out, 1)
            root(act, 1)
            for r in range(LAYERS + 2):
                evacuate_T(act, r)
                if 1 <= r <= LAYERS:
                    act.wait_ge(y_ok, r)
                    act.activation(sq[:, :, :], xc[:, :, :], ACT.Gelu).then_inc(g_ok, 1)
                    root(act, r + 1)
                if r == LAYERS:
                    root(act, r + 2)
            root(act, LAYERS + 3)
            evacuate_T(act, LAYERS + 2)
            act.wait_ge(list_zero, 64)
            act.wait_ge(nt_st, 64)
            act.wait_ge(hsum_st, 16)
            for k in range(9 * EXPERTS):
                e, t = divmod(k, 9)
                n = 512 if t < 8 else P
                act.wait_ge(hid_mm, k + 1)
                if k >= 2:
                    act.wait_ge(ye_mm, k - 1)
                act.activation(hidT[:, k % 2, 0:n], wide[:, (k % 2) * 512:(k % 2) * 512 + n], ACT.Gelu,
                               bias=b1c[:, e:e + 1]).then_inc(hid_ok, 1)
                if k >= 1:
                    ye_evacuate(act, k - 1)
            ye_evacuate(act, 9 * EXPERTS - 1)
            act.wait_ge(chunk_ok, 1)
            act.wait_ge(a_req, 1)
            act.activation(n4[:, 0:2], n4[:, 0:2], ACT.Exp).then_inc(a_done, 1)
            n = nc.scalar.value_load(ctl[0:1, 1:2], min_val=1, max_val=MAX_CHUNKS)
            with act.Fori(0, n) as t:
                act.wait_ge(a_req, 2 + 2 * t)
                act.activation(rh[:, :, :], rh[:, :, :], ACT.Exp)
                act.activation(wh[:, :, :], wh[:, :, :], ACT.Exp).then_inc(a_done, 1)
                act.wait_ge(a_req, 3 + 2 * t)
                act.activation(n4[:, 2:4], n4[:, 2:4], ACT.Exp).then_inc(a_done, 1)
            act.wait_ge(var_ok, LAYERS + 4)
            act.activation(s3[:, :], s2[:, :], ACT.Sqrt).then_inc(rt_ok, 1)
            act.wait_ge(a_req, 2 + 2 * n)
            act.activation(n4[:, 1], n4[:, 1], ACT.Exp).then_inc(a_done, 1)

        @block.gpsimd
        def _(pool):
            pool.memset(tokw[:, :, :], 0.0)
            pool.memset(win2[:, :, :], 0.0)
            pool.memset(conv[:, :, :], 0.0)
            pool.memset(h0[:, 32, :], 0.0)
            pool.memset(mean64[:, :], 1.0 / H)
            pool.memset(wg2[:, :, :], 0.0)
            pool.drain().then_inc(zero_ok, 1)
            pool.memset(zeros[:, :], 0.0)
            pool.memset(ones_b[:, :], 1.0)
            pool.memset(zero_b[:, :], 0.0)
            pool.iota(iota[:, :], [[1, CW]], base=0, channel_multiplier=0, allow_small_or_imprecise_dtypes=True)
            pool.iota(iota_b[:, :], [[1, P]], base=0, channel_multiplier=0, allow_small_or_imprecise_dtypes=True)
            pool.iota(ecnt[:, 7:8], [[0, 1]], base=0, channel_multiplier=1, allow_small_or_imprecise_dtypes=True)
            pool.drain().then_inc(pool_c, 1)
            pool.wait_ge(list_zero, 64)
            pool.wait_ge(nblk_ok, 1)
            nblk = nc.gpsimd.value_load(ctl[0:1, 0:1], min_val=2, max_val=MAX_BLK)
            pool.wait_ge(chunk_ok, 1)
            pool.wait_ge(rank_ok, 1)
            scatter_block(pool, 0)
            with pool.Fori(1, nblk) as i:
                pool.wait_ge(rank_ok, i + 1)
                scatter_block(pool, i)
            await_then_pass(pool, scat[0], nblk * (8 * BLK))
            await_then_pass(pool, scat[1], nblk * (8 * BLK))
            pool.wait_ge(nt_st, 16 * 4)
            n = nc.gpsimd.value_load(ctl[0:1, 1:2], min_val=1, max_val=MAX_CHUNKS)
            with pool.Fori(0, n) as t:
                await_then_pass(pool, rowi_ok, t + 1)
                for r in range(CROWS):
                    pool.indirect_dma_start(chunk[:, r * ROW:(r + 1) * ROW], None, edge_rows,
                                            bass.IndirectOffsetOnAxis(ap=rowi[:, r:r + 1], axis=0)).then_inc(chunk_in, 16)
                await_then_pass(pool, src_ok, t + 1)
                for l in range(CW):
                    pool.indirect_dma_start(gath[:, l, :], None, node_tab,
                                            bass.IndirectOffsetOnAxis(ap=srci[:, l:l + 1], axis=0)).then_inc(gath_in, 16)
                pool.wait_ge(scan_st, 16 * t + 16)
                await_then_pass(pool, endi_ok, t + 1)
                for k in range(SLOTS):
                    pool.indirect_dma_start(seg[:, k, :], None, scan_tab,
                                            bass.IndirectOffsetOnAxis(ap=endi[:, k:k + 1], axis=0)).then_inc(seg_in, 16)

        @block.tensor
        def _(pe):
            pe.wait_ge(c_in, 16 * 5)
            for i in range(16):
                pe.wait_ge(x_in[i // 4], 16)
                if i >= 4:
                    pe.wait_ge(x_rows_out, i - 3)
                for k in range(4):
                    last = pe.matmul(wide[0:SIDE, (i % 4) * 512 + 32 * k:(i % 4) * 512 + 32 * k + 32],
                                     xs[:, 4 * i + k, :], waver[:, :], start=True, stop=True)
                last.then_inc(x_rows, 1)
            pe.wait_ge(x_rows_out, 16)
            for i in range(4):
                pe.matmul(wide[0:32, i * 512:i * 512 + 512], wave[:, :],
                          y1[:, 16 * i:16 * i + 16, :], start=True, stop=True).then_inc(x_cols, 1)
            pe.wait_ge(x_cols_out, 4)
            pe.wait_ge(tokwd_ok, 1)
            for i in range(4):
                for g in range(4):
                    lhs = y2[:, 8 * g + 2 * i:8 * g + 2 * i + 2, :].rearrange("n q b -> n (q b)")
                    last = pe.matmul(wide[:, i * 512:i * 512 + 512], lhs,
                                     tokwd[:, g, :, :], start=(g == 0), stop=(g == 3))
                last.then_inc(tok_mm, 1)
            edges_pe(pe)
            prep(pe)
            for r in range(LAYERS + 2):
                pe.wait_ge(u_ok, r + 1)
                transposes(pe, r)
                pe.wait_ge(t_ev, 5 * r + 5)
                if 1 <= r <= LAYERS:
                    l = r - 1
                    for i in range(PAIRS):
                        if i < 16:
                            pe.matmul(bank5[:, 0:65], uT[:, i, :], conv[:, l, 63 - 2 * i:128 - 2 * i],
                                      start=(i == 0), stop=False, skip_group_check=True)
                        else:
                            pe.matmul(bank5[0:64, 0:65], uT[0:64, 16, 0:64], conv[0:64, l, 64:129],
                                      start=False, stop=True, skip_group_check=True)
                linear(pe, r)
                for g in range(H_ROUND * r, H_ROUND * r + H_ROUND):
                    count_last_pe(pe, g)
            r = LAYERS + 2
            pe.wait_ge(u_ok, r + 1)
            transposes(pe, r)
            pe.wait_ge(t_ev, 5 * r + 5)
            for i in range(PAIRS):
                last = (pe.matmul(wide[:, 32 * i:32 * i + 32], uT[:, i, :], wg2[:, :, :], start=True, stop=True)
                        if i < 16 else
                        pe.matmul(wide[:, 512:512 + HE], uT[0:64, 16, :], wg2[0:64, 0, :], start=True, stop=True))
            last.then_inc(y_mm, 1)
            for g in range(H_ROUND * r, H_ROUND * r + H_ROUND):
                count_last_pe(pe, g)
            pe.wait_ge(nt_ok, 1)
            for k in range(9 * EXPERTS + 1):
                if k < 9 * EXPERTS:
                    e, t = divmod(k, 9)
                    if k >= 2:
                        pe.wait_ge(hid_ok, k - 1)
                    lo = 64 * (t % 2) if t < 8 else 0
                    rhs = uT[lo:lo + 64, 4 * (t // 2):4 * (t // 2) + 4, :] if t < 8 else uT[0:64, 16, :]
                    n = 512 if t < 8 else P
                    pe.matmul(wide[:, (k % 2) * 512:(k % 2) * 512 + n], w1[lo:lo + 64, e, :], rhs,
                              start=True, stop=True).then_inc(hid_mm, 1)
                if k >= 1:
                    e, t = divmod(k - 1, 9)
                    b = (k - 1) % 2
                    pe.wait_ge(hid_ok, k)
                    if k >= 3:
                        pe.wait_ge(ye_ev, k - 2)
                    for r4 in range(4 if t < 8 else 1):
                        last = pe.matmul(wide[:, (2 + b) * 512 + H * r4:(2 + b) * 512 + H * r4 + H],
                                         hidT[:, b, P * r4:P * r4 + P], w2[:, e, :], start=True, stop=True)
                    last.then_inc(ye_mm, 1)
            with pe.Fori(H_EARLY, H_GROUPS - 1) as g:
                count_last_pe(pe, g)
            count_last_pe(pe, H_GROUPS - 1, last_group=True)

        @block.vector
        def _(v):
            dve_prep(v)
            edges_dve(v)
            for i in range(4):
                v.wait_ge(tok_mm, i + 1)
                v.tensor_tensor(h0[:, 8 * i:8 * i + 8, :],
                                wide[:, i * 512:i * 512 + 512].rearrange("p (s h) -> p s h", h=H),
                                mid(tokb[:, :], 8), ALU.add)
            v.drain()
            dve_kernels(v)
            layer_norm(v, 1, h0[:, :, :], u[:, :, :])
            v.drain().then_inc(u_ok, 1)
            count_round(v, 0)
            v.wait_ge(y_mm, 1)
            v.tensor_tensor(u[:, :, :], wtok, mid(binr[:, :], SLOTS), ALU.add)
            v.drain().then_inc(u_ok, 1)
            count_round(v, 1)
            for l in range(LAYERS):
                v.wait_ge(y_mm, 2 + l)
                v.tensor_copy(yrow[:, :], bank5[:, 1:33])
                v.tensor_copy(yfar[64:128, :], bank5[0:64, 33:65])
                v.drain()
                v.tensor_tensor(yrow[64:128, :], yrow[64:128, :], yfar[64:128, :], ALU.add)
                v.drain()
                v.tensor_tensor(xc[:, 0:32, :], wtok[:, 0:32, :], bc(yrow[:, :], H), ALU.add)
                v.tensor_copy(xc[:, 32, :], wtok[:, 32, :])
                v.drain().then_inc(y_ok, 1)
                v.wait_ge(g_ok, l + 1)
                v.tensor_tensor(u[:, :, :], u[:, :, :], sq[:, :, :], ALU.add)
                v.drain()
                layer_norm(v, 2 + l, u[:, :, :], u[:, :, :])
                if l == LAYERS - 1:
                    layer_norm(v, 3 + l, u[:, :, :], u[:, :, :])
                v.drain().then_inc(u_ok, 1)
                count_round(v, l + 2)
            v.wait_ge(y_mm, LAYERS + 2)
            v.tensor_tensor(xc[:, :, :], wtok, mid(boutr[:, :], SLOTS), ALU.add)
            v.drain()
            v.tensor_tensor(h0[:, :, :], h0[:, :, :], xc[:, :, :], ALU.add)
            v.drain()
            layer_norm(v, LAYERS + 3, h0[:, :, :], u[:, :, :])
            v.drain().then_inc(u_ok, 1)
            count_round(v, LAYERS + 2)
            v.wait_ge(y_mm, LAYERS + 3)
            hp = wide[:, 0:SLOTS * HE].rearrange("p (s f) -> p s f", f=HE)
            v.tensor_copy(nt[:, :, HF], hp)
            for a, part in enumerate((AS, AD)):
                v.tensor_tensor(n16[:, a], hp, mid(att[:, a, :], SLOTS), ALU.mult)
                v.drain()
                v.reduce_sum(nt[:, :, part], n16[:, a].rearrange("p s (a b) -> p s a b", a=HEADS), axis=X)
            v.drain().then_inc(nt_ok, 1)
            chunk_rows(v, None)
            with v.Fori(H_EARLY, H_GROUPS - 1) as g:
                count_last_dve(v, g)
            count_last_dve(v, H_GROUPS - 1)
            v.wait_ge(h_used[0], H_GROUPS)
            v.wait_ge(h_used[1], H_GROUPS)
            v.tensor_copy(hsum[:, :], bank7[0:DHI, 0:DLO]).then_inc(hsum_ok, 1)
            graph_start(v)
            n = nc.vector.value_load(ctl[0:1, 1:2], min_val=1, max_val=MAX_CHUNKS)
            with v.Fori(0, n) as t:
                graph_chunk(v, t)
            graph_end(v, n)
            v.wait_ge(ye_ev, 9 * EXPERTS)
            for e in range(EXPERTS):
                v.tensor_tensor(ye[:, e], ye[:, e], mid(b2r[:, e, :], SLOTS), ALU.add)
            v.drain()
            v.wait_ge(gate_in, 16 * 3)
            for e in range(EXPERTS):
                v.tensor_tensor(ye[:, e], ye[:, e], bc(gtok[:, :, e], H), ALU.mult)
                v.drain()
                v.tensor_tensor(h0[:, :, :], h0[:, :, :], ye[:, e], ALU.add)
                v.drain()
            v.drain().then_inc(done_dve, 1)


_INS = {'x': 'x', 'cls_tok': 'cls_tok', 'L0_tok_W': 'tok_W', 'L0_tok_b': 'tok_b', 'L0_attn_Win': 'Win',
        'L0_attn_bin_': 'bin_', 'L0_attn_Wout': 'Wout', 'L0_attn_bout': 'bout', 'L0_attn_A': 'A',
        'L0_attn_Bm': 'Bm', 'L0_attn_Cm': 'Cm', 'L0_attn_Dm': 'Dm', 'L0_ffn_W_gat': 'W_gat',
        'L0_ffn_att_src': 'att_src', 'L0_ffn_att_dst': 'att_dst', 'L0_ffn_b_gat': 'b_gat',
        'L0_ffn_ln_gamma': 'ln_gamma', 'L0_ffn_ln_beta': 'ln_beta', 'L0_ffn_W1': 'W1', 'L0_ffn_b1': 'b1',
        'L0_ffn_W2': 'W2', 'L0_ffn_b2': 'b2', 'L0_ffn_edge_index': 'edge_index'}


def kernel(**inputs):
    import concourse.bacc as bacc
    from concourse.bass_utils import run_bass_kernel_spmd

    nc = bacc.Bacc("TRN2", target_bir_lowering=False, num_devices=1)
    arrays, args = {}, {}
    for name, short in _INS.items():
        arrays[f"in_{short}"] = np.ascontiguousarray(inputs[name])
        args[short] = f"in_{short}"
    for name, a in constants().items():
        arrays[name] = a
        args[name] = name
    args = {k: nc.dram_tensor(n, arrays[n].shape, mybir.dt.from_np(arrays[n].dtype), kind="ExternalInput").ap()
            for k, n in args.items()}
    out = nc.dram_tensor("out_h", (IMAGES, TOK, H), F32, kind="ExternalOutput").ap()
    tower(nc, **args, out=out)
    r = run_bass_kernel_spmd(nc, [arrays], core_ids=[0])
    return r.results[0]["out_h"]
```

```python
from contextlib import ExitStack

import numpy as np
import concourse.bass as bass
from concourse import mybir

F32 = mybir.dt.float32
BF16 = mybir.dt.bfloat16
I32 = mybir.dt.int32
U32 = mybir.dt.uint32
ALU = mybir.AluOpType
ACT = mybir.ActivationFunctionType
X = mybir.AxisListType.X

P = 128
IMAGES, SIDE = 64, 96
TOK, H = 65, 64
NODES = IMAGES * TOK
SLOTS = 33
PAIRS = 17
LAYERS = 4
HEADS, EXPERTS, HE = 4, 4, 16
HID = 128
EDGES = 262144
ECOL = EDGES // P
EPS = 1e-5
NF = 24
NODE_ROWS = P * SLOTS
BLK = 16
BIG = 64
PARTS = 4
TAKE = 64
KEY0 = NODES // 2
DEAD = -4.0e9
LIVE = -1.0e8
ROW = 64
CROWS = 3
CW = CROWS * ROW
PSTEP = 48
LIST_ROWS = EDGES // ROW + P + 8
LAST_ROW = LIST_ROWS - 1
FAR = 1.0e6
HCOL = 256
DHI, DLO = 65, 64


def wavelet_operator():
    def resize(n):
        s = n / 8.0
        at = (np.arange(8) + 0.5) * s - 0.5
        w = np.maximum(0.0, 1.0 - np.abs(at[:, None] - np.arange(n)[None, :]) / s)
        return w / w.sum(1, keepdims=True)

    def haar(n, sign):
        m = np.zeros((n // 2, n))
        m[np.arange(n // 2), 2 * np.arange(n // 2)] = 0.7071067811865476
        m[np.arange(n // 2), 2 * np.arange(n // 2) + 1] = sign * 0.7071067811865476
        return m

    lo1, hi1, lo2, hi2 = haar(96, 1), haar(96, -1), haar(48, 1), haar(48, -1)
    rows = [resize(24) @ lo2 @ lo1, resize(24) @ hi2 @ lo1, resize(48) @ lo1, resize(48) @ hi1]
    return np.ascontiguousarray(np.concatenate(rows).T.astype(np.float32))


MAPS = [(0, 0), (1, 0), (0, 1), (1, 1), (3, 2), (2, 3), (3, 3)]


def constants():
    eye = np.eye(P, dtype=np.float32)
    before = np.triu(np.ones((P, P), np.float32), 1)
    pick = np.zeros((32, 8), np.float32)
    pick[np.arange(32), np.arange(32) % 8] = 1
    wave = wavelet_operator()
    order = [8 * g + 4 * q + i for g in range(4) for i in range(4) for q in range(2)]
    return {"c_eye": eye, "c_before": before, "c_pick": pick, "c_wave": wave,
            "c_waver": np.ascontiguousarray(wave[:, order])}


def tower(nc, x, cls_tok, tok_W, tok_b, Win, bin_, Wout, bout, A, Bm, Cm, Dm, W_gat, att_src, att_dst,
          b_gat, ln_gamma, ln_beta, W1, b1, W2, b2, edge_index, c_eye, c_before, c_pick, c_wave, c_waver, out,
          dbg=None):
    with ExitStack() as ctx:
        def sb(name, shape, dt=F32):
            return ctx.enter_context(nc.sbuf_tensor(name, shape, dt))

        def ps(name, shape, dt=F32):
            return ctx.enter_context(nc.psum_tensor(name, shape, dt))

        def sem(name):
            return ctx.enter_context(nc.semaphore(name))

        def rep(ap, n):
            return ap.rearrange("(a f) -> a f", a=1).broadcast_to([n, ap.shape[0]])

        def cut(flat):
            at = [0]

            def take(parts, *shape):
                n = int(np.prod(shape))
                ap = flat[0:parts, at[0]:at[0] + n]
                at[0] += n
                assert at[0] <= flat.shape[1]
                names = "abcd"[:len(shape)]
                if len(shape) == 1:
                    return ap
                return ap.rearrange(f"p ({' '.join(names)}) -> p {' '.join(names)}",
                                    **dict(zip(names[1:], shape[1:])))
            return take

        node_tab = nc.dram_tensor("node_tab", [NODE_ROWS, NF], F32).ap()
        edge_list = nc.dram_tensor("edge_list", [LIST_ROWS * ROW, 1], F32).ap()
        edge_rows = edge_list.rearrange("(r c) a -> r (c a)", c=ROW)
        scan_tab = nc.dram_tensor("scan_tab", [P * CW, NF], F32).ap()
        last_tab = nc.dram_tensor("last_tab", [NODE_ROWS], F32).ap()
        gate_tab = nc.dram_tensor("gate_tab", [NODE_ROWS, EXPERTS], F32).ap()

        eye = sb("eye", [P, P])
        before = sb("before", [P, P])
        pick = sb("pick", [32, 8])
        wave = sb("wave", [SIDE, 32])
        waver = sb("waver", [SIDE, 32])
        tokb = sb("tokb", [P, H])
        wlin = sb("wlin", [P, 6, P])
        binr = sb("binr", [P, H])
        boutr = sb("boutr", [P, H])
        mean64 = sb("mean64", [H, 1])
        conv = sb("conv", [P, LAYERS, 132])
        early = sb("early", [P, IMAGES * (SIDE + 32) + 2048])
        xs = early[0:SIDE, 0:IMAGES * SIDE].rearrange("p (b c) -> p b c", c=SIDE)
        y1 = early[0:SIDE, IMAGES * SIDE:IMAGES * (SIDE + 32)].rearrange("p (b m) -> p b m", m=32)
        y2 = early[0:32, IMAGES * (SIDE + 32):].rearrange("p (m b) -> p m b", b=IMAGES)
        scans = early[:, 0:CW * NF].rearrange("p (l f) -> p l f", f=NF)
        ye = sb("ye", [P, EXPERTS, SLOTS, H])
        prep_room = cut(ye[:, :, :, :].rearrange("p e s h -> p (e s h)"))
        tokwd = prep_room(32, 4, 8, H)
        win2 = prep_room(P, 6, P)
        a_pow = prep_room(H, 2, LAYERS, H)
        a_powT = prep_room(H, 2, LAYERS, H)
        bm = prep_room(H, LAYERS, 2, H)
        cm = prep_room(H, LAYERS, H)
        vee = prep_room(H, LAYERS, H)
        zeros = prep_room(P, 529)
        tokw = prep_room(32, 4, H)
        h0 = sb("h0", [P, SLOTS, H])
        u = sb("u", [P, SLOTS, H])
        xc = sb("xc", [P, SLOTS, H])
        sq = sb("sq", [P, SLOTS, H])
        s1 = sb("s1", [P, SLOTS])
        s2 = sb("s2", [P, SLOTS])
        s3 = sb("s3", [P, SLOTS])
        uT = sb("uT", [P, PAIRS, P])
        yrow = sb("yrow", [P, 32])
        yfar = sb("yfar", [P, 32])
        late = sb("late", [P, 4 * ECOL])
        raw = late[:, 0:2 * ECOL].bitcast(I32).rearrange("p (a e) -> p a e", a=2)
        srcf = late[:, 2 * ECOL:3 * ECOL]
        etmp = late[:, 3 * ECOL:4 * ECOL]
        gath = late[:, 0:CW * NF].rearrange("p (l f) -> p l f", f=NF)
        key = sb("key", [P, ECOL + PARTS * TAKE])
        tabs = sb("tabs", [P, 2 * ECOL])
        cls_tab = tabs[:, 0:ECOL]
        lkey_tab = tabs[:, ECOL:]
        rank_tab = cls_tab.bitcast(U32)
        top = sb("top", [P, BLK])
        jrow = sb("jrow", [P, BIG])
        oh = sb("oh", [P, 2, BLK, P], BF16)
        hidT = oh[:, :, :, :].rearrange("p q j c -> p (q j c)").bitcast(F32)[:, 0:1024].rearrange(
            "p (b n) -> p b n", b=2)
        ones_f = sb("ones_f", [P, 1])
        eye_b = sb("eye_b", [P, P], BF16)
        spread_h = ye[:, :, :, :].rearrange("p e s h -> p (e s h)").bitcast(BF16)[:, 0:DHI * HCOL].rearrange(
            "p (v j) -> p v j", j=HCOL)
        spread_l = early[:, 0:DLO * HCOL // 2].bitcast(BF16).rearrange("p (v j) -> p v j", j=HCOL)
        hcode = sb("hcode", [P, 2, ECOL], BF16)
        rank_room = cut(etmp)
        counts, countsT = rank_room(P, P), rank_room(P, P)
        base = rank_room(P, P)
        nafter = rank_room(P, P)
        rows64r, before64 = rank_room(P, P), rank_room(P, P)
        cw, ranks = rank_room(P, 4, BIG), rank_room(P, BIG)
        late_room = cut(late[:, CW * NF:])
        adst, eh, mh, rh = (late_room(P, HEADS, CW) for _ in range(4))
        tabs_room = cut(tabs[:, :])
        xh, wh = tabs_room(P, HE, CW), tabs_room(P, HEADS, CW)
        place_m = tabs[:, 0:SLOTS * CW // 2].bitcast(BF16)
        unused = early[:, DLO * HCOL // 2:].bitcast(BF16).rearrange("p (a b) -> p a b", b=P)
        place_f = cut(early[:, DLO * HCOL // 2:])(P, PSTEP * SLOTS)
        key_room = cut(key[:, :])
        chunk, skey, place, keep, ctmp = (key_room(P, CW) for _ in range(5))
        seg = key_room(P, SLOTS, NF)
        xc_room = cut(xc[:, :, :].rearrange("p s h -> p (s h)"))
        nn, st = xc_room(P, SLOTS, NF), xc_room(P, SLOTS, NF)
        sq_room = cut(sq[:, :, :].rearrange("p s h -> p (s h)"))
        n16, nt = sq_room(P, 2, SLOTS, HE), sq_room(P, SLOTS, NF)
        u_room = cut(u[:, :, :].rearrange("p s h -> p (s h)"))
        n4, gates, gtok = u_room(P, 8, SLOTS, HEADS), u_room(P, SLOTS, EXPERTS), u_room(P, SLOTS, EXPERTS)
        lastc = u_room(P, SLOTS)
        iota = sb("iota", [P, CW])
        iota_b = sb("iota_b", [P, P], BF16)
        zero_b = sb("zero_b", [P, P], BF16)
        junk = sb("junk", [P, P])
        ecnt = sb("ecnt", [P, 8])
        ctl = sb("ctl", [1, 4], I32)
        rows64 = sb("rows64", [P, 1], I32)
        ring_i = sb("ring_i", [P, 2, BLK // 2], U32)
        ring_k = sb("ring_k", [P, 2, BLK // 2])
        wg2 = sb("wg2", [P, 2, HE])
        att = sb("att", [P, 2, HE])
        lastr = sb("lastr", [P, NF])
        hsum = sb("hsum", [DHI, DLO])
        rowi = sb("rowi", [P, CROWS], U32)
        rowf = sb("rowf", [P, CROWS])
        srci = sb("srci", [P, CW], U32)
        ends = sb("ends", [P, SLOTS + 1])
        endi = sb("endi", [P, SLOTS], U32)
        has = sb("has", [P, SLOTS])
        gamr = sb("gamr", [P, 3, HE])
        w1 = sb("w1", [P, EXPERTS, HID])
        w2 = sb("w2", [HID, EXPERTS, H])
        b1c = sb("b1c", [HID, EXPERTS])
        b2r = sb("b2r", [P, EXPERTS, H])

        wide = ps("wide", [P, 5 * 512])
        bank5 = ps("bank5", [P, 512])
        bank6 = ps("bank6", [P, 512])
        bank7 = ps("bank7", [P, 512])
        wtok = wide[:, 0:SLOTS * H].rearrange("p (s h) -> p s h", h=H)

        c_in = sem("const_loaded")
        w_in = sem("weights_loaded")
        x_in = [sem(f"x_loaded{i}") for i in range(4)]
        zero_ok = sem("weight_tiles_zeroed")
        tokwd_ok = sem("token_weights_spread")
        x_rows = sem("rows_mapped")
        x_rows_out = sem("rows_evacuated")
        x_cols = sem("columns_mapped")
        x_cols_out = sem("columns_evacuated")
        tok_mm = sem("tokens_multiplied")
        tok_out = sem("tokens_evacuated")
        prep_mm = sem("prep_products")
        prep_ev = sem("prep_evacuated")
        u_ok = sem("normed_ready")
        t_mm = sem("transposed")
        t_ev = sem("transposed_evacuated")
        y_mm = sem("mixed")
        y_ok = sem("mixed_summed")
        g_ok = sem("gelu_done")
        var_ok = sem("variance_ready")
        rt_ok = sem("root_ready")
        d_out = sem("output_stored")
        e_in = sem("edges_loaded")
        pool_passed = sem("pool_passed_a_wait")
        pool_c = sem("pool_constants_ready")
        nblk_ok = sem("block_count_ready")
        ctl_mm = sem("counts_transposed")
        oh_ok = [sem("classes_spread0"), sem("classes_spread1")]
        oh_used = [sem("classes_counted0"), sem("classes_counted1")]
        cnt_ev = sem("counts_read")
        start_mm = sem("list_starts_ready")
        base_mm = sem("list_places_ready")
        rank_ok = sem("ranks_ready")
        chunk_ok = sem("chunk_count_ready")
        scat = [sem("scattered0"), sem("scattered1")]
        list_zero = sem("list_zeroed")
        h_ok = sem("last_spread")
        h_used = sem("last_counted")
        hsum_ok = sem("last_count_ready")
        hsum_st = sem("last_count_stored")
        hsum_in = sem("last_count_loaded")
        nt_ok = sem("node_rows_ready")
        nt_st = sem("node_rows_stored")
        nn_in = sem("node_rows_loaded")
        rowi_ok = sem("chunk_rows_known")
        chunk_in = sem("chunk_loaded")
        fetched = sem("rows_fetched")
        src_ok = sem("chunk_sources_known")
        gath_in = sem("source_rows_gathered")
        a_req = sem("exponents_ready")
        a_done = sem("exponentials_done")
        scan_ok = sem("scans_ready")
        scan_st = sem("scans_stored")
        endi_ok = sem("segment_ends_known")
        seg_in = sem("segment_ends_gathered")
        seg_used = sem("segments_merged")
        hid_mm = sem("hidden_multiplied")
        hid_ok = sem("hidden_activated")
        ye_mm = sem("expert_multiplied")
        ye_ev = sem("expert_evacuated")
        gate_ok = sem("gates_ready")
        gate_st = sem("gates_stored")
        gate_in = sem("gates_loaded")
        done_dve = sem("result_ready")

        block = ctx.enter_context(nc.Block())
        DVE, PE, SC, PL = nc.vector, nc.tensor, nc.scalar, nc.gpsimd

        def bc(ap2, n):
            return ap2.unsqueeze(2).broadcast_to([ap2.shape[0], ap2.shape[1], n])

        def mid(ap2, n):
            return ap2.unsqueeze(1).broadcast_to([ap2.shape[0], n, ap2.shape[1]])

        LIN_IN, LIN_OUT = 0, 5
        X_PARTS = 4
        NX = IMAGES // X_PARTS
        MAX_BLK = ECOL // BLK
        MAX_CHUNKS = EDGES // CW + 1
        MAGIC = 12582912.0
        H_GROUPS = ECOL // HCOL
        AS, AD, HF = slice(0, 4), slice(4, 8), slice(8, 24)
        MX, DN, NM = slice(0, 4), slice(4, 8), slice(8, 24)

        def store_tokens(eng, table, tile, width, s):
            rows = table[0:NODES].rearrange("(b t) h -> b t h", t=TOK)
            for half in range(2):
                eng.dma_start(rows[:, 1 + 32 * half:33 + 32 * half, :],
                              tile[64 * half:64 * half + 64, 0:32, 0:width]).then_inc(s, 16)
            eng.dma_start(rows[:, 0, :], tile[0:64, 32, 0:width]).then_inc(s, 16)

        weight_dmas = []
        for m, (g, gc) in enumerate(MAPS):
            weight_dmas.append((tokw[gc * 8:gc * 8 + 8, g, :], rep(tok_W[m], 8)))
        for i, w in enumerate([Win] + [Dm[l] for l in range(LAYERS)] + [Wout]):
            for q in range(2):
                weight_dmas.append((win2[64 * q:64 * q + 64, i, 64 * q:64 * q + 64], w))
        weight_dmas += [
            (tokb[:, :], rep(tok_b, P)), (binr[:, :], rep(bin_, P)), (boutr[:, :], rep(bout, P)),
            (a_pow[:, 0, :, :], A.rearrange("l n m -> n l m")),
            (bm[:, :, 0, :], Bm.rearrange("l n h -> n l h")),
            (cm[:, :, :], Cm.rearrange("l a n -> a l n")),
            (h0[0:64, 32, :], cls_tok[0, 0:1, :].broadcast_to([64, H])),
            (wg2[0:64, 0, :], W_gat), (wg2[64:128, 1, :], W_gat),
            (att[:, 0, :], rep(att_src.rearrange("a b -> (a b)"), P)),
            (att[:, 1, :], rep(att_dst.rearrange("a b -> (a b)"), P)),
            (gamr[:, 0, :], rep(b_gat, P)), (gamr[:, 1, :], rep(ln_gamma, P)), (gamr[:, 2, :], rep(ln_beta, P)),
            (w1[0:64, :, :], W1.rearrange("e h f -> h e f")), (w1[64:128, :, :], W1.rearrange("e h f -> h e f")),
            (w2[:, :, :], W2.rearrange("e f h -> f e h")), 
            (b2r[:, :, :].rearrange("p e h -> p (e h)"), rep(b2.rearrange("e h -> (e h)"), P)),
        ]

        def count_last_dve(v, g):
            if g:
                v.wait_ge(h_used, g)
            cols = slice(g * HCOL, (g + 1) * HCOL)
            for a, spread, n in ((0, spread_h, DHI), (1, spread_l, DLO)):
                for d in range(n):
                    v.tensor_scalar(spread[:, d, :], hcode[:, a, cols], float(d), None, ALU.is_equal)
            v.drain().then_inc(h_ok, 1)

        def count_last_pe(pe, g):
            pe.wait_ge(h_ok, g + 1)
            for j in range(HCOL):
                m = pe.matmul(bank7[0:DHI, 0:DLO], spread_h[:, :, j], spread_l[:, :, j],
                              start=(g == 0 and j == 0), stop=(g == H_GROUPS - 1 and j == HCOL - 1),
                              skip_group_check=True)
            m.then_inc(h_used, 1)

        def evacuate_T(act, r):
            for k in range(5):
                act.wait_ge(t_mm, 5 * r + k + 1)
                if k < 4:
                    act.activation(uT[:, 4 * k:4 * k + 4, :],
                                   wide[:, 512 * k:512 * k + 512].rearrange("p (s f) -> p s f", f=P),
                                   ACT.Copy).then_inc(t_ev, 1)
                else:
                    act.activation(uT[0:64, 16, :], wide[0:64, 2048:2048 + P], ACT.Copy).then_inc(t_ev, 1)

        def ye_slots(k):
            e, t = divmod(k, 9)
            if t == 8:
                return ye[:, e, 32:33, :]
            q, s2 = t // 2, t % 2
            return ye[:, e, 8 * q:8 * q + 8, :].rearrange("p (r s) h -> p s r h", s=2)[:, s2]

        def ye_evacuate(act, k):
            n = 4 if k % 9 < 8 else 1
            act.wait_ge(ye_mm, k + 1)
            act.activation(ye_slots(k), wide[:, (2 + k % 2) * 512:(2 + k % 2) * 512 + n * H].rearrange(
                "p (r h) -> p r h", h=H), ACT.Copy).then_inc(ye_ev, 1)

        def root(act, n):
            act.wait_ge(var_ok, n)
            act.activation(s3[:, :], s2[:, :], ACT.Sqrt).then_inc(rt_ok, 1)

        def transposes(pe, r):
            for k in range(5):
                for i in range(4 * k, min(4 * k + 4, PAIRS)):
                    last = (pe.transpose(wide[:, 128 * i:128 * i + 128], u[:, 2 * i:2 * i + 2, :], eye[:, :])
                            if i < 16 else
                            pe.transpose(wide[0:64, 2048:2048 + P], u[:, 32, :], eye[:, :]))
                last.then_inc(t_mm, 1)

        def mix(pe, l):
            for i in range(PAIRS):
                if i < 16:
                    pe.matmul(bank5[:, 0:65], uT[:, i, :], conv[:, l, 63 - 2 * i:128 - 2 * i],
                              start=(i == 0), stop=False, skip_group_check=True)
                else:
                    pe.matmul(bank5[0:64, 0:65], uT[0:64, 16, 0:64], conv[0:64, l, 64:129],
                              start=False, stop=True, skip_group_check=True)

        def linear(pe, w):
            for i in range(PAIRS):
                last = (pe.matmul(wide[:, 128 * i:128 * i + 128], uT[:, i, :], wlin[:, w, :], start=True, stop=True)
                        if i < 16 else
                        pe.matmul(wide[:, 2048:2048 + H], uT[0:64, 16, :], wlin[0:64, w, 0:64], start=True, stop=True))
            last.then_inc(y_mm, 1)

        def bounds_pe(pe):
            pe.wait_ge(ctl_mm, 1)
            pe.transpose(bank6[0:1, 0:P], ecnt[:, 0:1], eye[:, :])
            pe.transpose(bank6[0:1, P:2 * P], ecnt[:, 6:7], eye[:, :]).then_inc(ctl_mm, 1)

        def edges_pe(pe):
            pe.wait_ge(nblk_ok, 1)
            nbig = nc.tensor.value_load(ctl[0:1, 2:3], min_val=1, max_val=ECOL // BIG)
            m = pe.matmul(bank6[:, 256:384], eye_b[:, :], zero_b[:, :], start=True, stop=False,
                          skip_group_check=True)
            m.then_inc(oh_used[0], 1)
            m = pe.matmul(bank6[:, 256:384], eye_b[:, :], zero_b[:, :], start=False, stop=False,
                          skip_group_check=True)
            m.then_inc(oh_used[1], 1)
            with pe.Fori(0, nbig) as i:
                for q in range(BIG // BLK):
                    pe.wait_ge(oh_ok[q % 2], i * (BIG // BLK // 2) + (q // 2 + 1))
                    for j in range(BLK):
                        m = pe.matmul(bank6[:, 256:384], eye_b[:, :], oh[:, q % 2, j, :], start=False, stop=False,
                                      skip_group_check=True)
                    m.then_inc(oh_used[q % 2], 1)
            pe.matmul(bank6[:, 256:384], eye_b[:, :], zero_b[:, :], start=False, stop=True,
                      skip_group_check=True).then_inc(cnt_ev, 1)
            pe.wait_ge(cnt_ev, 2)
            pe.matmul(bank6[:, 0:1], counts[:, :], ones_f[:, :], start=True, stop=True)
            pe.transpose(bank6[:, 384:512], counts[:, :], eye[:, :]).then_inc(start_mm, 1)
            pe.wait_ge(cnt_ev, 3)
            pe.transpose(bank6[0:1, 128:256], ecnt[:, 1:2], eye[:, :])
            pe.matmul(bank6[:, 2:3], before[:, :], ecnt[:, 2:3], start=True, stop=True)
            pe.matmul(bank6[:, 256:384], rows64r[:, :], before64[:, :], start=True, stop=False)
            pe.matmul(bank6[:, 256:384], before[:, :], counts[:, :], start=False, stop=False)
            pe.matmul(bank6[:, 256:384], countsT[:, :], nafter[:, :], start=False, stop=True).then_inc(base_mm, 1)

        def prep(pe):
            n = 0
            pe.wait_ge(w_in, 16 * (len(weight_dmas) + 1))
            for i in range(6):
                b = [bank5, bank6, bank7][i % 3]
                if i >= 3:
                    pe.wait_ge(prep_ev, i - 2)
                pe.transpose(b[:, 0:P], win2[:, i, :], eye[:, :]).then_inc(prep_mm, 1)
            pe.wait_ge(prep_ev, 6)
            for l in range(LAYERS):
                pe.transpose(bank5[0:64, 64 * l:64 * l + 64], a_pow[:, 0, l, :], eye[0:64, 0:64])
                last = pe.matmul(bank6[0:64, l:l + 1], cm[:, l, :], mean64[:, :], start=True, stop=True)
            last.then_inc(prep_mm, 1)
            n = 7
            for d in range(6):
                pe.wait_ge(prep_ev, n)
                c, w = d % 2, 1 << d
                for l in range(LAYERS):
                    last = pe.matmul(bank6[0:64, 64 * l:64 * l + w], a_pow[:, c, l, :], vee[:, l, 0:w],
                                     start=True, stop=True)
                    if d < 5:
                        pe.matmul(bank5[0:64, 64 * l:64 * l + 64], a_powT[:, c, l, :], a_pow[:, c, l, :],
                                  start=True, stop=True)
                        last = pe.matmul(bank7[0:64, 64 * l:64 * l + 64], a_pow[:, c, l, :], a_powT[:, c, l, :],
                                         start=True, stop=True)
                last.then_inc(prep_mm, 1)
                n += 1
            pe.wait_ge(prep_ev, n)
            for l in range(LAYERS):
                last = pe.matmul(bank5[:, 64 * l:64 * l + 64], bm[:, l, :, :], vee[:, l, :], start=True, stop=True)
            last.then_inc(prep_mm, 1)
            pe.wait_ge(prep_ev, n + 1)

        def dve_prep(v):
            v.wait_ge(c_in, 16 * 5)
            v.wait_ge(w_in, 16 * (len(weight_dmas) + 1))
            for g in range(4):
                v.tensor_tensor(tokwd[:, g, :, :], mid(tokw[:, g, :], 8), bc(pick[:, :], H), ALU.mult)
            v.tensor_copy(bm[:, :, 1, :], bm[:, :, 0, :])
            v.drain().then_inc(tokwd_ok, 1)

        def kernel_step(v, n):
            v.wait_ge(prep_mm, n + 1)
            if n < 6:
                v.tensor_copy(wlin[:, n, :], [bank5, bank6, bank7][n % 3][:, 0:P])
            elif n == 6:
                v.tensor_copy(a_powT[:, 0, :, :], by_layer(bank5))
                v.tensor_copy(vee[:, :, 0:1], bank6[0:64, 0:LAYERS].unsqueeze(2))
            elif n < 13:
                d = n - 7
                c, w = 1 - d % 2, 1 << d
                if d < 5:
                    v.tensor_copy(a_pow[:, c, :, :], by_layer(bank5))
                    v.tensor_copy(a_powT[:, c, :, :], by_layer(bank7))
                v.tensor_copy(vee[:, :, w:2 * w], by_layer(bank6)[:, :, 0:w])
            else:
                w = bank5[:, 0:256].rearrange("p (l m) -> p l m", l=LAYERS)
                v.tensor_copy(conv[0:64, :, 65:129], w[0:64])
                v.tensor_copy(conv[64:128, :, 66:130], w[64:128])
            v.drain().then_inc(prep_ev, 1)

        def by_layer(bank):
            return bank[0:64, 0:256].rearrange("p (l m) -> p l m", l=LAYERS)

        def layer_norm(v, n, src, dst):
            v.reduce_sum(s1[:, :], src, axis=X)
            v.drain()
            v.tensor_scalar(s1[:, :], s1[:, :], 1.0 / H, None, ALU.mult)
            v.drain()
            v.tensor_tensor(xc[:, :, :], src, bc(s1[:, :], H), ALU.subtract)
            v.drain()
            v.tensor_tensor(sq[:, :, :], xc[:, :, :], xc[:, :, :], ALU.mult)
            v.drain()
            v.reduce_sum(s2[:, :], sq[:, :, :], axis=X)
            v.drain()
            v.tensor_scalar(s2[:, :], s2[:, :], 1.0 / H, EPS, ALU.mult, ALU.add).then_inc(var_ok, 1)
            v.wait_ge(rt_ok, n)
            v.reciprocal(s1[:, :], s3[:, :])
            v.drain()
            v.tensor_tensor(dst, xc[:, :, :], bc(s1[:, :], H), ALU.mult)
            v.drain()

        def fetch(pool, tiles, table, index, signal, before):
            for k, tile in enumerate(tiles):
                pool.indirect_dma_start(tile, None, table, bass.IndirectOffsetOnAxis(ap=index[:, k:k + 1], axis=0))\
                    .then_inc(fetched, 16)
            pool.wait_ge(fetched, 16 * (before + len(tiles)))
            pool.sem_inc(signal, 1)

        def chunk_pool(pool, t):
            fetch(pool, [gath[:, l, :] for l in range(CW)], node_tab, srci, gath_in, CROWS)
            await_then_pass(pool, scan_st, t * 16 + 16)
            await_then_pass(pool, endi_ok, t + 1)
            fetch(pool, [seg[:, k, :] for k in range(SLOTS)], scan_tab, endi, seg_in, CROWS + CW)

        def await_then_pass(pool, s, value):
            pool.wait_ge(s, value)
            pool.sem_inc(pool_passed, 1)

        def scatter_block(pool, i):
            for h in range(2):
                c = i * BLK + h * (BLK // 2)
                if not (isinstance(i, int) and i == 0):
                    pool.wait_ge(scat[h], i * (8 * BLK))
                pool.tensor_copy(ring_i[:, h, :], rank_tab[:, bass.ds(c, BLK // 2)])
                pool.tensor_copy(ring_k[:, h, :], lkey_tab[:, bass.ds(c, BLK // 2)])
                pool.drain()
                for j in range(BLK // 2):
                    pool.indirect_dma_start(
                        edge_list, bass.IndirectOffsetOnAxis(ap=ring_i[:, h, j:j + 1], axis=0),
                        ring_k[:, h, j:j + 1], None, bounds_check=LIST_ROWS * ROW - 1,
                        oob_is_err=False).then_inc(scat[h], 16)

        def round_to(v, ap):
            v.tensor_scalar(ap, ap, MAGIC, MAGIC, ALU.add, ALU.subtract)
            v.drain()

        def keys_dve(v):
            keys = key[:, 0:ECOL]
            v.wait_ge(e_in, 32)
            v.tensor_copy(keys, raw[:, 1, :])
            v.tensor_scalar(srcf, raw[:, 0, :], float(NODES - 1), None, ALU.min)
            v.drain()
            v.tensor_scalar(etmp, keys, float(NODES), DEAD, ALU.is_ge, ALU.mult)
            v.drain()
            v.tensor_scalar(keys, keys, float(-KEY0), float(NODES), ALU.add, ALU.mult)
            v.drain()
            v.tensor_tensor(keys, keys, srcf, ALU.add)
            v.drain()
            v.tensor_tensor(keys, keys, etmp, ALU.add)
            v.drain()
            v.tensor_scalar(etmp, srcf, float(NODES - 1), DEAD, ALU.is_ge, ALU.mult)
            v.drain()
            v.tensor_tensor(keys, keys, etmp, ALU.add)
            v.drain()
            v.tensor_scalar(etmp, keys, LIVE, 0.0, ALU.is_ge, ALU.add, accum_out=ecnt[:, 0:1])
            v.drain()
            v.tensor_scalar(srcf, srcf, float(NODES - 1), 1024.0, ALU.is_lt, ALU.mult)
            v.tensor_scalar(etmp.bitcast(I32), raw[:, 1, :], 6, None, ALU.logical_shift_right)
            v.drain()
            v.tensor_tensor(hcode[:, 0, :], etmp.bitcast(I32), srcf, ALU.add)
            v.drain()
            v.tensor_scalar(etmp.bitcast(I32), raw[:, 1, :], DLO - 1, None, ALU.bitwise_and)
            v.drain()
            v.tensor_copy(hcode[:, 1, :], etmp.bitcast(I32))
            v.drain()
            v.wait_ge(c_in, 16 * 5)
            v.wait_ge(pool_c, 1)
            v.tensor_copy(eye_b[:, :], eye[:, :])
            v.tensor_scalar(before64[:, :], before[:, :], float(ROW), None, ALU.mult)
            v.tensor_tensor(nafter[:, :], before[:, :], eye[:, :], ALU.add)
            v.memset(lkey_tab, 4 * DEAD)
            v.tensor_copy(jrow[:, :], iota[:, 0:BIG])
            v.drain()
            v.tensor_scalar(nafter[:, :], nafter[:, :], -1.0, None, ALU.add)
            v.drain()

        def take_round(v, k):
            n = ECOL // PARTS
            for q in range(PARTS):
                v.max(key[:, ECOL + q * TAKE + 8 * k:ECOL + q * TAKE + 8 * k + 8], key[:, q * n:(q + 1) * n])
            v.drain()
            for q in range(PARTS):
                v.match_replace(key[:, q * n:(q + 1) * n], key[:, ECOL + q * TAKE + 8 * k:ECOL + q * TAKE + 8 * k + 8],
                                key[:, q * n:(q + 1) * n], 4 * DEAD)
            v.drain()

        def bounds_dve(v):
            v.tensor_reduce(ecnt[:, 6:7], key[:, ECOL + TAKE - 1:ECOL + PARTS * TAKE:TAKE], axis=X, op=ALU.max)
            v.drain().then_inc(ctl_mm, 1)
            v.wait_ge(ctl_mm, 2)
            v.reduce_max(junk[0:1, 0:1], bank6[0:1, 0:P], axis=X)
            v.reduce_max(junk[0:1, 1:2], bank6[0:1, P:2 * P], axis=X)
            v.drain()
            v.tensor_scalar(ctl[0:1, 3:4], junk[0:1, 1:2], LIVE, None, ALU.is_ge)
            to_blocks(v, ctl[0:1, 0:1], junk[0:1, 0:1], BLK - 1, 4, 2)
            to_blocks(v, ctl[0:1, 2:3], junk[0:1, 0:1], BIG - 1, 6, 1)
            v.drain().then_inc(nblk_ok, 1)

        def order_dve(v, nblk, keys):
            with v.Fori(0, nblk) as i:
                for q in range(BLK // 8):
                    v.max(top[:, 8 * q:8 * q + 8], keys)
                    v.drain()
                    v.match_replace(keys, top[:, 8 * q:8 * q + 8], keys, 4 * DEAD)
                    v.drain()
                v.tensor_copy(lkey_tab[:, bass.ds(i * BLK, BLK)], top[:, :])
                v.drain()

        def extract_dve(v):
            nblk = nc.vector.value_load(ctl[0:1, 0:1], min_val=2, max_val=MAX_BLK)
            more = nc.vector.value_load(ctl[0:1, 3:4], min_val=0, max_val=1)
            with v.If(more == 1):
                order_dve(v, nblk, key[:, :])
            with v.Else():
                order_dve(v, nblk, key[:, ECOL:])
            v.drain()

        def rank_dve(v):
            nbig = nc.vector.value_load(ctl[0:1, 2:3], min_val=1, max_val=ECOL // BIG)
            with v.Fori(0, nbig) as i:
                q_, r_, t_, c_ = cw[:, 0, :], cw[:, 1, :], cw[:, 2, :], cw[:, 3, :]
                keys = lkey_tab[:, bass.ds(i * BIG, BIG)]
                v.tensor_scalar(q_, keys, -0.5 * (NODES - 1), 1.0 / NODES, ALU.add, ALU.mult)
                v.drain()
                round_to(v, q_)
                v.scalar_tensor_tensor(r_, q_, float(-NODES), keys, ALU.mult, ALU.add)
                v.drain()
                v.tensor_scalar(t_, r_, 0.0, None, ALU.is_lt)
                v.tensor_scalar(c_, r_, float(NODES), None, ALU.is_ge)
                v.drain()
                v.tensor_tensor(q_, q_, t_, ALU.subtract)
                v.drain()
                v.tensor_tensor(q_, q_, c_, ALU.add)
                v.drain()
                v.tensor_scalar(c_, q_, float(KEY0 - SLOTS // 2), 1.0 / SLOTS, ALU.add, ALU.mult)
                v.drain()
                round_to(v, c_)
                v.tensor_scalar(t_, c_, float(SLOTS * NODES), float(KEY0 * NODES), ALU.mult, ALU.subtract)
                v.tensor_copy(cls_tab[:, bass.ds(i * BIG, BIG)], c_)
                v.drain()
                v.tensor_tensor(t_, keys, t_, ALU.subtract)
                v.drain()
                v.tensor_scalar(keys, t_, 1.0, None, ALU.add)
                for q in range(BIG // BLK):
                    v.wait_ge(oh_used[q % 2], i * (BIG // BLK // 2) + (q // 2 + 1))
                    v.tensor_tensor(oh[:, q % 2, :, :], bc(cw[:, 3, q * BLK:(q + 1) * BLK], P),
                                    mid(iota_b[:, :], BLK), ALU.is_equal)
                    v.drain().then_inc(oh_ok[q % 2], 1)
            v.wait_ge(cnt_ev, 1)
            v.tensor_copy(counts[:, :], bank6[:, 256:384])
            v.drain().then_inc(cnt_ev, 1)
            v.wait_ge(start_mm, 1)
            v.tensor_copy(ecnt[:, 1:2], bank6[:, 0:1])
            v.tensor_copy(countsT[:, :], bank6[:, 384:512])
            v.drain()
            to_blocks(v, rows64[:, :], ecnt[:, 1:2], ROW - 1, 6, 0)
            v.drain()
            v.tensor_copy(ecnt[:, 2:3], rows64[:, :])
            v.drain()
            v.tensor_copy(rows64r[:, :], ecnt[:, 2:3].broadcast_to([P, P]))
            v.drain().then_inc(cnt_ev, 1)
            v.wait_ge(base_mm, 1)
            v.tensor_copy(base[:, :], bank6[:, 256:384])
            v.tensor_copy(ecnt[:, 3:4], bank6[:, 2:3])
            v.reduce_max(junk[0:1, 0:1], bank6[0:1, P:2 * P], axis=X)
            v.drain()
            v.tensor_scalar(junk[0:1, 0:1], junk[0:1, 0:1], 0.5 * (CW - 1), 1.0 / CW, ALU.add, ALU.mult)
            v.drain()
            round_to(v, junk[0:1, 0:1])
            v.tensor_scalar(junk[0:1, 0:1], junk[0:1, 0:1], 1.0, None, ALU.max)
            v.drain()
            v.tensor_copy(ctl[0:1, 1:2], junk[0:1, 0:1])
            v.drain().then_inc(chunk_ok, 1)
            with v.Fori(0, nbig) as i:
                cls = cls_tab[:, bass.ds(i * BIG, BIG)]
                v.tensor_scalar(cw[:, 1, :], cls, 0.0, FAR, ALU.is_lt, ALU.mult)
                v.tensor_copy(cw[:, 0, :], cls)
                v.drain()
                v.tensor_tensor(cw[:, 1, :], cw[:, 1, :], jrow[:, :], ALU.add)
                for j in range(BIG):
                    if j == BIG // 2:
                        v.drain()
                    v.scalar_tensor_tensor(unused[:, j % (BIG // 2), :], iota[:, 0:P], cw[:, 0, j:j + 1], base[:, :],
                                           ALU.is_equal, ALU.mult, accum_out=ranks[:, j:j + 1])
                v.drain()
                v.tensor_tensor(rank_tab[:, bass.ds(i * BIG, BIG)], ranks[:, :], cw[:, 1, :], ALU.add)
                v.tensor_scalar(jrow[:, :], jrow[:, :], float(BIG), None, ALU.add)
                v.drain().then_inc(rank_ok, BIG // BLK)

        def to_blocks(v, out_i, in_f, less_one, shift, least):
            v.tensor_scalar(out_i, in_f, float(less_one), None, ALU.add)
            v.drain()
            v.tensor_scalar(out_i, out_i, shift, None, ALU.logical_shift_right)
            if least:
                v.drain()
                v.tensor_scalar(out_i, out_i, float(least), None, ALU.max)

        PREP_STEPS = 14

        def chunk_rows(v, t):
            if t is None:
                for r in range(CROWS):
                    v.tensor_scalar(rowf[:, r:r + 1], ecnt[:, 3:4], float(r), float(LAST_ROW), ALU.add, ALU.min)
                v.tensor_copy(ecnt[:, 4:5], ecnt[:, 1:2])
                v.drain()
                v.tensor_copy(rowi[:, :], rowf[:, :])
                v.drain().then_inc(rowi_ok, 1)
            else:
                v.tensor_scalar(rowf[:, :], rowf[:, :], float(CROWS), float(LAST_ROW), ALU.add, ALU.min)
                v.tensor_scalar(ecnt[:, 4:5], ecnt[:, 4:5], float(CW), None, ALU.subtract)
                v.drain()
                v.tensor_copy(rowi[:, :], rowf[:, :])
                v.drain().then_inc(rowi_ok, 1)

        def leaky(v, out, z, tmp):
            v.tensor_scalar(tmp, z, 0.2, None, ALU.mult)
            v.drain()
            v.tensor_tensor(out, z, tmp, ALU.max)
            v.drain()

        def graph_start(v):
            v.wait_ge(nn_in, 32)
            v.wait_ge(hsum_in, 16)
            own, last, t4, lcb = n4[:, 0], n4[:, 1], n4[:, 2], n4[:, 3]
            v.tensor_tensor(t4, nn[:, :, AS], nn[:, :, AD], ALU.add)
            v.drain()
            leaky(v, own, t4, lcb)
            v.tensor_tensor(t4, mid(lastr[:, AS], SLOTS), nn[:, :, AD], ALU.add)
            v.drain()
            leaky(v, last, t4, lcb)
            v.tensor_copy(lcb, bc(lastc[:, :], HEADS))
            v.drain()
            v.tensor_scalar(t4, lcb, 0.5, -1.0e30, ALU.is_lt, ALU.mult)
            v.drain()
            v.tensor_tensor(t4, last, t4, ALU.add)
            v.drain()
            v.tensor_tensor(st[:, :, MX], own, t4, ALU.max)
            v.drain()
            v.tensor_tensor(own, own, st[:, :, MX], ALU.subtract)
            v.tensor_tensor(last, last, st[:, :, MX], ALU.subtract)
            v.drain()
            v.tensor_scalar(last, last, 0.0, None, ALU.min)
            v.drain().then_inc(a_req, 1)
            v.wait_ge(a_done, 1)
            v.tensor_tensor(last, last, lcb, ALU.mult)
            v.drain()
            v.tensor_tensor(st[:, :, DN], own, last, ALU.add)
            v.tensor_tensor(heads(n16[:, 0]), heads(nn[:, :, HF]), bc4(own), ALU.mult)
            v.tensor_tensor(heads(n16[:, 1]), heads(mid(lastr[:, HF], SLOTS)), bc4(last), ALU.mult)
            v.drain()
            v.tensor_tensor(st[:, :, NM], n16[:, 0], n16[:, 1], ALU.add)
            v.drain()

        def heads(ap):
            return ap.rearrange("p s (a b) -> p s a b", a=HEADS)

        def bc4(ap):
            return ap.unsqueeze(3).broadcast_to([P, SLOTS, HEADS, EXPERTS])

        def chunk_sort(v, t):
            v.wait_ge(chunk_in, t + 1)
            v.tensor_scalar(ctmp[:, :], iota[:, :], ecnt[:, 4:5], None, ALU.is_lt)
            v.drain()
            v.tensor_tensor(chunk[:, :], chunk[:, :], ctmp[:, :], ALU.mult)
            v.drain()
            for k in range(CW // 8):
                v.max(skey[:, 8 * k:8 * k + 8], chunk[:, :])
                v.drain()
                if k < CW // 8 - 1:
                    v.match_replace(chunk[:, :], skey[:, 8 * k:8 * k + 8], chunk[:, :], -1.0)
                    v.drain()
            v.tensor_scalar(place[:, :], skey[:, :], -1.0 - 0.5 * (NODES - 1), 1.0 / NODES, ALU.add, ALU.mult)
            v.drain()
            round_to(v, place[:, :])
            v.scalar_tensor_tensor(ctmp[:, :], place[:, :], float(-NODES), skey[:, :], ALU.mult, ALU.add)
            v.drain()
            v.tensor_scalar(srci[:, :], ctmp[:, :], -1.0, None, ALU.add)
            v.drain().then_inc(src_ok, 1)
            v.memset(keep[:, 0:1], 0.0)
            v.tensor_tensor(keep[:, 1:CW], place[:, 1:CW], place[:, 0:CW - 1], ALU.is_equal)
            v.drain()
            v.tensor_scalar(ctmp[:, :], keep[:, :], -1.0, 1.0e30, ALU.add, ALU.mult)
            v.drain()

        def chunk_places(v):
            pms = place_m.rearrange("p (s l) -> p s l", l=CW)
            v.tensor_tensor(pms, mid(place[:, :], SLOTS), bc(iota[:, 0:SLOTS], CW), ALU.is_ge)
            v.memset(ends[:, SLOTS:SLOTS + 1], 0.0)
            v.drain()
            v.reduce_sum(ends[:, 0:SLOTS], pms, axis=X)
            v.drain()
            v.tensor_tensor(has[:, :], ends[:, 0:SLOTS], ends[:, 1:SLOTS + 1], ALU.is_gt)
            v.drain()
            v.tensor_scalar(ends[:, 0:SLOTS], ends[:, 0:SLOTS], -1.0, 0.0, ALU.add, ALU.max)
            v.tensor_scalar(ecnt[:, 5:6], ecnt[:, 7:8], float(CW), None, ALU.mult)
            v.tensor_tensor(place_m.rearrange("p (l s) -> p l s", s=SLOTS), bc(place[:, :], SLOTS),
                            mid(iota[:, 0:SLOTS], CW), ALU.is_equal)
            v.drain()
            v.tensor_scalar(ends[:, 0:SLOTS], ends[:, 0:SLOTS], ecnt[:, 5:6], None, ALU.add)
            v.drain()
            v.tensor_copy(endi[:, :], ends[:, 0:SLOTS])
            v.drain().then_inc(endi_ok, 1)

        def chunk_dst(v, h):
            pm = place_m.rearrange("p (l s) -> p l s", s=SLOTS)
            pf = place_f.rearrange("p (l s) -> p l s", s=SLOTS)
            for l in range(0, CW, PSTEP):
                v.tensor_tensor(pf, pm[:, l:l + PSTEP, :], mid(nn[:, :, 4 + h], PSTEP), ALU.mult)
                v.drain()
                v.reduce_sum(adst[:, h, l:l + PSTEP], pf, axis=X)
                v.drain()

        def chunk_scans(v, t):
            v.wait_ge(gath_in, t + 1)
            v.tensor_tensor(adst[:, :, :], adst[:, :, :], gath[:, :, AS].rearrange("p l a -> p a l"), ALU.add)
            v.drain()
            leaky(v, eh[:, :, :], adst[:, :, :], mh[:, :, :])
            for h in range(HEADS):
                v.tensor_tensor_scan(mh[:, h, :], ctmp[:, :], eh[:, h, :], 0.0, ALU.add, ALU.max)
            v.drain()
            v.memset(rh[:, :, 0:1], 0.0)
            v.tensor_tensor(rh[:, :, 1:CW], mh[:, :, 0:CW - 1], mh[:, :, 1:CW], ALU.subtract)
            v.tensor_tensor(wh[:, :, :], eh[:, :, :], mh[:, :, :], ALU.subtract)
            v.drain()
            v.tensor_scalar(rh[:, :, :], rh[:, :, :], 0.0, None, ALU.min)
            v.drain().then_inc(a_req, 1)
            v.wait_ge(a_done, 2 + 2 * t)
            v.tensor_tensor(rh[:, :, :], rh[:, :, :], mid(keep[:, :], HEADS), ALU.mult)
            for h in range(HEADS):
                v.tensor_tensor(xh[:, 4 * h:4 * h + 4, :],
                                gath[:, :, 8 + 4 * h:12 + 4 * h].rearrange("p l a -> p a l"),
                                mid(wh[:, h, :], EXPERTS), ALU.mult)
            v.tensor_copy(scans[:, :, MX], mh[:, :, :].rearrange("p a l -> p l a"))
            v.drain()
            for h in range(HEADS):
                v.tensor_tensor_scan(scans[:, :, 4 + h], rh[:, h, :], wh[:, h, :], 0.0, ALU.mult, ALU.add)
            for f in range(HE):
                v.tensor_tensor_scan(scans[:, :, 8 + f], rh[:, f // 4, :], xh[:, f, :], 0.0, ALU.mult, ALU.add)
            v.drain().then_inc(scan_ok, 1)

        def chunk_merge(v, t):
            v.wait_ge(seg_in, t + 1)
            hb, mc, old, new, dn = n4[:, 0], n4[:, 1], n4[:, 2], n4[:, 3], n4[:, 4]
            v.tensor_copy(hb, bc(has[:, :], HEADS))
            v.drain()
            v.tensor_scalar(mc, hb, -1.0, 1.0e30, ALU.add, ALU.mult)
            v.drain()
            v.tensor_tensor(mc, mc, seg[:, :, MX], ALU.add)
            v.drain()
            v.tensor_tensor(mc, mc, st[:, :, MX], ALU.max)
            v.drain()
            v.tensor_tensor(old, st[:, :, MX], mc, ALU.subtract)
            v.tensor_tensor(new, seg[:, :, MX], mc, ALU.subtract)
            v.drain()
            v.tensor_scalar(new, new, 0.0, None, ALU.min)
            v.tensor_copy(st[:, :, MX], mc)
            v.drain().then_inc(a_req, 1)
            v.wait_ge(a_done, 3 + 2 * t)
            v.tensor_tensor(new, new, hb, ALU.mult)
            v.drain()
            v.tensor_tensor(st[:, :, DN], st[:, :, DN], old, ALU.mult)
            v.tensor_tensor(dn, seg[:, :, DN], new, ALU.mult)
            v.tensor_tensor(heads(n16[:, 0]), heads(st[:, :, NM]), bc4(old), ALU.mult)
            v.tensor_tensor(heads(n16[:, 1]), heads(seg[:, :, NM]), bc4(new), ALU.mult)
            v.drain()
            v.tensor_tensor(st[:, :, DN], st[:, :, DN], dn, ALU.add)
            v.tensor_tensor(st[:, :, NM], n16[:, 0], n16[:, 1], ALU.add)
            v.drain()

        def graph_end(v, n):
            inv, agg, x2 = n4[:, 0], n16[:, 0], n16[:, 1]
            v.tensor_scalar(inv, st[:, :, DN], 1e-16, None, ALU.add)
            v.drain()
            v.reciprocal(inv, inv)
            v.drain()
            v.tensor_tensor(heads(agg), heads(st[:, :, NM]), bc4(inv), ALU.mult)
            v.drain()
            v.tensor_tensor(agg, agg, mid(gamr[:, 0, :], SLOTS), ALU.add)
            v.drain()
            v.reduce_sum(s1[:, :], agg, axis=X)
            v.drain()
            v.tensor_scalar(s1[:, :], s1[:, :], 1.0 / HE, None, ALU.mult)
            v.drain()
            v.tensor_tensor(agg, agg, bc(s1[:, :], HE), ALU.subtract)
            v.drain()
            v.tensor_tensor(x2, agg, agg, ALU.mult)
            v.drain()
            v.reduce_sum(s2[:, :], x2, axis=X)
            v.drain()
            v.tensor_scalar(s2[:, :], s2[:, :], 1.0 / HE, EPS, ALU.mult, ALU.add).then_inc(var_ok, 1)
            v.wait_ge(rt_ok, LAYERS + 4)
            v.reciprocal(s1[:, :], s3[:, :])
            v.drain()
            v.tensor_tensor(agg, agg, bc(s1[:, :], HE), ALU.mult)
            v.drain()
            v.tensor_tensor(agg, agg, mid(gamr[:, 1, :], SLOTS), ALU.mult)
            v.drain()
            v.tensor_tensor(agg, agg, mid(gamr[:, 2, :], SLOTS), ALU.add)
            v.drain()
            sc, ex, sel = n4[:, 0], n4[:, 1], n4[:, 2]
            v.reduce_sum(sc, agg.rearrange("p s (a b) -> p s b a", a=HEADS), axis=X)
            v.drain()
            v.tensor_scalar(sc, sc, 1.0 / HEADS, None, ALU.mult)
            v.drain()
            for e in range(EXPERTS):
                for o in range(EXPERTS):
                    if o != e:
                        v.tensor_tensor(n4[:, 3 + e, :, o], sc[:, :, o], sc[:, :, e],
                                        ALU.is_ge if o < e else ALU.is_gt)
                    else:
                        v.memset(n4[:, 3 + e, :, o], 0.0)
            v.drain()
            for e in range(EXPERTS):
                v.reduce_sum(sel[:, :, e], n4[:, 3 + e], axis=X)
            v.reduce_max(s1[:, :], sc, axis=X)
            v.drain()
            v.tensor_scalar(sel, sel, 1.5, None, ALU.is_lt)
            v.tensor_tensor(ex, sc, bc(s1[:, :], EXPERTS), ALU.subtract)
            v.drain().then_inc(a_req, 1)
            v.wait_ge(a_done, n * 2 + 2)
            v.tensor_tensor(ex, ex, sel, ALU.mult)
            v.drain()
            v.reduce_sum(s1[:, :], ex, axis=X)
            v.drain()
            v.reciprocal(s1[:, :], s1[:, :])
            v.drain()
            v.memset(gtok[:, :, :], 0.0)
            v.tensor_tensor(gates[:, :, :], ex, bc(s1[:, :], EXPERTS), ALU.mult)
            v.drain().then_inc(gate_ok, 1)

        @block.sync
        def _(sp):
            ev = edge_index.rearrange("a (p e) -> p a e", p=P)
            sp.dma_start(raw[:, 1, :], ev[:, 1, :]).then_inc(e_in, 16)
            sp.dma_start(raw[:, 0, :], ev[:, 0, :]).then_inc(e_in, 16)
            sp.dma_start(waver[:, :], c_waver).then_inc(c_in, 16)
            sp.dma_start(wave[:, :], c_wave).then_inc(c_in, 16)
            for i in range(X_PARTS):
                sp.dma_start(xs[:, i * NX:(i + 1) * NX, :],
                             x[i * NX:(i + 1) * NX, 0].rearrange("b r c -> r b c")).then_inc(x_in[i], 16)
            sp.dma_start(eye[:, :], c_eye).then_inc(c_in, 16)
            sp.dma_start(before[:, :], c_before).then_inc(c_in, 16)
            sp.dma_start(pick[:, :], c_pick).then_inc(c_in, 16)
            sp.wait_ge(pool_c, 1)
            lz = edge_list.rearrange("(k p f) a -> k p (f a)", p=P, f=529)
            for k in range(4):
                sp.dma_start(lz[k], zeros[:, :]).then_inc(list_zero, 16)
            pad = NODE_ROWS - NODES
            sp.dma_start(node_tab[NODES:NODE_ROWS, :], zeros[0:pad, 0:NF]).then_inc(nt_st, 16)
            sp.dma_start(last_tab[NODES:NODE_ROWS].rearrange("(a b) -> a b", a=1),
                         zeros[0:1, 0:pad]).then_inc(hsum_st, 16)
            sp.wait_ge(nt_ok, 1)
            store_tokens(sp, node_tab, nt, NF, nt_st)
            sp.wait_ge(nt_st, 16 * 4)
            sp.dma_start(nn[:, :, :], node_tab.rearrange("(p s) f -> p s f", s=SLOTS)).then_inc(nn_in, 16)
            sp.dma_start(lastr[:, :], node_tab[NODES - 1:NODES, :].broadcast_to([P, NF])).then_inc(nn_in, 16)
            sp.wait_ge(hsum_ok, 1)
            sp.dma_start(last_tab[0:NODES].rearrange("(a b) -> a b", b=DLO), hsum[:, :]).then_inc(hsum_st, 16)
            sp.wait_ge(hsum_st, 32)
            sp.dma_start(lastc[:, :], last_tab.rearrange("(p s) -> p s", s=SLOTS)).then_inc(hsum_in, 16)
            sp.wait_ge(chunk_ok, 1)
            n = nc.sync.value_load(ctl[0:1, 1:2], min_val=1, max_val=MAX_CHUNKS)
            with sp.Fori(0, n) as t:
                sp.wait_ge(scan_ok, t + 1)
                sp.dma_start(scan_tab.rearrange("(p l) f -> p l f", l=CW), scans).then_inc(scan_st, 16)
            sp.wait_ge(gate_ok, 1)
            sp.dma_start(gate_tab.rearrange("(p s) f -> p s f", s=SLOTS), gates[:, :, :]).then_inc(gate_st, 16)
            sp.wait_ge(gate_st, 16)
            grow = gate_tab[0:NODES].rearrange("(b t) f -> b t f", t=TOK)
            for half in range(2):
                sp.dma_start(gtok[64 * half:64 * half + 64, 0:32, :],
                             grow[:, 1 + 32 * half:33 + 32 * half, :]).then_inc(gate_in, 16)
            sp.dma_start(gtok[0:64, 32, :], grow[:, 0, :]).then_inc(gate_in, 16)
            sp.wait_ge(done_dve, 1)
            store_tokens(sp, out.rearrange("b t h -> (b t) h"), h0, H, d_out)
            sp.wait_ge(d_out, 16 * 3)

        @block.scalar
        def _(act):
            act.wait_ge(zero_ok, 1)
            for dst, src in weight_dmas:
                act.dma_start(dst, src).then_inc(w_in, 16)
            act.dma_start(b1c[:, :], b1.rearrange("e f -> f e"), allow_slow_non_contiguous=True).then_inc(w_in, 16)
            for i in range(16):
                act.wait_ge(x_rows, i + 1)
                act.activation(y1[:, 4 * i:4 * i + 4, :],
                               wide[0:SIDE, (i % 4) * 512:(i % 4) * 512 + 128].rearrange("p (b m) -> p b m", b=4),
                               ACT.Copy).then_inc(x_rows_out, 1)
            for i in range(4):
                act.wait_ge(x_cols, i + 1)
                act.activation(y2[:, :, 16 * i:16 * i + 16].rearrange("n m b -> n b m"),
                               wide[0:32, i * 512:i * 512 + 512].rearrange("n (b m) -> n b m", m=32),
                               ACT.Copy).then_inc(x_cols_out, 1)
            root(act, 1)
            for r in range(LAYERS + 2):
                evacuate_T(act, r)
                if 1 <= r <= LAYERS:
                    act.wait_ge(y_ok, r)
                    act.activation(sq[:, :, :], xc[:, :, :], ACT.Gelu).then_inc(g_ok, 1)
                    root(act, r + 1)
                if r == LAYERS:
                    root(act, r + 2)
            root(act, LAYERS + 3)
            evacuate_T(act, LAYERS + 2)
            act.wait_ge(list_zero, 64)
            act.wait_ge(nt_st, 64)
            act.wait_ge(hsum_st, 16)
            for k in range(9 * EXPERTS):
                e, t = divmod(k, 9)
                n = 512 if t < 8 else P
                act.wait_ge(hid_mm, k + 1)
                if k >= 2:
                    act.wait_ge(ye_mm, k - 1)
                act.activation(hidT[:, k % 2, 0:n], wide[:, (k % 2) * 512:(k % 2) * 512 + n], ACT.Gelu,
                               bias=b1c[:, e:e + 1]).then_inc(hid_ok, 1)
                if k >= 1:
                    ye_evacuate(act, k - 1)
            ye_evacuate(act, 9 * EXPERTS - 1)
            act.wait_ge(chunk_ok, 1)
            act.wait_ge(a_req, 1)
            act.activation(n4[:, 0:2], n4[:, 0:2], ACT.Exp).then_inc(a_done, 1)
            n = nc.scalar.value_load(ctl[0:1, 1:2], min_val=1, max_val=MAX_CHUNKS)
            with act.Fori(0, n) as t:
                act.wait_ge(a_req, 2 + 2 * t)
                act.activation(rh[:, :, :], rh[:, :, :], ACT.Exp)
                act.activation(wh[:, :, :], wh[:, :, :], ACT.Exp).then_inc(a_done, 1)
                act.wait_ge(a_req, 3 + 2 * t)
                act.activation(n4[:, 2:4], n4[:, 2:4], ACT.Exp).then_inc(a_done, 1)
            act.wait_ge(var_ok, LAYERS + 4)
            act.activation(s3[:, :], s2[:, :], ACT.Sqrt).then_inc(rt_ok, 1)
            act.wait_ge(a_req, 2 + 2 * n)
            act.activation(n4[:, 1], n4[:, 1], ACT.Exp).then_inc(a_done, 1)

        @block.gpsimd
        def _(pool):
            pool.memset(tokw[:, :, :], 0.0)
            pool.memset(win2[:, :, :], 0.0)
            pool.memset(conv[:, :, :], 0.0)
            pool.memset(h0[:, 32, :], 0.0)
            pool.memset(mean64[:, :], 1.0 / H)
            pool.memset(wg2[:, :, :], 0.0)
            pool.drain().then_inc(zero_ok, 1)
            pool.memset(zeros[:, :], 0.0)
            pool.memset(ones_f[:, :], 1.0)
            pool.memset(zero_b[:, :], 0.0)
            pool.iota(iota[:, :], [[1, CW]], base=0, channel_multiplier=0, allow_small_or_imprecise_dtypes=True)
            pool.iota(iota_b[:, :], [[1, P]], base=0, channel_multiplier=0, allow_small_or_imprecise_dtypes=True)
            pool.iota(ecnt[:, 7:8], [[0, 1]], base=0, channel_multiplier=1, allow_small_or_imprecise_dtypes=True)
            pool.drain().then_inc(pool_c, 1)
            pool.wait_ge(list_zero, 64)
            pool.wait_ge(nblk_ok, 1)
            nblk = nc.gpsimd.value_load(ctl[0:1, 0:1], min_val=2, max_val=MAX_BLK)
            pool.wait_ge(rank_ok, 1)
            scatter_block(pool, 0)
            with pool.Fori(1, nblk) as i:
                pool.wait_ge(rank_ok, i + 1)
                scatter_block(pool, i)
            await_then_pass(pool, scat[0], nblk * (8 * BLK))
            await_then_pass(pool, scat[1], nblk * (8 * BLK))
            pool.wait_ge(rowi_ok, 1)
            fetch(pool, [chunk[:, r * ROW:(r + 1) * ROW] for r in range(CROWS)], edge_rows, rowi, chunk_in, 0)
            pool.wait_ge(nt_st, 16 * 4)
            pool.wait_ge(src_ok, 1)
            chunk_pool(pool, 0)
            n = nc.gpsimd.value_load(ctl[0:1, 1:2], min_val=1, max_val=MAX_CHUNKS)
            with pool.If(n > 1):
                with pool.Fori(1, n) as t:
                    pool.dma_reset()
                    pool.sem_clear(fetched)
                    await_then_pass(pool, rowi_ok, t + 1)
                    fetch(pool, [chunk[:, r * ROW:(r + 1) * ROW] for r in range(CROWS)], edge_rows, rowi, chunk_in, 0)
                    await_then_pass(pool, src_ok, t + 1)
                    chunk_pool(pool, t)
                pool.drain()

        @block.tensor
        def _(pe):
            pe.wait_ge(c_in, 16 * 5)
            for i in range(16):
                pe.wait_ge(x_in[i // 4], 16)
                if i >= 4:
                    pe.wait_ge(x_rows_out, i - 3)
                for k in range(4):
                    last = pe.matmul(wide[0:SIDE, (i % 4) * 512 + 32 * k:(i % 4) * 512 + 32 * k + 32],
                                     xs[:, 4 * i + k, :], waver[:, :], start=True, stop=True)
                last.then_inc(x_rows, 1)
            pe.wait_ge(x_rows_out, 16)
            for i in range(4):
                pe.matmul(wide[0:32, i * 512:i * 512 + 512], wave[:, :],
                          y1[:, 16 * i:16 * i + 16, :], start=True, stop=True).then_inc(x_cols, 1)
            pe.wait_ge(x_cols_out, 4)
            pe.wait_ge(tokwd_ok, 1)
            for i in range(4):
                for g in range(4):
                    lhs = y2[:, 8 * g + 2 * i:8 * g + 2 * i + 2, :].rearrange("n q b -> n (q b)")
                    last = pe.matmul(wide[:, i * 512:i * 512 + 512], lhs,
                                     tokwd[:, g, :, :], start=(g == 0), stop=(g == 3))
                last.then_inc(tok_mm, 1)
            prep(pe)
            bounds_pe(pe)
            for r in range(LAYERS + 2):
                pe.wait_ge(u_ok, r + 1)
                transposes(pe, r)
                pe.wait_ge(t_ev, 5 * r + 5)
                if 1 <= r <= LAYERS:
                    if r == 1:
                        pe.wait_ge(prep_ev, PREP_STEPS)
                    mix(pe, r - 1)
                linear(pe, r)
                count_last_pe(pe, r)
                if r == 1:
                    edges_pe(pe)
            r = LAYERS + 2
            pe.wait_ge(u_ok, r + 1)
            transposes(pe, r)
            pe.wait_ge(t_ev, 5 * r + 5)
            for i in range(PAIRS):
                last = (pe.matmul(wide[:, 32 * i:32 * i + 32], uT[:, i, :], wg2[:, :, :], start=True, stop=True)
                        if i < 16 else
                        pe.matmul(wide[:, 512:512 + HE], uT[0:64, 16, :], wg2[0:64, 0, :], start=True, stop=True))
            last.then_inc(y_mm, 1)
            count_last_pe(pe, H_GROUPS - 2)
            count_last_pe(pe, H_GROUPS - 1)
            pe.wait_ge(nt_ok, 1)
            for k in range(9 * EXPERTS + 1):
                if k < 9 * EXPERTS:
                    e, t = divmod(k, 9)
                    if k >= 2:
                        pe.wait_ge(hid_ok, k - 1)
                    lo = 64 * (t % 2) if t < 8 else 0
                    rhs = uT[lo:lo + 64, 4 * (t // 2):4 * (t // 2) + 4, :] if t < 8 else uT[0:64, 16, :]
                    n = 512 if t < 8 else P
                    pe.matmul(wide[:, (k % 2) * 512:(k % 2) * 512 + n], w1[lo:lo + 64, e, :], rhs,
                              start=True, stop=True).then_inc(hid_mm, 1)
                if k >= 1:
                    e, t = divmod(k - 1, 9)
                    b = (k - 1) % 2
                    pe.wait_ge(hid_ok, k)
                    if k >= 3:
                        pe.wait_ge(ye_ev, k - 2)
                    for r4 in range(4 if t < 8 else 1):
                        last = pe.matmul(wide[:, (2 + b) * 512 + H * r4:(2 + b) * 512 + H * r4 + H],
                                         hidT[:, b, P * r4:P * r4 + P], w2[:, e, :], start=True, stop=True)
                    last.then_inc(ye_mm, 1)

        @block.vector
        def _(v):
            dve_prep(v)
            keys_dve(v)
            for k in range(TAKE // 8):
                take_round(v, k)
                for n in range(2 * k, min(2 * k + 2, PREP_STEPS)):
                    kernel_step(v, n)
            bounds_dve(v)
            for i in range(4):
                v.wait_ge(tok_mm, i + 1)
                v.tensor_tensor(h0[:, 8 * i:8 * i + 8, :],
                                wide[:, i * 512:i * 512 + 512].rearrange("p (s h) -> p s h", h=H),
                                mid(tokb[:, :], 8), ALU.add)
            v.drain()
            layer_norm(v, 1, h0[:, :, :], u[:, :, :])
            v.drain().then_inc(u_ok, 1)
            v.wait_ge(list_zero, 64)
            v.wait_ge(nt_st, 16)
            v.wait_ge(hsum_st, 16)
            count_last_dve(v, 0)
            extract_dve(v)
            v.wait_ge(y_mm, 1)
            v.tensor_tensor(u[:, :, :], wtok, mid(binr[:, :], SLOTS), ALU.add)
            v.drain().then_inc(u_ok, 1)
            count_last_dve(v, 1)
            rank_dve(v)
            chunk_rows(v, None)
            for l in range(LAYERS):
                v.wait_ge(y_mm, 2 + l)
                v.tensor_copy(yrow[:, :], bank5[:, 1:33])
                v.tensor_copy(yfar[64:128, :], bank5[0:64, 33:65])
                v.drain()
                v.tensor_tensor(yrow[64:128, :], yrow[64:128, :], yfar[64:128, :], ALU.add)
                v.drain()
                v.tensor_tensor(xc[:, 0:32, :], wtok[:, 0:32, :], bc(yrow[:, :], H), ALU.add)
                v.tensor_copy(xc[:, 32, :], wtok[:, 32, :])
                v.drain().then_inc(y_ok, 1)
                v.wait_ge(g_ok, l + 1)
                v.tensor_tensor(u[:, :, :], u[:, :, :], sq[:, :, :], ALU.add)
                v.drain()
                layer_norm(v, 2 + l, u[:, :, :], u[:, :, :])
                if l == LAYERS - 1:
                    layer_norm(v, 3 + l, u[:, :, :], u[:, :, :])
                v.drain().then_inc(u_ok, 1)
                count_last_dve(v, 2 + l)
            v.wait_ge(y_mm, LAYERS + 2)
            v.tensor_tensor(xc[:, :, :], wtok, mid(boutr[:, :], SLOTS), ALU.add)
            v.drain()
            v.tensor_tensor(h0[:, :, :], h0[:, :, :], xc[:, :, :], ALU.add)
            v.drain()
            layer_norm(v, LAYERS + 3, h0[:, :, :], u[:, :, :])
            v.drain().then_inc(u_ok, 1)
            chunk_sort(v, 0)
            v.wait_ge(y_mm, LAYERS + 3)
            hp = wide[:, 0:SLOTS * HE].rearrange("p (s f) -> p s f", f=HE)
            v.tensor_copy(nt[:, :, HF], hp)
            for a, part in enumerate((AS, AD)):
                v.tensor_tensor(n16[:, a], hp, mid(att[:, a, :], SLOTS), ALU.mult)
                v.drain()
                v.reduce_sum(nt[:, :, part], n16[:, a].rearrange("p s (a b) -> p s a b", a=HEADS), axis=X)
            v.drain().then_inc(nt_ok, 1)
            count_last_dve(v, H_GROUPS - 2)
            chunk_places(v)
            v.wait_ge(nn_in, 32)
            chunk_dst(v, 0)
            count_last_dve(v, H_GROUPS - 1)
            for h in range(1, HEADS):
                chunk_dst(v, h)
            v.wait_ge(h_used, H_GROUPS)
            v.tensor_copy(hsum[:, :], bank7[0:DHI, 0:DLO])
            v.drain().then_inc(hsum_ok, 1)
            graph_start(v)
            for e in range(EXPERTS):
                v.wait_ge(ye_ev, 9 * (e + 1))
                v.tensor_tensor(ye[:, e], ye[:, e], mid(b2r[:, e, :], SLOTS), ALU.add)
            chunk_scans(v, 0)
            chunk_merge(v, 0)
            n = nc.vector.value_load(ctl[0:1, 1:2], min_val=1, max_val=MAX_CHUNKS)
            with v.If(n > 1):
                with v.Fori(1, n) as t:
                    chunk_rows(v, t)
                    chunk_sort(v, t)
                    chunk_places(v)
                    for h in range(HEADS):
                        chunk_dst(v, h)
                    chunk_scans(v, t)
                    chunk_merge(v, t)
                v.drain()
            graph_end(v, n)
            v.wait_ge(gate_in, 16 * 3)
            for e in range(EXPERTS):
                v.tensor_tensor(ye[:, e], ye[:, e], bc(gtok[:, :, e], H), ALU.mult)
                v.drain()
                v.tensor_tensor(h0[:, :, :], h0[:, :, :], ye[:, e], ALU.add)
                v.drain()
            v.drain().then_inc(done_dve, 1)


_INS = {'x': 'x', 'cls_tok': 'cls_tok', 'L0_tok_W': 'tok_W', 'L0_tok_b': 'tok_b', 'L0_attn_Win': 'Win',
        'L0_attn_bin_': 'bin_', 'L0_attn_Wout': 'Wout', 'L0_attn_bout': 'bout', 'L0_attn_A': 'A',
        'L0_attn_Bm': 'Bm', 'L0_attn_Cm': 'Cm', 'L0_attn_Dm': 'Dm', 'L0_ffn_W_gat': 'W_gat',
        'L0_ffn_att_src': 'att_src', 'L0_ffn_att_dst': 'att_dst', 'L0_ffn_b_gat': 'b_gat',
        'L0_ffn_ln_gamma': 'ln_gamma', 'L0_ffn_ln_beta': 'ln_beta', 'L0_ffn_W1': 'W1', 'L0_ffn_b1': 'b1',
        'L0_ffn_W2': 'W2', 'L0_ffn_b2': 'b2', 'L0_ffn_edge_index': 'edge_index'}


def kernel(**inputs):
    import concourse.bacc as bacc
    from concourse.bass_utils import run_bass_kernel_spmd

    nc = bacc.Bacc("TRN2", target_bir_lowering=False, num_devices=1)
    arrays, args = {}, {}
    for name, short in _INS.items():
        arrays[f"in_{short}"] = np.ascontiguousarray(inputs[name])
        args[short] = f"in_{short}"
    for name, a in constants().items():
        arrays[name] = a
        args[name] = name
    args = {k: nc.dram_tensor(n, arrays[n].shape, mybir.dt.from_np(arrays[n].dtype), kind="ExternalInput").ap()
            for k, n in args.items()}
    out = nc.dram_tensor("out_h", (IMAGES, TOK, H), F32, kind="ExternalOutput").ap()
    tower(nc, **args, out=out)
    r = run_bass_kernel_spmd(nc, [arrays], core_ids=[0])
    return r.results[0]["out_h"]
```

```python
from contextlib import ExitStack

import numpy as np
import concourse.bass as bass
from concourse import mybir

F32 = mybir.dt.float32
BF16 = mybir.dt.bfloat16
I32 = mybir.dt.int32
U32 = mybir.dt.uint32
U16 = mybir.dt.uint16
ALU = mybir.AluOpType
ACT = mybir.ActivationFunctionType
X = mybir.AxisListType.X

P = 128
IMAGES, SIDE = 64, 96
TOK, H = 65, 64
NODES = IMAGES * TOK
SLOTS = 33
PAIRS = 17
LAYERS = 4
HEADS, EXPERTS, HE = 4, 4, 16
HID = 128
EDGES = 262144
ECOL = EDGES // P
EPS = 1e-5
NF = 24
NODE_ROWS = P * SLOTS
BLK = 16
BIG = 32
WIDE = 256
UPPER = 13
FIXED = 6
PARTS = 16
TAKE = 24
KEY0 = NODES // 2
DEAD = -4.0e9
LIVE = -1.0e8
ROW = 64
CROWS = 3
CW = CROWS * ROW
GATHER = 4
FEW_ROUNDS = 21
LEAST_COLS = 128
LIST_ROWS = EDGES // ROW + P + 8
LAST_ROW = LIST_ROWS - 1
FAR = 1.0e6
HCOL = 256
DHI, DLO = 65, 64


def wavelet_operator():
    def resize(n):
        s = n / 8.0
        at = (np.arange(8) + 0.5) * s - 0.5
        w = np.maximum(0.0, 1.0 - np.abs(at[:, None] - np.arange(n)[None, :]) / s)
        return w / w.sum(1, keepdims=True)

    def haar(n, sign):
        m = np.zeros((n // 2, n))
        m[np.arange(n // 2), 2 * np.arange(n // 2)] = 0.7071067811865476
        m[np.arange(n // 2), 2 * np.arange(n // 2) + 1] = sign * 0.7071067811865476
        return m

    lo1, hi1, lo2, hi2 = haar(96, 1), haar(96, -1), haar(48, 1), haar(48, -1)
    rows = [resize(24) @ lo2 @ lo1, resize(24) @ hi2 @ lo1, resize(48) @ lo1, resize(48) @ hi1]
    return np.ascontiguousarray(np.concatenate(rows).T.astype(np.float32))


MAPS = [(0, 0), (1, 0), (0, 1), (1, 1), (3, 2), (2, 3), (3, 3)]


def constants():
    eye = np.eye(P, dtype=np.float32)
    before = np.triu(np.ones((P, P), np.float32), 1)
    pick = np.zeros((32, 8), np.float32)
    pick[np.arange(32), np.arange(32) % 8] = 1
    wave = wavelet_operator()
    order = [8 * g + 4 * q + i for g in range(4) for i in range(4) for q in range(2)]
    return {"c_eye": eye, "c_before": before, "c_pick": pick, "c_wave": wave,
            "c_waver": np.ascontiguousarray(wave[:, order])}


def tower(nc, x, cls_tok, tok_W, tok_b, Win, bin_, Wout, bout, A, Bm, Cm, Dm, W_gat, att_src, att_dst,
          b_gat, ln_gamma, ln_beta, W1, b1, W2, b2, edge_index, c_eye, c_before, c_pick, c_wave, c_waver, out):
    with ExitStack() as ctx:
        def sb(name, shape, dt=F32):
            return ctx.enter_context(nc.sbuf_tensor(name, shape, dt))

        def ps(name, shape, dt=F32):
            return ctx.enter_context(nc.psum_tensor(name, shape, dt))

        def sem(name):
            return ctx.enter_context(nc.semaphore(name))

        def rep(ap, n):
            return ap.rearrange("(a f) -> a f", a=1).broadcast_to([n, ap.shape[0]])

        def cut(flat):
            at = [0]

            def take(parts, *shape):
                n = int(np.prod(shape))
                ap = flat[0:parts, at[0]:at[0] + n]
                at[0] += n
                assert at[0] <= flat.shape[1]
                names = "abcd"[:len(shape)]
                if len(shape) == 1:
                    return ap
                return ap.rearrange(f"p ({' '.join(names)}) -> p {' '.join(names)}",
                                    **dict(zip(names[1:], shape[1:])))
            return take

        node_tab = nc.dram_tensor("node_tab", [NODE_ROWS, NF], F32).ap()
        edge_list = nc.dram_tensor("edge_list", [LIST_ROWS * ROW, 1], F32).ap()
        edge_rows = edge_list.rearrange("(r c) a -> r (c a)", c=ROW)
        scan_tab = nc.dram_tensor("scan_tab", [P * CW, NF], F32).ap()
        first_tab = nc.dram_tensor("first_tab", [P * LEAST_COLS, NF], F32).ap()
        last_tab = nc.dram_tensor("last_tab", [NODE_ROWS], F32).ap()
        ye_tab = nc.dram_tensor("ye_tab", [P, EXPERTS, SLOTS, H], F32).ap()
        gate_tab = nc.dram_tensor("gate_tab", [NODE_ROWS, EXPERTS], F32).ap()

        eye = sb("eye", [P, P])
        before = sb("before", [P, P])
        pick = sb("pick", [32, 8])
        wave = sb("wave", [SIDE, 32])
        waver = sb("waver", [SIDE, 32])
        tokb = sb("tokb", [P, H])
        wlin = sb("wlin", [P, 6, P])
        binr = sb("binr", [P, H])
        boutr = sb("boutr", [P, H])
        mean64 = sb("mean64", [H, 1])
        conv = sb("conv", [P, LAYERS, 132])
        spread_room = sb("spread_room", [P, EXPERTS * SLOTS * H + IMAGES * (SIDE + 32) + 2048])
        early = spread_room[:, EXPERTS * SLOTS * H:]
        xs = early[0:SIDE, 0:IMAGES * SIDE].rearrange("p (b c) -> p b c", c=SIDE)
        y1 = early[0:SIDE, IMAGES * SIDE:IMAGES * (SIDE + 32)].rearrange("p (b m) -> p b m", m=32)
        y2 = early[0:32, IMAGES * (SIDE + 32):].rearrange("p (m b) -> p m b", b=IMAGES)
        ye = spread_room[:, 0:EXPERTS * SLOTS * H].rearrange("p (e s h) -> p e s h", e=EXPERTS, s=SLOTS)
        prep_room = cut(ye[:, :, :, :].rearrange("p e s h -> p (e s h)"))
        tokwd = prep_room(32, 4, 8, H)
        win2 = prep_room(P, 6, P)
        a_pow = prep_room(H, 2, LAYERS, H)
        a_powT = prep_room(H, 2, LAYERS, H)
        bm = prep_room(H, LAYERS, 2, H)
        cm = prep_room(H, LAYERS, H)
        vee = prep_room(H, LAYERS, H)
        zeros = prep_room(P, 529)
        tokw = prep_room(32, 4, H)
        h0 = sb("h0", [P, SLOTS, H])
        u = sb("u", [P, SLOTS, H])
        xc = sb("xc", [P, SLOTS, H])
        sq = sb("sq", [P, SLOTS, H])
        s1 = sb("s1", [P, SLOTS])
        s2 = sb("s2", [P, SLOTS])
        s3 = sb("s3", [P, SLOTS])
        uT = sb("uT", [P, PAIRS, P])
        yrow = sb("yrow", [P, 32])
        yfar = sb("yfar", [P, 32])
        late = sb("late", [P, 4 * ECOL])
        raw = late[:, 0:2 * ECOL].bitcast(I32).rearrange("p (a e) -> p a e", a=2)
        srcf = late[:, 2 * ECOL:3 * ECOL]
        etmp = late[:, 3 * ECOL:4 * ECOL]
        gath = late[:, 0:CW * NF].rearrange("p (l f) -> p l f", f=NF)
        scans = gath
        key = sb("key", [P, ECOL + PARTS * TAKE])
        tabs = sb("tabs", [P, 2 * ECOL])
        cls_tab = tabs[:, 0:ECOL]
        lkey_tab = tabs[:, ECOL:]
        rank_tab = cls_tab.bitcast(U32)
        top = sb("top", [P, BIG])
        jrow = sb("jrow", [P, BIG])
        oh = sb("oh", [P, 2, BLK, P], BF16)
        hidT = oh[:, :, :, :].rearrange("p q j c -> p (q j c)").bitcast(F32)[:, 0:1024].rearrange(
            "p (b n) -> p b n", b=2)
        STAGES = 4
        ye_stage = oh[:, :, :, :].rearrange("p q j c -> p (q j c)").bitcast(F32)[:, 1024:2048].rearrange(
            "p (b n) -> p b n", b=STAGES)
        ones_f = sb("ones_f", [P, 1])
        eye_b = sb("eye_b", [P, P], BF16)
        half = 2 * EXPERTS * SLOTS * H
        spread = spread_room[:, 0:half].bitcast(BF16).rearrange("p (a n) -> p a n", a=2)
        spread_h = spread[:, 0, 0:DHI * HCOL].rearrange("p (v j) -> p v j", j=HCOL)
        spread_l = spread[:, 1, 0:DLO * HCOL].rearrange("p (v j) -> p v j", j=HCOL)
        spread_hl = spread[:, :, 0:DLO * HCOL].rearrange("p a (v j) -> p a v j", j=HCOL)
        hcode = sb("hcode", [P, 2, ECOL], BF16)
        rank_room = cut(etmp)
        counts, countsT = rank_room(P, P), rank_room(P, P)
        base = rank_room(P, P)
        nafter = rank_room(P, P)
        rows64r, before64 = rank_room(P, P), rank_room(P, P)
        cw, ranks = rank_room(P, 2, WIDE), rank_room(P, BIG)
        late_room = cut(late[:, CW * NF:])
        adst, eh, mh, rh = (late_room(P, HEADS, CW) for _ in range(4))
        tabs_room = cut(tabs[:, :])
        xh, wh = tabs_room(P, HE, CW), tabs_room(P, HEADS, CW)
        place_m = tabs[:, 0:SLOTS * CW // 2].bitcast(BF16).rearrange("p (s l) -> p s l", l=CW)
        place_b = tabs[:, SLOTS * CW // 2:(SLOTS + 1) * CW // 2].bitcast(BF16)
        unused = early[:, DLO * HCOL // 2:].bitcast(BF16).rearrange("p (a b) -> p a b", b=P)
        key_room = cut(key[:, :])
        chunk, skey, place, keep, ctmp = (key_room(P, CW) for _ in range(5))
        seg = key_room(P, SLOTS, NF)
        xc_room = cut(xc[:, :, :].rearrange("p s h -> p (s h)"))
        nn, st = xc_room(P, SLOTS, NF), xc_room(P, SLOTS, NF)
        sq_room = cut(sq[:, :, :].rearrange("p s h -> p (s h)"))
        n16, nt = sq_room(P, 2, SLOTS, HE), sq_room(P, SLOTS, NF)
        code_a = xc[:, :, :].rearrange("p s h -> p (s h)")[:, 0:ECOL]
        code_b = sq[:, :, :].rearrange("p s h -> p (s h)")[:, 0:ECOL]
        u_room = cut(u[:, :, :].rearrange("p s h -> p (s h)"))
        n4, gates, gtok = u_room(P, 8, SLOTS, HEADS), u_room(P, SLOTS, EXPERTS), u_room(P, SLOTS, EXPERTS)
        lastc = u_room(P, SLOTS)
        iota = sb("iota", [P, CW])
        iota_b = sb("iota_b", [P, P], BF16)
        zero_b = sb("zero_b", [P, P], BF16)
        junk = sb("junk", [P, P])
        ecnt = sb("ecnt", [P, 8])
        ctl = sb("ctl", [1, 8], I32)
        rows64 = sb("rows64", [P, 1], I32)
        ring_i = sb("ring_i", [P, 2, BLK // 2], U32)
        ring_k = sb("ring_k", [P, 2, BLK // 2])
        wg2 = sb("wg2", [P, 2, NF])
        att = sb("att", [P, 2, HE])
        lastr = sb("lastr", [P, NF])
        hsum = sb("hsum", [DHI, DLO])
        rowi = sb("rowi", [P, CROWS], U32)
        rowf = sb("rowf", [P, CROWS])
        srci = sb("srci", [P, CW], U32)
        ends = sb("ends", [P, SLOTS + 1])
        upper = sb("upper", [P, SLOTS - UPPER])
        upperi = sb("upperi", [P, SLOTS - UPPER], U32)
        endi = sb("endi", [P, SLOTS], U32)
        has = sb("has", [P, SLOTS])
        gamr = sb("gamr", [P, 3, HE])
        w1 = sb("w1", [P, EXPERTS, HID])
        w2 = sb("w2", [HID, EXPERTS, H])
        b1c = sb("b1c", [HID, EXPERTS])
        b2r = sb("b2r", [P, EXPERTS, H])

        wide = ps("wide", [P, 5 * 512])
        bank4 = wide[:, 2048:2560]
        bank5 = ps("bank5", [P, 512])
        node_dst = bank5[:, 256:256 + SLOTS * HEADS].rearrange("p (s a) -> p s a", a=HEADS)
        bank6 = ps("bank6", [P, 512])
        bank7 = ps("bank7", [P, 512])
        wtok = wide[:, 0:SLOTS * H].rearrange("p (s h) -> p s h", h=H)

        c_in = sem("const_loaded")
        w_in = sem("weights_loaded")
        x_in = [sem(f"x_loaded{i}") for i in range(4)]
        zero_ok = sem("weight_tiles_zeroed")
        tokwd_ok = sem("token_weights_spread")
        x_rows = sem("rows_mapped")
        x_rows_out = sem("rows_evacuated")
        x_cols = sem("columns_mapped")
        x_cols_out = sem("columns_evacuated")
        tok_mm = sem("tokens_multiplied")
        prep_mm = sem("prep_products")
        prep_ev = sem("prep_evacuated")
        u_ok = sem("normed_ready")
        t_mm = sem("transposed")
        t_ev = sem("transposed_evacuated")
        y_mm = sem("mixed")
        mix_ok = sem("state_terms_ready")
        y_ok = sem("mixed_summed")
        g_ok = sem("gelu_done")
        xc_ok = sem("centred_ready")
        sq_ok = sem("squares_ready")
        var_ok = sem("variance_ready")
        rt_ok = sem("root_ready")
        d_out = sem("output_stored")
        e_in = [sem("sources_loaded"), sem("destinations_loaded")]
        pool_passed = sem("pool_passed_a_wait")
        sp_passed = sem("sp_passed_a_wait")
        pool_c = sem("pool_constants_ready")
        nblk_ok = sem("block_count_ready")
        ctl_mm = sem("counts_transposed")
        oh_ok = [sem("classes_spread0"), sem("classes_spread1")]
        oh_used = [sem("classes_counted0"), sem("classes_counted1")]
        cnt_ev = sem("counts_read")
        start_mm = sem("list_starts_ready")
        base_mm = sem("list_places_ready")
        rank_ok = sem("ranks_ready")
        chunk_ok = sem("chunk_count_ready")
        ring_in = [sem("edges_to_scatter0"), sem("edges_to_scatter1")]
        scat = [sem("scattered0"), sem("scattered1")]
        list_zero = sem("list_zeroed")
        h_ok = sem("last_spread")
        h_used = sem("last_counted")
        hsum_ok = sem("last_count_ready")
        hsum_st = sem("last_count_stored")
        hsum_in = sem("last_count_loaded")
        codes_ok = sem("last_codes_ready")
        nt_ok = sem("node_rows_ready")
        nt_st = sem("node_rows_stored")
        nn_in = sem("node_rows_loaded")
        rowi_ok = sem("chunk_rows_known")
        chunk_in = sem("chunk_loaded")
        fetched = sem("rows_fetched")
        src_ok = sem("chunk_sources_known")
        first_in = sem("first_source_rows_gathered")
        gath_in = sem("source_rows_gathered")
        a_req = sem("exponents_ready")
        a_done = sem("exponentials_done")
        scan_ok = sem("scans_ready")
        scan_st = sem("scans_stored")
        endi_ok = sem("segment_ends_known")
        upper_ok = sem("upper_ends_known")
        upper_mm = sem("upper_counts_transposed")
        upper_known = sem("upper_places_checked")
        first_st = sem("first_scans_stored")
        seg_in = sem("segment_ends_gathered")
        hid_mm = sem("hidden_multiplied")
        hid_ok = sem("hidden_activated")
        ye_mm = sem("expert_multiplied")
        ye_ev = sem("expert_evacuated")
        ye_st = sem("expert_stored")
        ye_in = [sem("first_experts_loaded"), sem("last_expert_loaded")]
        bias_ok = sem("experts_biased")
        prod_ok = sem("last_experts_multiplied")
        slots_ok = sem("last_slots_summed")
        gate_ok = sem("gates_ready")
        gate_st = sem("gates_stored")
        gate_in = sem("gates_loaded")
        done_dve = sem("result_ready")

        block = ctx.enter_context(nc.Block())

        def bc(ap2, n):
            return ap2.unsqueeze(2).broadcast_to([ap2.shape[0], ap2.shape[1], n])

        def mid(ap2, n):
            return ap2.unsqueeze(1).broadcast_to([ap2.shape[0], n, ap2.shape[1]])

        X_PARTS = 4
        NX = IMAGES // X_PARTS
        MAX_BLK = ECOL // BLK
        MAX_CHUNKS = EDGES // CW + 1
        V_SLOTS = 24
        OWN = 3
        HALVES = [slice(0, 16), slice(16, SLOTS)]
        EIGHTS = [slice(k, min(k + 8, SLOTS)) for k in range(0, SLOTS, 8)]
        MAGIC = 12582912.0
        H_GROUPS = ECOL // HCOL
        PREP_STEPS = 14
        ACT_LOADS = 20
        EARLY = 1
        TILES = [3, 5, 5, 5, 6, 5, 3]
        MX, DN, NM = slice(0, 4), slice(4, 8), slice(8, 24)

        def store_tokens(eng, table, tile, width, s, slots=slice(0, SLOTS)):
            rows = table[0:NODES].rearrange("(b t) h -> b t h", t=TOK)
            lo, hi = slots.start, min(slots.stop, 32)
            for half in range(2):
                eng.dma_start(rows[:, 1 + 32 * half + lo:1 + 32 * half + hi, :],
                              tile[64 * half:64 * half + 64, lo:hi, 0:width]).then_inc(s, 16)
            if slots.stop == SLOTS:
                eng.dma_start(rows[:, 0, :], tile[0:64, 32, 0:width]).then_inc(s, 16)

        AS, AD, HF = slice(0, 4), slice(4, 8), slice(8, 24)
        weight_dmas = []
        for m, (g, gc) in enumerate(MAPS):
            weight_dmas.append((tokw[gc * 8:gc * 8 + 8, g, :], rep(tok_W[m], 8)))
        for i, w in enumerate([Win] + [Dm[l] for l in range(LAYERS)] + [Wout]):
            for q in range(2):
                weight_dmas.append((win2[64 * q:64 * q + 64, i, 64 * q:64 * q + 64], w))
        weight_dmas += [
            (tokb[:, :], rep(tok_b, P)), (binr[:, :], rep(bin_, P)), (boutr[:, :], rep(bout, P)),
            (a_pow[:, 0, :, :], A.rearrange("l n m -> n l m")),
            (bm[:, :, 0, :], Bm.rearrange("l n h -> n l h")),
            (cm[:, :, :], Cm.rearrange("l a n -> a l n")),
            (h0[0:64, 32, :], cls_tok[0, 0:1, :].broadcast_to([64, H])),
            (wg2[0:64, 0, HF], W_gat), (wg2[64:128, 1, HF], W_gat),
            (att[:, 0, :], rep(att_src.rearrange("a b -> (a b)"), P)),
            (att[:, 1, :], rep(att_dst.rearrange("a b -> (a b)"), P)),
            (gamr[:, 0, :], rep(b_gat, P)), (gamr[:, 1, :], rep(ln_gamma, P)), (gamr[:, 2, :], rep(ln_beta, P)),
            (w1[0:64, :, :], W1.rearrange("e h f -> h e f")), (w1[64:128, :, :], W1.rearrange("e h f -> h e f")),
            (w2[:, :, :], W2.rearrange("e f h -> f e h")),
            (b2r[:, :, :].rearrange("p e h -> p (e h)"), rep(b2.rearrange("e h -> (e h)"), P)),
        ]

        def count_last_dve(v, g, part, parts=2):
            if g == 0 and part == 0:
                v.wait_ge(prep_ev, PREP_STEPS)
                v.wait_ge(list_zero, 64)
                v.wait_ge(nt_st, 16)
                v.wait_ge(hsum_st, 16)
            elif part == 0:
                v.wait_ge(h_used, g)
            cols = slice(g * HCOL, (g + 1) * HCOL)
            for d in range(DLO * part // parts, DLO * (part + 1) // parts):
                v.tensor_scalar(spread_hl[:, :, d, :], hcode[:, :, cols], float(d), None, ALU.is_equal)
            if part == parts - 1:
                v.tensor_scalar(spread_h[:, DLO, :], hcode[:, 0, cols], float(DLO), None, ALU.is_equal)
                v.drain().then_inc(h_ok, 1)

        def count_last_pe(pe, g):
            pe.wait_ge(h_ok, g + 1)
            for j in range(HCOL):
                m = pe.matmul(bank7[0:DHI, 0:DLO], spread_h[:, :, j], spread_l[:, :, j],
                              start=(g == 0 and j == 0), stop=(g == H_GROUPS - 1 and j == HCOL - 1),
                              skip_group_check=True)
            m.then_inc(h_used, 1)

        def expert_tile(pe, k):
            if k < 9 * EXPERTS:
                e, t = divmod(k, 9)
                if k >= 2:
                    pe.wait_ge(hid_ok, k - 1)
                lo = 64 * (t % 2) if t < 8 else 0
                rhs = uT[lo:lo + 64, 4 * (t // 2):4 * (t // 2) + 4, :] if t < 8 else uT[0:64, 16, :]
                n = 512 if t < 8 else P
                pe.matmul(wide[:, (k % 2) * 512:(k % 2) * 512 + n], w1[lo:lo + 64, e, :], rhs,
                          start=True, stop=True).then_inc(hid_mm, 1)
            if k >= 1:
                e, t = divmod(k - 1, 9)
                b = (k - 1) % 2
                pe.wait_ge(hid_ok, k)
                if k >= 3:
                    pe.wait_ge(ye_ev, k - 2)
                for r4 in range(4 if t < 8 else 1):
                    last = pe.matmul(wide[:, (2 + b) * 512 + H * r4:(2 + b) * 512 + H * r4 + H],
                                     hidT[:, b, P * r4:P * r4 + P], w2[:, e, :], start=True, stop=True)
                last.then_inc(ye_mm, 1)

        def evacuate_T(act, r):
            for k in range(5):
                act.wait_ge(t_mm, 5 * r + k + 1)
                if k < 4:
                    act.activation(uT[:, 4 * k:4 * k + 4, :],
                                   wide[:, 512 * k:512 * k + 512].rearrange("p (s f) -> p s f", f=P),
                                   ACT.Copy).then_inc(t_ev, 1)
                else:
                    act.activation(uT[0:64, 16, :], wide[0:64, 2048:2048 + P], ACT.Copy).then_inc(t_ev, 1)

        def ye_slots(table, k):
            e, t = divmod(k, 9)
            if t == 8:
                return table[:, e, 32:33, :]
            q, s2 = t // 2, t % 2
            return table[:, e, 8 * q:8 * q + 8, :].rearrange("p (r s) h -> p s r h", s=2)[:, s2]

        def ye_evacuate(act, k):
            n = 4 if k % 9 < 8 else 1
            act.wait_ge(ye_mm, k + 1)
            if k >= STAGES:
                act.wait_ge(ye_st, 16 * (k - STAGES + 1))
            act.activation(ye_stage[:, k % STAGES, 0:n * H], wide[:, (2 + k % 2) * 512:(2 + k % 2) * 512 + n * H],
                           ACT.Copy).then_inc(ye_ev, 1)

        def exp_edges(act, lo, hi):
            act.activation(rh[:, :, lo:hi], rh[:, :, lo:hi], ACT.Exp)
            act.activation(wh[:, :, lo:hi], wh[:, :, lo:hi], ACT.Exp).then_inc(a_done, 1)

        def expert_act(act, k):
            if k < 9 * EXPERTS:
                e, t = divmod(k, 9)
                n = 512 if t < 8 else P
                act.wait_ge(hid_mm, k + 1)
                if k >= 2:
                    act.wait_ge(ye_mm, k - 1)
                act.activation(hidT[:, k % 2, 0:n], wide[:, (k % 2) * 512:(k % 2) * 512 + n], ACT.Gelu,
                               bias=b1c[:, e:e + 1]).then_inc(hid_ok, 1)
            if k >= 1:
                ye_evacuate(act, k - 1)

        def expert_store(sp, k):
            n = 4 if k % 9 < 8 else 1
            sp.wait_ge(ye_ev, k + 1)
            if k >= 1:
                sp.wait_ge(ye_st, 16 * k)
            sp.dma_start(ye_slots(ye_tab, k), ye_stage[:, k % STAGES, 0:n * H].rearrange(
                "p (r h) -> p r h", h=H)).then_inc(ye_st, 16)

        def root(act, n):
            for k, a in enumerate(HALVES):
                act.wait_ge(xc_ok, 2 * n - 1 + k)
                act.activation(sq[:, a, :], xc[:, a, :], ACT.Square).then_inc(sq_ok, 1)
            act.wait_ge(var_ok, n)
            act.activation(s3[:, :], s2[:, :], ACT.Sqrt).then_inc(rt_ok, 1)

        def transposes(pe, r):
            for k in range(5):
                pe.wait_ge(u_ok, 5 * r + k + 1)
                for i in range(4 * k, min(4 * k + 4, PAIRS)):
                    last = (pe.transpose(wide[:, 128 * i:128 * i + 128], u[:, 2 * i:2 * i + 2, :], eye[:, :])
                            if i < 16 else
                            pe.transpose(wide[0:64, 2048:2048 + P], u[:, 32, :], eye[:, :]))
                last.then_inc(t_mm, 1)

        def mix(pe, l, i):
            if i < 16:
                return pe.matmul(bank5[:, 0:65], uT[:, i, :], conv[:, l, 63 - 2 * i:128 - 2 * i],
                          start=(i == 0), stop=False, skip_group_check=True)
            return pe.matmul(bank5[0:64, 0:65], uT[0:64, 16, 0:64], conv[0:64, l, 64:129],
                          start=False, stop=True, skip_group_check=True)

        def linear(pe, w, i):
            if i < 16:
                return pe.matmul(wide[:, 128 * i:128 * i + 128], uT[:, i, :], wlin[:, w, :], start=True, stop=True)
            return pe.matmul(wide[:, 2048:2048 + H], uT[0:64, 16, :], wlin[0:64, w, 0:64], start=True, stop=True)

        def bounds_pe(pe):
            pe.wait_ge(ctl_mm, 1)
            pe.transpose(bank6[0:1, 0:P], ecnt[:, 0:1], eye[:, :])
            pe.transpose(bank6[0:1, P:2 * P], ecnt[:, 6:7], eye[:, :]).then_inc(ctl_mm, 1)

        def edges_pe(pe):
            pe.wait_ge(nblk_ok, 1)
            nbig = nc.tensor.value_load(ctl[0:1, 2:3], min_val=1, max_val=ECOL // BIG)
            m = pe.matmul(bank6[:, 256:384], eye_b[:, :], zero_b[:, :], start=True, stop=False,
                          skip_group_check=True)
            m.then_inc(oh_used[0], 1)
            m = pe.matmul(bank6[:, 256:384], eye_b[:, :], zero_b[:, :], start=False, stop=False,
                          skip_group_check=True)
            m.then_inc(oh_used[1], 1)
            with pe.Fori(0, nbig) as i:
                for q in range(BIG // BLK):
                    pe.wait_ge(oh_ok[q % 2], i * (BIG // BLK // 2) + (q // 2 + 1))
                    for j in range(BLK):
                        m = pe.matmul(bank6[:, 256:384], eye_b[:, :], oh[:, q % 2, j, :], start=False, stop=False,
                                      skip_group_check=True)
                    m.then_inc(oh_used[q % 2], 1)
            pe.matmul(bank6[:, 256:384], eye_b[:, :], zero_b[:, :], start=False, stop=True,
                      skip_group_check=True).then_inc(cnt_ev, 1)
            pe.wait_ge(cnt_ev, 2)
            pe.matmul(bank6[:, 0:1], counts[:, :], ones_f[:, :], start=True, stop=True)
            pe.transpose(bank6[:, 384:512], counts[:, :], eye[:, :]).then_inc(start_mm, 1)
            pe.wait_ge(cnt_ev, 3)
            pe.transpose(bank6[0:1, 128:256], ecnt[:, 1:2], eye[:, :])
            pe.matmul(bank6[:, 2:3], before[:, :], ecnt[:, 2:3], start=True, stop=True)
            pe.matmul(bank6[:, 256:384], rows64r[:, :], before64[:, :], start=True, stop=False)
            pe.matmul(bank6[:, 256:384], before[:, :], counts[:, :], start=False, stop=False)
            pe.matmul(bank6[:, 256:384], countsT[:, :], nafter[:, :], start=False, stop=True).then_inc(base_mm, 1)

        def prep_weights(pe):
            pe.wait_ge(w_in, 16 * (len(weight_dmas) + 1))
            for i in range(6):
                b = [bank5, bank4, bank7][i % 3]
                if i >= 3:
                    pe.wait_ge(prep_ev, i - 2)
                pe.transpose(b[:, 0:P], win2[:, i, :], eye[:, :]).then_inc(prep_mm, 1)
            pe.wait_ge(prep_ev, 6)
            for l in range(LAYERS):
                pe.transpose(bank5[0:64, 64 * l:64 * l + 64], a_pow[:, 0, l, :], eye[0:64, 0:64])
                last = pe.matmul(bank4[0:64, l:l + 1], cm[:, l, :], mean64[:, :], start=True, stop=True)
            last.then_inc(prep_mm, 1)

        def prep_powers(pe):
            n = 7
            for d in range(6):
                pe.wait_ge(prep_ev, n)
                c, w = d % 2, 1 << d
                for l in range(LAYERS):
                    last = pe.matmul(bank4[0:64, 64 * l:64 * l + w], a_pow[:, c, l, :], vee[:, l, 0:w],
                                     start=True, stop=True)
                    if d < 5:
                        pe.matmul(bank5[0:64, 64 * l:64 * l + 64], a_powT[:, c, l, :], a_pow[:, c, l, :],
                                  start=True, stop=True)
                        last = pe.matmul(bank7[0:64, 64 * l:64 * l + 64], a_pow[:, c, l, :], a_powT[:, c, l, :],
                                         start=True, stop=True)
                last.then_inc(prep_mm, 1)
                n += 1
            pe.wait_ge(prep_ev, n)
            for l in range(LAYERS):
                last = pe.matmul(bank5[:, 64 * l:64 * l + 64], bm[:, l, :, :], vee[:, l, :], start=True, stop=True)
            last.then_inc(prep_mm, 1)
            pe.wait_ge(prep_ev, n + 1)

        def spread_weights(pool):
            pool.wait_ge(c_in, 16 * 5)
            pool.wait_ge(w_in, 16 * (len(weight_dmas) + 1))
            for g in range(4):
                pool.tensor_tensor(tokwd[:, g, :, :], mid(tokw[:, g, :], 8), bc(pick[:, :], H), ALU.mult)
            pool.tensor_copy(bm[:, :, 1, :], bm[:, :, 0, :])
            pool.drain().then_inc(tokwd_ok, 1)

        def kernel_step(act, n):
            act.wait_ge(prep_mm, n + 1)
            if n < 6:
                act.activation(wlin[:, n, :], [bank5, bank4, bank7][n % 3][:, 0:P], ACT.Copy)
            elif n == 6:
                act.activation(a_powT[:, 0, :, :], by_layer(bank5), ACT.Copy)
                act.activation(vee[:, :, 0:1], bank4[0:64, 0:LAYERS].unsqueeze(2), ACT.Copy)
            elif n < 13:
                d = n - 7
                c, w = 1 - d % 2, 1 << d
                if d < 5:
                    act.activation(a_pow[:, c, :, :], by_layer(bank5), ACT.Copy)
                    act.activation(a_powT[:, c, :, :], by_layer(bank7), ACT.Copy)
                act.activation(vee[:, :, w:2 * w], by_layer(bank4)[:, :, 0:w], ACT.Copy)
            else:
                w = bank5[:, 0:256].rearrange("p (l m) -> p l m", l=LAYERS)
                act.activation(conv[0:64, :, 65:129], w[0:64], ACT.Copy)
                act.activation(conv[64:128, :, 66:130], w[64:128], ACT.Copy)
            act.drain().then_inc(prep_ev, 1)

        def by_layer(bank):
            return bank[0:64, 0:256].rearrange("p (l m) -> p l m", l=LAYERS)

        def layer_norm(v, n, src, dst, signal=True):
            v.reduce_sum(s1[:, :], src, axis=X)
            v.drain()
            for a in HALVES:
                v.scalar_tensor_tensor(xc[:, a, :], bc(s1[:, a], H), -1.0 / H, src[:, a, :], ALU.mult,
                                       ALU.add).then_inc(xc_ok, 1)
            for k, a in enumerate(HALVES):
                v.wait_ge(sq_ok, 2 * n - 1 + k)
                v.reduce_sum(s2[:, a], sq[:, a, :], axis=X)
            v.drain()
            v.tensor_scalar(s2[:, :], s2[:, :], 1.0 / H, EPS, ALU.mult, ALU.add).then_inc(var_ok, 1)
            v.wait_ge(rt_ok, n)
            v.reciprocal(s1[:, :], s3[:, :])
            v.drain()
            for a in EIGHTS:
                m = v.tensor_tensor(dst[:, a, :], xc[:, a, :], bc(s1[:, a], H), ALU.mult)
                if signal:
                    m.then_inc(u_ok, 1)
            v.drain()

        def fetch(pool, tiles, table, index, signal, before):
            for k, tile in enumerate(tiles):
                pool.indirect_dma_start(tile, None, table, bass.IndirectOffsetOnAxis(ap=index[:, k:k + 1], axis=0))\
                    .then_inc(fetched, 16)
            pool.wait_ge(fetched, 16 * (before + len(tiles)))
            pool.sem_inc(signal, 1)

        def gather_column(pool, l, signal):
            pool.indirect_dma_start(gath[:, l, :], None, node_tab,
                                    bass.IndirectOffsetOnAxis(ap=srci[:, l:l + 1], axis=0)).then_inc(signal, 16)

        def chunk_pool(pool, t, first=False):
            if first:
                groups = nc.gpsimd.value_load(ctl[0:1, 4:5], min_val=0, max_val=(CW - LEAST_COLS) // GATHER)
                for c in range(0, LEAST_COLS):
                    if c == CW // 2:
                        pool.wait_ge(src_ok, 2)
                    gather_column(pool, c, first_in)
                for c in range(LEAST_COLS, CW, GATHER):
                    with pool.If(groups > (c - LEAST_COLS) // GATHER):
                        for l in range(c, c + GATHER):
                            gather_column(pool, l, fetched)
                await_then_pass(pool, fetched, 16 * CROWS + 16 * GATHER * groups, pool_passed)
                pool.sem_inc(gath_in, 1)
            else:
                fetch(pool, [gath[:, l, :] for l in range(CW)], node_tab, srci, gath_in, CROWS)
            if first:
                pool.wait_ge(upper_known, 1)
                upper_in = nc.gpsimd.value_load(ctl[0:1, 6:7], min_val=0, max_val=1)
                with pool.If(upper_in == 1):
                    pool.wait_ge(first_st, 16)
                    pool.drain()
                    for k in range(UPPER, SLOTS):
                        gather_end(pool, k, first_tab, upperi[:, k - UPPER:k - UPPER + 1])
                pool.wait_ge(scan_st, 32)
                pool.wait_ge(endi_ok, 1)
                for k in range(0, UPPER):
                    gather_end(pool, k, scan_tab, endi[:, k:k + 1])
                with pool.If(upper_in == 0):
                    for k in range(UPPER, SLOTS):
                        gather_end(pool, k, scan_tab, endi[:, k:k + 1])
                await_then_pass(pool, fetched, 16 * GATHER * groups + 16 * (CROWS + SLOTS), pool_passed)
                pool.sem_inc(seg_in, 1)
            else:
                await_then_pass(pool, scan_st, t * 16 + 32, pool_passed)
                await_then_pass(pool, endi_ok, t + 1, pool_passed)
                fetch(pool, [seg[:, k, :] for k in range(SLOTS)], scan_tab, endi, seg_in, CROWS + CW)

        def gather_end(pool, k, table, index):
            pool.indirect_dma_start(seg[:, k, :], None, table, bass.IndirectOffsetOnAxis(ap=index, axis=0))\
                .then_inc(fetched, 16)

        def await_then_pass(eng, s, value, passed):
            eng.wait_ge(s, value)
            eng.sem_inc(passed, 1)

        def ring_fill(sp, i):
            await_then_pass(sp, rank_ok, i + 1, sp_passed)
            for h in range(2):
                c = i * BLK + h * (BLK // 2)
                await_then_pass(sp, scat[h], i * (8 * BLK), sp_passed)
                sp.dma_start(ring_i[:, h, :], rank_tab[:, bass.ds(c, BLK // 2)]).then_inc(ring_in[h], 16)
                sp.dma_start(ring_k[:, h, :], lkey_tab[:, bass.ds(c, BLK // 2)]).then_inc(ring_in[h], 16)

        def scatter_column(pool, h, places, keys):
            pool.indirect_dma_start(edge_list, bass.IndirectOffsetOnAxis(ap=places, axis=0), keys, None,
                                    bounds_check=LIST_ROWS * ROW - 1, oob_is_err=False).then_inc(scat[h], 16)

        def scatter_block(pool, i):
            for h in range(2):
                await_then_pass(pool, ring_in[h], i * 32, pool_passed)
                for j in range(BLK // 2):
                    scatter_column(pool, h, ring_i[:, h, j:j + 1], ring_k[:, h, j:j + 1])

        def round_to(v, ap):
            v.tensor_scalar(ap, ap, MAGIC, MAGIC, ALU.add, ALU.subtract)
            v.drain()

        def keys_dve(v):
            keys = key[:, 0:ECOL]
            v.wait_ge(e_in[0], 16)
            v.wait_ge(e_in[1], 16)
            v.tensor_scalar(keys, raw[:, 1, :], float(NODES), float(NODES), ALU.min, ALU.mult)
            v.tensor_scalar(etmp, raw[:, 0, :], float(NODES - 1), DEAD, ALU.is_ge, ALU.mult)
            v.drain()
            v.scalar_tensor_tensor(srcf, raw[:, 0, :], float(NODES - 1), etmp, ALU.min, ALU.add)
            v.drain()
            v.scalar_tensor_tensor(keys, keys, float(-KEY0 * NODES), srcf, ALU.add, ALU.add)
            v.drain()
            v.tensor_scalar(etmp, keys, float(KEY0 * NODES), DEAD, ALU.is_ge, ALU.mult)
            v.drain()
            v.tensor_tensor(keys, keys, etmp, ALU.add)
            v.memset(lkey_tab, 4 * DEAD)
            v.drain()
            v.tensor_scalar(srcf, keys, LIVE, 0.0, ALU.is_ge, ALU.add, accum_out=ecnt[:, 0:1])

        def rank_constants(v):
            v.wait_ge(c_in, 16 * 5)
            v.wait_ge(pool_c, 1)
            v.tensor_copy(eye_b[:, :], eye[:, :])
            v.tensor_scalar(before64[:, :], before[:, :], float(ROW), None, ALU.mult)
            v.tensor_tensor(nafter[:, :], before[:, :], eye[:, :], ALU.add)
            v.tensor_copy(jrow[:, :], iota[:, 0:BIG])
            v.drain()
            v.tensor_scalar(nafter[:, :], nafter[:, :], -1.0, None, ALU.add)
            v.drain()

        def last_codes(pool):
            pool.wait_ge(e_in[0], 16)
            pool.wait_ge(e_in[1], 16)
            pool.tensor_scalar(code_a, raw[:, 1, :], 2.0 * NODES, 0.5 * (DLO - 1), ALU.min, ALU.subtract)
            pool.drain()
            pool.tensor_scalar(code_b, code_a, 1.0 / DLO, MAGIC, ALU.mult, ALU.add)
            pool.drain()
            pool.tensor_scalar(code_b, code_b, MAGIC, None, ALU.subtract)
            pool.drain()
            pool.tensor_copy(hcode[:, 0, :], code_b)
            pool.tensor_scalar(code_b, code_b, float(DLO), None, ALU.mult)
            pool.drain()
            pool.tensor_tensor(code_a, code_a, code_b, ALU.subtract)
            pool.drain()
            pool.tensor_scalar(hcode[:, 1, :], code_a, 0.5 * (DLO - 1), None, ALU.add)
            pool.drain()
            pool.tensor_scalar(code_a, raw[:, 0, :], float(NODES - 1), 1024.0, ALU.is_lt, ALU.mult)
            pool.drain()
            pool.tensor_tensor(hcode[:, 0, :], hcode[:, 0, :], code_a, ALU.add)
            pool.drain().then_inc(codes_ok, 1)

        def take_round(v, k):
            n = ECOL // PARTS
            for q in range(PARTS):
                v.max(key[:, ECOL + q * TAKE + 8 * k:ECOL + q * TAKE + 8 * k + 8], key[:, q * n:(q + 1) * n])
            v.drain()
            for q in range(PARTS):
                part, at = key[:, q * n:(q + 1) * n], ECOL + q * TAKE + 8 * k
                v.match_replace(part, key[:, at:at + 8], part, 4 * DEAD)
            v.drain()

        def score_weights(v):
            v.wait_ge(w_in, 16 * (len(weight_dmas) + 1))
            tmp = junk[:, 0:4 * HE].rearrange("p (k q f) -> p k q f", k=2, q=2)
            for k in range(2):
                v.tensor_tensor(tmp[:, k], wg2[:, :, HF], mid(att[:, k, :], 2), ALU.mult)
            v.drain()
            for k, part in enumerate((AS, AD)):
                v.reduce_sum(wg2[:, :, part], tmp[:, k].rearrange("p q (a b) -> p q a b", a=HEADS), axis=X)
            v.drain()

        def bounds_dve(v):
            v.tensor_reduce(ecnt[:, 6:7], key[:, ECOL + TAKE - 1:ECOL + PARTS * TAKE:TAKE], axis=X, op=ALU.max)
            v.drain().then_inc(ctl_mm, 1)
            rank_constants(v)
            score_weights(v)
            v.wait_ge(ctl_mm, 2)
            v.reduce_max(junk[0:1, 0:1], bank6[0:1, 0:P], axis=X)
            v.reduce_max(junk[0:1, 1:2], bank6[0:1, P:2 * P], axis=X)
            v.drain()
            v.tensor_scalar(ctl[0:1, 3:4], junk[0:1, 1:2], LIVE, None, ALU.is_ge)
            to_blocks(v, ctl[0:1, 0:1], junk[0:1, 0:1], BLK - 1, 4, 2)
            to_blocks(v, ctl[0:1, 2:3], junk[0:1, 0:1], BIG - 1, 5, 1)
            to_blocks(v, ctl[0:1, 5:6], junk[0:1, 0:1], WIDE - 1, 8, 1)
            v.drain().then_inc(nblk_ok, 1)

        def order_dve(v, nbig, keys, start=0):
            with v.Fori(start, nbig) as i:
                for q in range(BIG // 8):
                    v.max(top[:, 8 * q:8 * q + 8], keys)
                    v.drain()
                    v.match_replace(keys, top[:, 8 * q:8 * q + 8], keys, 4 * DEAD)
                    v.drain()
                v.tensor_copy(lkey_tab[:, bass.ds(i * BIG, BIG)], top[:, :])
                v.drain()

        def extract_dve(v, nbig):
            more = nc.vector.value_load(ctl[0:1, 3:4], min_val=0, max_val=1)
            with v.If(more == 1):
                order_dve(v, nbig, key[:, :])
            with v.Else():
                keys = key[:, ECOL:]
                for b in range(FIXED):
                    with v.If(nbig > b):
                        for q in range(BIG // 8):
                            best = lkey_tab[:, b * BIG + 8 * q:b * BIG + 8 * q + 8]
                            v.max(best, keys)
                            v.drain()
                            v.match_replace(keys, best, keys, 4 * DEAD)
                            v.drain()
                with v.If(nbig > FIXED):
                    order_dve(v, nbig, keys, FIXED)
            v.drain()

        def classes_dve(v, nwide, nbig):
            with v.Fori(0, nwide) as i:
                q_, r_ = cw[:, 0, :], cw[:, 1, :]
                keys, cls = lkey_tab[:, bass.ds(i * WIDE, WIDE)], cls_tab[:, bass.ds(i * WIDE, WIDE)]
                v.tensor_scalar(q_, keys, -0.5 * (NODES - 1), 1.0 / NODES, ALU.add, ALU.mult)
                v.drain()
                round_to(v, q_)
                v.scalar_tensor_tensor(r_, q_, float(-NODES), keys, ALU.mult, ALU.add)
                v.drain()
                v.scalar_tensor_tensor(q_, r_, float(NODES), q_, ALU.is_ge, ALU.add)
                v.drain()
                v.scalar_tensor_tensor(q_, r_, 0.0, q_, ALU.is_lt, ALU.subtract)
                v.drain()
                v.tensor_scalar(cls, q_, float(SLOTS // 2 - KEY0), -1.0 / SLOTS, ALU.add, ALU.mult)
                v.drain()
                round_to(v, cls)
                v.scalar_tensor_tensor(r_, cls, float(-SLOTS * NODES), keys, ALU.mult, ALU.add)
                v.drain()
                v.tensor_scalar(keys, r_, float(KEY0 * NODES + 1), None, ALU.add)
                v.drain()
            with v.Fori(0, nbig) as i:
                for q in range(BIG // BLK):
                    v.wait_ge(oh_used[q % 2], i * (BIG // BLK // 2) + (q // 2 + 1))
                    v.tensor_tensor(oh[:, q % 2, :, :], bc(cls_tab[:, bass.ds(i * BIG + q * BLK, BLK)], P),
                                    mid(iota_b[:, :], BLK), ALU.is_equal).then_inc(oh_ok[q % 2], 1)

        def starts_dve(v):
            v.wait_ge(cnt_ev, 1)
            v.tensor_copy(counts[:, :], bank6[:, 256:384])
            v.drain().then_inc(cnt_ev, 1)
            v.wait_ge(start_mm, 1)
            v.tensor_copy(ecnt[:, 1:2], bank6[:, 0:1])
            v.tensor_copy(countsT[:, :], bank6[:, 384:512])
            v.drain()
            to_blocks(v, rows64[:, :], ecnt[:, 1:2], ROW - 1, 6, 0)
            v.drain()
            v.tensor_copy(ecnt[:, 2:3], rows64[:, :])
            v.drain()
            v.tensor_copy(rows64r[:, :], ecnt[:, 2:3].broadcast_to([P, P]))
            v.drain().then_inc(cnt_ev, 1)
            v.wait_ge(base_mm, 1)
            v.tensor_copy(base[:, :], bank6[:, 256:384])
            v.tensor_copy(ecnt[:, 3:4], bank6[:, 2:3])
            v.reduce_max(junk[0:1, 0:1], bank6[0:1, P:2 * P], axis=X)
            v.drain()
            to_blocks(v, ctl[0:1, 4:5], junk[0:1, 0:1], GATHER - 1, 2, LEAST_COLS // GATHER)
            v.drain()
            v.tensor_scalar(ctl[0:1, 4:5], ctl[0:1, 4:5], float(CW // GATHER), float(-(LEAST_COLS // GATHER)),
                            ALU.min, ALU.add)
            v.tensor_scalar(junk[0:1, 0:1], junk[0:1, 0:1], 0.5 * (CW - 1), 1.0 / CW, ALU.add, ALU.mult)
            v.drain()
            round_to(v, junk[0:1, 0:1])
            v.tensor_scalar(junk[0:1, 0:1], junk[0:1, 0:1], 1.0, None, ALU.max)
            v.drain()
            v.tensor_copy(ctl[0:1, 1:2], junk[0:1, 0:1])
            v.drain().then_inc(chunk_ok, 1)

        def ranks_block(v, i):
            cls, column = cw[:, 0, 0:BIG], cw[:, 1, 0:BIG]
            v.tensor_scalar(column, cls_tab[:, bass.ds(i * BIG, BIG)], 0.0, FAR, ALU.is_lt, ALU.mult)
            v.tensor_copy(cls, cls_tab[:, bass.ds(i * BIG, BIG)])
            v.drain()
            v.tensor_tensor(column, column, jrow[:, :], ALU.add)
            for b in range(BIG // BLK):
                for j in range(b * BLK, (b + 1) * BLK):
                    v.scalar_tensor_tensor(unused[:, j, :], iota[:, 0:P], cls[:, j:j + 1], base[:, :],
                                           ALU.is_equal, ALU.mult, accum_out=ranks[:, j:j + 1])
                v.drain()
                v.tensor_tensor(rank_tab[:, bass.ds(i * BIG + b * BLK, BLK)], ranks[:, b * BLK:(b + 1) * BLK],
                                column[:, b * BLK:(b + 1) * BLK], ALU.add).then_inc(rank_ok, 1)
            v.tensor_scalar(jrow[:, :], jrow[:, :], float(BIG), None, ALU.add)
            v.drain()

        def to_blocks(v, out_i, in_f, less_one, shift, least):
            v.tensor_scalar(out_i, in_f, float(less_one), None, ALU.add)
            v.drain()
            v.tensor_scalar(out_i, out_i, shift, None, ALU.logical_shift_right)
            if least:
                v.drain()
                v.tensor_scalar(out_i, out_i, float(least), None, ALU.max)


        def chunk_rows(v, t):
            if t is None:
                for r in range(CROWS):
                    v.tensor_scalar(rowf[:, r:r + 1], ecnt[:, 3:4], float(r), float(LAST_ROW), ALU.add, ALU.min)
                v.tensor_copy(ecnt[:, 4:5], ecnt[:, 1:2])
                v.drain()
                v.tensor_copy(rowi[:, :], rowf[:, :])
                v.drain().then_inc(rowi_ok, 1)
            else:
                v.tensor_scalar(rowf[:, :], rowf[:, :], float(CROWS), float(LAST_ROW), ALU.add, ALU.min)
                v.tensor_scalar(ecnt[:, 4:5], ecnt[:, 4:5], float(CW), None, ALU.subtract)
                v.drain()
                v.tensor_copy(rowi[:, :], rowf[:, :])
                v.drain().then_inc(rowi_ok, 1)

        def leaky(v, out, z, tmp):
            v.tensor_scalar(tmp, z, 0.2, None, ALU.mult)
            v.drain()
            v.tensor_tensor(out, z, tmp, ALU.max)
            v.drain()

        def graph_start(v):
            v.wait_ge(nn_in, 32)
            v.wait_ge(hsum_in, 16)
            own, last, t4, lcb = n4[:, 0], n4[:, 1], n4[:, 2], n4[:, 3]
            v.tensor_tensor(t4, nn[:, :, AS], nn[:, :, AD], ALU.add)
            v.drain()
            leaky(v, own, t4, lcb)
            v.tensor_tensor(t4, mid(lastr[:, AS], SLOTS), nn[:, :, AD], ALU.add)
            v.drain()
            leaky(v, last, t4, lcb)
            v.tensor_copy(lcb, bc(lastc[:, :], HEADS))
            v.drain()
            v.tensor_scalar(t4, lcb, 0.5, -1.0e30, ALU.is_lt, ALU.mult)
            v.drain()
            v.tensor_tensor(t4, last, t4, ALU.add)
            v.drain()
            v.tensor_tensor(st[:, :, MX], own, t4, ALU.max)
            v.drain()
            v.tensor_tensor(own, own, st[:, :, MX], ALU.subtract)
            v.tensor_tensor(last, last, st[:, :, MX], ALU.subtract)
            v.drain()
            v.tensor_scalar(last, last, 0.0, None, ALU.min)
            v.drain().then_inc(a_req, 1)
            v.wait_ge(a_done, 3)
            v.tensor_tensor(last, last, lcb, ALU.mult)
            v.drain()
            v.tensor_tensor(st[:, :, DN], own, last, ALU.add)
            v.tensor_tensor(heads(n16[:, 0]), heads(nn[:, :, HF]), bc4(own), ALU.mult)
            v.tensor_tensor(heads(n16[:, 1]), heads(mid(lastr[:, HF], SLOTS)), bc4(last), ALU.mult)
            v.drain()
            v.tensor_tensor(st[:, :, NM], n16[:, 0], n16[:, 1], ALU.add)
            v.drain()

        def add_bias(v, e):
            v.tensor_tensor(ye[:, e], ye[:, e], mid(b2r[:, e, :], SLOTS), ALU.add)

        def combine(eng, slots, own, done=0):
            eng.wait_ge(bias_ok, 1)
            eng.wait_ge(gate_in, 16 * 3)
            n = slots.stop - slots.start
            for e in range(own):
                eng.tensor_tensor(ye[:, e, slots, :], ye[:, e, slots, :],
                                  gtok[:, slots, e].unsqueeze(2).broadcast_to([P, n, H]), ALU.mult)
            eng.drain()
            for e in range(EXPERTS):
                if e >= own:
                    eng.wait_ge(prod_ok, done + e - own + 1)
                eng.tensor_tensor(h0[:, slots, :], h0[:, slots, :], ye[:, e, slots, :], ALU.add)
                eng.drain()

        def heads(ap):
            return ap.rearrange("p s (a b) -> p s a b", a=HEADS)

        def bc4(ap):
            return ap.unsqueeze(3).broadcast_to([P, SLOTS, HEADS, EXPERTS])

        def sort_rounds(v, start, end):
            for k in range(start, end):
                v.max(skey[:, 8 * k:8 * k + 8], chunk[:, :])
                v.drain()
                if k < CW // 8 - 1:
                    v.match_replace(chunk[:, :], skey[:, 8 * k:8 * k + 8], chunk[:, :], -1.0)
                    v.drain()

        def chunk_sort(v, t):
            v.wait_ge(chunk_in, t + 1)
            v.tensor_scalar(ctmp[:, :], iota[:, :], ecnt[:, 4:5], None, ALU.is_lt)
            v.drain()
            v.tensor_tensor(chunk[:, :], chunk[:, :], ctmp[:, :], ALU.mult)
            v.drain()
            sort_rounds(v, 0, CW // 16)

        def sources(v, lo, hi):
            at = slice(lo, hi)
            v.tensor_scalar(place[:, at], skey[:, at], -1.0 - 0.5 * (NODES - 1), 1.0 / NODES, ALU.add, ALU.mult)
            v.drain()
            round_to(v, place[:, at])
            v.scalar_tensor_tensor(ctmp[:, at], place[:, at], float(-NODES), skey[:, at], ALU.mult, ALU.add)
            v.drain()
            v.tensor_scalar(srci[:, at], ctmp[:, at], -1.0, None, ALU.add)
            v.drain().then_inc(src_ok, 1)

        def chunk_sources(v, first=False):
            if first:
                extra = nc.vector.value_load(ctl[0:1, 4:5], min_val=0, max_val=(CW - LEAST_COLS) // GATHER)
                v.memset(skey[:, 8 * FEW_ROUNDS:], 0.0)
                sort_rounds(v, CW // 16, FEW_ROUNDS)
                with v.If(extra > (8 * FEW_ROUNDS - LEAST_COLS) // GATHER):
                    sort_rounds(v, FEW_ROUNDS, CW // 8)
                v.drain()
            else:
                sort_rounds(v, CW // 16, CW // 8)
            if first:
                v.memset(gath[:, LEAST_COLS:, :], 0.0)
            sources(v, CW // 2 if first else 0, CW)
            v.memset(keep[:, 0:1], 0.0)
            v.tensor_tensor(keep[:, 1:CW], place[:, 1:CW], place[:, 0:CW - 1], ALU.is_equal)
            v.drain()
            v.tensor_scalar(ctmp[:, :], keep[:, :], -1.0, 1.0e30, ALU.add, ALU.mult)
            v.drain()

        def chunk_places(v, first=False):
            v.tensor_copy(place_b[:, :], place[:, :])
            v.memset(ends[:, SLOTS:SLOTS + 1], 0.0)
            v.drain()
            for s in range(SLOTS):
                v.tensor_scalar(place_m[:, s, :], place_b[:, :], float(s), 0.0, ALU.is_ge, ALU.add,
                                accum_out=ends[:, s:s + 1])
            v.drain()
            for s in range(SLOTS):
                v.tensor_scalar(place_m[:, s, :], place_b[:, :], float(s), None, ALU.is_equal)
            v.tensor_tensor(has[:, :], ends[:, 0:SLOTS], ends[:, 1:SLOTS + 1], ALU.is_gt)
            if first:
                v.tensor_copy(ecnt[:, 6:7], ends[:, UPPER:UPPER + 1])
            v.drain()
            v.tensor_scalar(ends[:, 0:SLOTS], ends[:, 0:SLOTS], -1.0, 0.0, ALU.add, ALU.max)
            v.tensor_scalar(ecnt[:, 5:6], ecnt[:, 7:8], float(CW), None, ALU.mult)
            v.drain()
            if first:
                v.tensor_scalar(upper[:, :], ends[:, UPPER:SLOTS], float(LEAST_COLS - 1), None, ALU.min)
                v.tensor_scalar(ecnt[:, 1:2], ecnt[:, 7:8], float(LEAST_COLS), None, ALU.mult)
                v.drain()
                v.tensor_scalar(upper[:, :], upper[:, :], ecnt[:, 1:2], None, ALU.add)
                v.drain()
                v.tensor_copy(upperi[:, :], upper[:, :])
                v.drain().then_inc(upper_ok, 1)
            v.tensor_scalar(ends[:, 0:SLOTS], ends[:, 0:SLOTS], ecnt[:, 5:6], None, ALU.add)
            v.drain()
            v.tensor_copy(endi[:, :], ends[:, 0:SLOTS])
            v.drain().then_inc(endi_ok, 1)

        def upper_dve(v):
            v.wait_ge(upper_mm, 1)
            v.reduce_max(junk[0:1, 0:1], bank6[0:1, 0:P], axis=X)
            v.drain()
            v.tensor_scalar(ctl[0:1, 6:7], junk[0:1, 0:1], float(LEAST_COLS), None, ALU.is_le)
            v.drain().then_inc(upper_known, 1)

        def nodes_dst(v):
            v.tensor_copy(node_dst, nn[:, :, AD])
            v.drain()

        def chunk_dst(v, start, end):
            if start == 0:
                v.memset(adst[:, :, :], 0.0)
                v.drain()
            for s in range(start, end):
                v.copy_predicated(adst[:, :, :], mid(place_m[:, s, :].bitcast(U16), HEADS), bc(node_dst[:, s, :], CW))
                v.drain()

        def scan_scores(v, lo, hi):
            v.tensor_tensor(adst[:, :, lo:hi], adst[:, :, lo:hi], gath[:, lo:hi, AS].rearrange("p l a -> p a l"),
                            ALU.add)
            v.drain()
            leaky(v, eh[:, :, lo:hi], adst[:, :, lo:hi], mh[:, :, lo:hi])
            for h in range(HEADS):
                v.tensor_tensor_scan(mh[:, h, lo:hi], ctmp[:, lo:hi], eh[:, h, lo:hi],
                                     mh[:, h, lo - 1:lo] if lo else 0.0, ALU.add, ALU.max)
            v.drain()
            after = max(lo, 1)
            if not lo:
                v.memset(rh[:, :, 0:1], 0.0)
            v.tensor_tensor(rh[:, :, after:hi], mh[:, :, after - 1:hi - 1], mh[:, :, after:hi], ALU.subtract)
            v.tensor_tensor(wh[:, :, lo:hi], eh[:, :, lo:hi], mh[:, :, lo:hi], ALU.subtract)
            v.drain()
            v.tensor_scalar(rh[:, :, lo:hi], rh[:, :, lo:hi], 0.0, None, ALU.min)
            v.drain().then_inc(a_req, 1)

        def scan_sums(v, lo, hi, done):
            v.wait_ge(a_done, done)
            v.tensor_tensor(rh[:, :, lo:hi], rh[:, :, lo:hi], mid(keep[:, lo:hi], HEADS), ALU.mult)
            for h in range(HEADS):
                v.tensor_tensor(xh[:, 4 * h:4 * h + 4, lo:hi],
                                gath[:, lo:hi, 8 + 4 * h:12 + 4 * h].rearrange("p l a -> p a l"),
                                mid(wh[:, h, lo:hi], EXPERTS), ALU.mult)
            v.tensor_copy(scans[:, lo:hi, MX], mh[:, :, lo:hi].rearrange("p a l -> p l a"))
            v.drain()
            for f in range(HEADS + HE):
                h = f if f < HEADS else (f - HEADS) // 4
                v.tensor_tensor_scan(scans[:, lo:hi, 4 + f], rh[:, h, lo:hi],
                                     wh[:, h, lo:hi] if f < HEADS else xh[:, f - HEADS, lo:hi],
                                     scans[:, lo - 1, 4 + f:5 + f] if lo else 0.0, ALU.mult, ALU.add)
            v.drain().then_inc(scan_ok, 1)

        def chunk_merge(v, t):
            hb, mc, old, new, dn = n4[:, 0], n4[:, 1], n4[:, 2], n4[:, 3], n4[:, 4]
            v.tensor_copy(hb, bc(has[:, :], HEADS))
            v.drain()
            v.tensor_scalar(mc, hb, -1.0, 1.0e30, ALU.add, ALU.mult)
            v.drain()
            v.wait_ge(seg_in, t + 1)
            v.tensor_tensor(mc, mc, seg[:, :, MX], ALU.add)
            v.drain()
            v.tensor_tensor(mc, mc, st[:, :, MX], ALU.max)
            v.drain()
            v.tensor_tensor(old, st[:, :, MX], mc, ALU.subtract)
            v.tensor_tensor(new, seg[:, :, MX], mc, ALU.subtract)
            v.drain()
            v.tensor_scalar(new, new, 0.0, None, ALU.min)
            v.tensor_copy(st[:, :, MX], mc)
            v.drain().then_inc(a_req, 1)
            v.wait_ge(a_done, 4 + 2 * t)
            v.tensor_tensor(new, new, hb, ALU.mult)
            v.drain()
            v.tensor_tensor(st[:, :, DN], st[:, :, DN], old, ALU.mult)
            v.tensor_tensor(dn, seg[:, :, DN], new, ALU.mult)
            v.tensor_tensor(heads(n16[:, 0]), heads(st[:, :, NM]), bc4(old), ALU.mult)
            v.tensor_tensor(heads(n16[:, 1]), heads(seg[:, :, NM]), bc4(new), ALU.mult)
            v.drain()
            v.tensor_tensor(st[:, :, DN], st[:, :, DN], dn, ALU.add)
            v.tensor_tensor(st[:, :, NM], n16[:, 0], n16[:, 1], ALU.add)
            v.drain()

        def graph_end(v, n):
            inv, agg, x2 = n4[:, 0], n16[:, 0], n16[:, 1]
            v.tensor_scalar(inv, st[:, :, DN], 1e-16, None, ALU.add)
            v.drain()
            v.reciprocal(inv, inv)
            v.drain()
            v.tensor_tensor(heads(agg), heads(st[:, :, NM]), bc4(inv), ALU.mult)
            v.drain()
            v.tensor_tensor(agg, agg, mid(gamr[:, 0, :], SLOTS), ALU.add)
            v.drain()
            v.reduce_sum(s1[:, :], agg, axis=X)
            v.drain()
            v.tensor_scalar(s1[:, :], s1[:, :], 1.0 / HE, None, ALU.mult)
            v.drain()
            v.tensor_tensor(agg, agg, bc(s1[:, :], HE), ALU.subtract)
            v.drain()
            v.tensor_tensor(x2, agg, agg, ALU.mult)
            v.drain()
            v.reduce_sum(s2[:, :], x2, axis=X)
            v.drain()
            v.tensor_scalar(s2[:, :], s2[:, :], 1.0 / HE, EPS, ALU.mult, ALU.add).then_inc(var_ok, 1)
            v.wait_ge(rt_ok, LAYERS + 4)
            v.reciprocal(s1[:, :], s3[:, :])
            v.drain()
            v.tensor_tensor(agg, agg, bc(s1[:, :], HE), ALU.mult)
            v.drain()
            v.tensor_tensor(agg, agg, mid(gamr[:, 1, :], SLOTS), ALU.mult)
            v.drain()
            v.tensor_tensor(agg, agg, mid(gamr[:, 2, :], SLOTS), ALU.add)
            v.drain()
            sc, ex, sel = n4[:, 0], n4[:, 1], n4[:, 2]
            v.reduce_sum(sc, agg.rearrange("p s (a b) -> p s b a", a=HEADS), axis=X)
            v.drain()
            v.tensor_scalar(sc, sc, 1.0 / HEADS, None, ALU.mult)
            v.drain()
            for e in range(EXPERTS):
                for o in range(EXPERTS):
                    if o != e:
                        v.tensor_tensor(n4[:, 3 + e, :, o], sc[:, :, o], sc[:, :, e],
                                        ALU.is_ge if o < e else ALU.is_gt)
                    else:
                        v.memset(n4[:, 3 + e, :, o], 0.0)
            v.drain()
            for e in range(EXPERTS):
                v.reduce_sum(sel[:, :, e], n4[:, 3 + e], axis=X)
            v.reduce_max(s1[:, :], sc, axis=X)
            v.drain()
            v.tensor_scalar(sel, sel, 1.5, None, ALU.is_lt)
            v.tensor_tensor(ex, sc, bc(s1[:, :], EXPERTS), ALU.subtract)
            v.drain().then_inc(a_req, 1)
            v.wait_ge(a_done, n * 2 + 3)
            v.tensor_tensor(ex, ex, sel, ALU.mult)
            v.drain()
            v.reduce_sum(s1[:, :], ex, axis=X)
            v.drain()
            v.reciprocal(s1[:, :], s1[:, :])
            v.drain()
            v.memset(gtok[:, :, :], 0.0)
            v.tensor_tensor(gates[:, :, :], ex, bc(s1[:, :], EXPERTS), ALU.mult)
            v.drain().then_inc(gate_ok, 1)

        @block.sync
        def _(sp):
            ev = edge_index.rearrange("a (p e) -> p a e", p=P)
            sp.dma_start(raw[:, 1, :], ev[:, 1, :]).then_inc(e_in[1], 16)
            sp.dma_start(raw[:, 0, :], ev[:, 0, :]).then_inc(e_in[0], 16)
            sp.dma_start(waver[:, :], c_waver).then_inc(c_in, 16)
            sp.dma_start(wave[:, :], c_wave).then_inc(c_in, 16)
            for i in range(X_PARTS):
                sp.dma_start(xs[:, i * NX:(i + 1) * NX, :],
                             x[i * NX:(i + 1) * NX, 0].rearrange("b r c -> r b c")).then_inc(x_in[i], 16)
            sp.dma_start(eye[:, :], c_eye).then_inc(c_in, 16)
            sp.dma_start(before[:, :], c_before).then_inc(c_in, 16)
            sp.dma_start(pick[:, :], c_pick).then_inc(c_in, 16)
            sp.wait_ge(zero_ok, 1)
            for dst, src in weight_dmas[ACT_LOADS:]:
                sp.dma_start(dst, src).then_inc(w_in, 16)
            sp.wait_ge(pool_c, 1)
            lz = edge_list.rearrange("(k p f) a -> k p (f a)", p=P, f=529)
            for k in range(4):
                sp.dma_start(lz[k], zeros[:, :]).then_inc(list_zero, 16)
            pad = NODE_ROWS - NODES
            sp.dma_start(node_tab[NODES:NODE_ROWS, :], zeros[0:pad, 0:NF]).then_inc(nt_st, 16)
            sp.dma_start(last_tab[NODES:NODE_ROWS].rearrange("(a b) -> a b", a=1),
                         zeros[0:1, 0:pad]).then_inc(hsum_st, 16)
            sp.wait_ge(nblk_ok, 1)
            nblk = nc.sync.value_load(ctl[0:1, 0:1], min_val=2, max_val=MAX_BLK)
            with sp.Fori(1, nblk) as i:
                ring_fill(sp, i)
            sp.wait_ge(nt_ok, 1)
            store_tokens(sp, node_tab, nt, NF, nt_st)
            sp.wait_ge(nt_st, 16 * 4)
            sp.dma_start(nn[:, :, :], node_tab.rearrange("(p s) f -> p s f", s=SLOTS)).then_inc(nn_in, 16)
            sp.dma_start(lastr[:, :], node_tab[NODES - 1:NODES, :].broadcast_to([P, NF])).then_inc(nn_in, 16)
            for k in range(sum(TILES) - 1):
                expert_store(sp, k)
            scan_rows = scan_tab.rearrange("(p l) f -> p l f", l=CW)
            sp.wait_ge(scan_ok, 1)
            sp.dma_start(first_tab.rearrange("(p l) f -> p l f", l=LEAST_COLS),
                         scans[:, 0:LEAST_COLS, :]).then_inc(first_st, 16)
            sp.dma_start(scan_rows[:, 0:LEAST_COLS, :], scans[:, 0:LEAST_COLS, :]).then_inc(scan_st, 16)
            sp.wait_ge(hsum_ok, 1)
            sp.dma_start(last_tab[0:NODES].rearrange("(a b) -> a b", b=DLO), hsum[:, :]).then_inc(hsum_st, 16)
            sp.wait_ge(hsum_st, 32)
            sp.dma_start(lastc[:, :], last_tab.rearrange("(p s) -> p s", s=SLOTS)).then_inc(hsum_in, 16)
            sp.wait_ge(ye_st, 16 * 9 * (EXPERTS - 1))
            sp.dma_start(ye[:, 0:EXPERTS - 1], ye_tab[:, 0:EXPERTS - 1]).then_inc(ye_in[0], 16)
            sp.wait_ge(scan_ok, 2)
            sp.dma_start(scan_rows[:, LEAST_COLS:, :], scans[:, LEAST_COLS:, :]).then_inc(scan_st, 16)
            for k in range(sum(TILES) - 1, 9 * EXPERTS):
                expert_store(sp, k)
            sp.wait_ge(ye_st, 16 * 9 * EXPERTS)
            sp.dma_start(ye[:, EXPERTS - 1], ye_tab[:, EXPERTS - 1]).then_inc(ye_in[1], 16)
            sp.wait_ge(chunk_ok, 1)
            n = nc.sync.value_load(ctl[0:1, 1:2], min_val=1, max_val=MAX_CHUNKS)
            with sp.If(n > 1):
                with sp.Fori(1, n) as t:
                    sp.wait_ge(scan_ok, t + 2)
                    sp.dma_start(scan_rows, scans).then_inc(scan_st, 16)
            sp.wait_ge(gate_ok, 1)
            sp.dma_start(gate_tab.rearrange("(p s) f -> p s f", s=SLOTS), gates[:, :, :]).then_inc(gate_st, 16)
            sp.wait_ge(gate_st, 16)
            grow = gate_tab[0:NODES].rearrange("(b t) f -> b t f", t=TOK)
            for half in range(2):
                sp.dma_start(gtok[64 * half:64 * half + 64, 0:32, :],
                             grow[:, 1 + 32 * half:33 + 32 * half, :]).then_inc(gate_in, 16)
            sp.dma_start(gtok[0:64, 32, :], grow[:, 0, :]).then_inc(gate_in, 16)
            result = out.rearrange("b t h -> (b t) h")
            sp.wait_ge(done_dve, 1)
            store_tokens(sp, result, h0, H, d_out, slice(0, V_SLOTS // 2))
            sp.wait_ge(slots_ok, 1)
            store_tokens(sp, result, h0, H, d_out, slice(V_SLOTS, SLOTS))
            sp.wait_ge(done_dve, 2)
            store_tokens(sp, result, h0, H, d_out, slice(V_SLOTS // 2, V_SLOTS))
            sp.wait_ge(d_out, 16 * 7)

        @block.scalar
        def _(act):
            act.wait_ge(zero_ok, 1)
            for dst, src in weight_dmas[:ACT_LOADS]:
                act.dma_start(dst, src).then_inc(w_in, 16)
            act.dma_start(b1c[:, :], b1.rearrange("e f -> f e"), allow_slow_non_contiguous=True).then_inc(w_in, 16)
            for i in range(16):
                act.wait_ge(x_rows, i + 1)
                act.activation(y1[:, 4 * i:4 * i + 4, :],
                               wide[0:SIDE, (i % 4) * 512:(i % 4) * 512 + 128].rearrange("p (b m) -> p b m", b=4),
                               ACT.Copy).then_inc(x_rows_out, 1)
            for i in range(4):
                act.wait_ge(x_cols, i + 1)
                act.activation(y2[:, :, 16 * i:16 * i + 16].rearrange("n m b -> n b m"),
                               wide[0:32, i * 512:i * 512 + 512].rearrange("n (b m) -> n b m", m=32),
                               ACT.Copy).then_inc(x_cols_out, 1)
            for n in range(PREP_STEPS):
                kernel_step(act, n)
            root(act, 1)
            for r in range(LAYERS + 2):
                evacuate_T(act, r)
                if 1 <= r <= LAYERS:
                    for k, a in enumerate(HALVES):
                        act.wait_ge(y_ok, 2 * r - 1 + k)
                        act.activation(sq[:, a, :], xc[:, a, :], ACT.Gelu).then_inc(g_ok, 1)
                    root(act, r + 1)
                if r == LAYERS:
                    root(act, r + 2)
            root(act, LAYERS + 3)
            evacuate_T(act, LAYERS + 2)
            for k in range(sum(TILES[:-1])):
                expert_act(act, k)
            act.wait_ge(a_req, 1)
            exp_edges(act, 0, LEAST_COLS)
            for k in range(sum(TILES[:-1]), sum(TILES)):
                expert_act(act, k)
            act.wait_ge(a_req, 2)
            exp_edges(act, LEAST_COLS, CW)
            act.wait_ge(a_req, 3)
            act.activation(n4[:, 0:2], n4[:, 0:2], ACT.Exp).then_inc(a_done, 1)
            for k in range(sum(TILES), 9 * EXPERTS + 1):
                expert_act(act, k)
            act.wait_ge(a_req, 4)
            act.activation(n4[:, 2:4], n4[:, 2:4], ACT.Exp).then_inc(a_done, 1)
            n = nc.scalar.value_load(ctl[0:1, 1:2], min_val=1, max_val=MAX_CHUNKS)
            with act.If(n > 1):
                with act.Fori(1, n) as t:
                    act.wait_ge(a_req, 3 + 2 * t)
                    exp_edges(act, 0, CW)
                    act.wait_ge(a_req, 4 + 2 * t)
                    act.activation(n4[:, 2:4], n4[:, 2:4], ACT.Exp).then_inc(a_done, 1)
            act.wait_ge(var_ok, LAYERS + 4)
            act.activation(s3[:, :], s2[:, :], ACT.Sqrt).then_inc(rt_ok, 1)
            act.wait_ge(a_req, 3 + 2 * n)
            act.activation(n4[:, 1], n4[:, 1], ACT.Exp).then_inc(a_done, 1)
            act.wait_ge(bias_ok, 1)
            act.wait_ge(gate_in, 16 * 3)
            for k in range(2):
                for s_ in range(k * V_SLOTS // 2, (k + 1) * V_SLOTS // 2):
                    last = act.activation(ye[:, OWN, s_, :], ye[:, OWN, s_, :], ACT.Copy,
                                          scale=gtok[:, s_, OWN:OWN + 1])
                last.then_inc(prod_ok, 1)

        @block.gpsimd
        def _(pool):
            pool.memset(tokw[:, :, :], 0.0)
            pool.memset(win2[:, :, :], 0.0)
            pool.memset(conv[:, :, :], 0.0)
            pool.memset(h0[:, 32, :], 0.0)
            pool.memset(mean64[:, :], 1.0 / H)
            pool.memset(wg2[:, :, :], 0.0)
            pool.drain().then_inc(zero_ok, 1)
            pool.memset(zeros[:, :], 0.0)
            pool.memset(ones_f[:, :], 1.0)
            pool.memset(zero_b[:, :], 0.0)
            pool.iota(iota[:, :], [[1, CW]], base=0, channel_multiplier=0, allow_small_or_imprecise_dtypes=True)
            pool.iota(iota_b[:, :], [[1, P]], base=0, channel_multiplier=0, allow_small_or_imprecise_dtypes=True)
            pool.iota(ecnt[:, 7:8], [[0, 1]], base=0, channel_multiplier=1, allow_small_or_imprecise_dtypes=True)
            pool.drain().then_inc(pool_c, 1)
            spread_weights(pool)
            last_codes(pool)
            pool.wait_ge(list_zero, 64)
            pool.wait_ge(nblk_ok, 1)
            nblk = nc.gpsimd.value_load(ctl[0:1, 0:1], min_val=2, max_val=MAX_BLK)
            pool.wait_ge(rank_ok, 1)
            for j in range(BLK):
                scatter_column(pool, j // (BLK // 2), rank_tab[:, j:j + 1], lkey_tab[:, j:j + 1])
            with pool.Fori(1, nblk) as i:
                scatter_block(pool, i)
            await_then_pass(pool, scat[0], nblk * (8 * BLK), pool_passed)
            await_then_pass(pool, scat[1], nblk * (8 * BLK), pool_passed)
            pool.wait_ge(rowi_ok, 1)
            fetch(pool, [chunk[:, r * ROW:(r + 1) * ROW] for r in range(CROWS)], edge_rows, rowi, chunk_in, 0)
            pool.wait_ge(nt_st, 16 * 4)
            pool.wait_ge(src_ok, 1)
            chunk_pool(pool, 0, first=True)
            n = nc.gpsimd.value_load(ctl[0:1, 1:2], min_val=1, max_val=MAX_CHUNKS)
            with pool.If(n > 1):
                with pool.Fori(1, n) as t:
                    pool.dma_reset()
                    pool.sem_clear(fetched)
                    await_then_pass(pool, rowi_ok, t + 1, pool_passed)
                    fetch(pool, [chunk[:, r * ROW:(r + 1) * ROW] for r in range(CROWS)], edge_rows, rowi, chunk_in, 0)
                    await_then_pass(pool, src_ok, t + 2, pool_passed)
                    chunk_pool(pool, t)
                pool.drain()
            combine(pool, slice(V_SLOTS, SLOTS), EXPERTS)
            pool.drain().then_inc(slots_ok, 1)

        @block.tensor
        def _(pe):
            pe.wait_ge(c_in, 16 * 5)
            for i in range(16):
                pe.wait_ge(x_in[i // 4], 16)
                if i >= 4:
                    pe.wait_ge(x_rows_out, i - 3)
                for k in range(4):
                    last = pe.matmul(wide[0:SIDE, (i % 4) * 512 + 32 * k:(i % 4) * 512 + 32 * k + 32],
                                     xs[:, 4 * i + k, :], waver[:, :], start=True, stop=True)
                last.then_inc(x_rows, 1)
            bounds_pe(pe)
            pe.wait_ge(x_rows_out, 16)
            for i in range(4):
                pe.matmul(wide[0:32, i * 512:i * 512 + 512], wave[:, :],
                          y1[:, 16 * i:16 * i + 16, :], start=True, stop=True).then_inc(x_cols, 1)
            pe.wait_ge(x_cols_out, 4)
            pe.wait_ge(tokwd_ok, 1)
            for i in range(4):
                for g in range(4):
                    lhs = y2[:, 8 * g + 2 * i:8 * g + 2 * i + 2, :].rearrange("n q b -> n (q b)")
                    last = pe.matmul(wide[:, i * 512:i * 512 + 512], lhs,
                                     tokwd[:, g, :, :], start=(g == 0), stop=(g == 3))
                last.then_inc(tok_mm, 1)
            prep_weights(pe)
            edges_pe(pe)
            prep_powers(pe)
            for r in range(LAYERS + 2):
                transposes(pe, r)
                for k in range(5):
                    pe.wait_ge(t_ev, 5 * r + k + 1)
                    if 1 <= r <= LAYERS:
                        for i in range(4 * k, min(4 * k + 4, PAIRS)):
                            m = mix(pe, r - 1, i)
                        if k == 4:
                            m.then_inc(mix_ok, 1)
                    if k >= 1:
                        for i in range(4 * k - 4, 4 * k):
                            linear(pe, r, i)
                linear(pe, r, PAIRS - 1).then_inc(y_mm, 1)
                if r == 5:
                    count_last_pe(pe, 0)
            r = LAYERS + 2
            transposes(pe, r)
            pe.wait_ge(t_ev, 5 * r + 5)
            for i in range(PAIRS):
                at = 512 * (i // 10) + 2 * NF * (i % 10)
                last = (pe.matmul(wide[:, at:at + 2 * NF], uT[:, i, :], wg2[:, :, :], start=True, stop=True)
                        if i < 16 else
                        pe.matmul(wide[:, at:at + NF], uT[0:64, 16, :], wg2[0:64, 0, :], start=True, stop=True))
            last.then_inc(y_mm, 1)
            pe.wait_ge(nt_ok, 1)
            k = 0
            for g, tiles in zip(range(EARLY, H_GROUPS), TILES):
                for _ in range(tiles):
                    expert_tile(pe, k)
                    k += 1
                count_last_pe(pe, g)
                if g == EARLY:
                    pe.wait_ge(upper_ok, 1)
                    pe.transpose(bank6[0:1, 0:P], ecnt[:, 6:7], eye[:, :]).then_inc(upper_mm, 1)
            for k in range(k, 9 * EXPERTS + 1):
                expert_tile(pe, k)

        @block.vector
        def _(v):
            keys_dve(v)
            for k in range(TAKE // 8):
                take_round(v, k)
            bounds_dve(v)
            nbig = nc.vector.value_load(ctl[0:1, 2:3], min_val=1, max_val=ECOL // BIG)
            extract_dve(v, nbig)
            nwide = nc.vector.value_load(ctl[0:1, 5:6], min_val=1, max_val=ECOL // WIDE)
            classes_dve(v, nwide, nbig)
            starts_dve(v)
            chunk_rows(v, None)
            ranks_block(v, 0)
            for i in range(4):
                v.wait_ge(tok_mm, i + 1)
                v.tensor_tensor(h0[:, 8 * i:8 * i + 8, :],
                                wide[:, i * 512:i * 512 + 512].rearrange("p (s h) -> p s h", h=H),
                                mid(tokb[:, :], 8), ALU.add)
            v.drain()
            v.wait_ge(codes_ok, 1)
            layer_norm(v, 1, h0[:, :, :], u[:, :, :])
            with v.If(nbig > 1):
                ranks_block(v, 1)
            v.wait_ge(y_mm, 1)
            for a in EIGHTS:
                v.tensor_tensor(u[:, a, :], wtok[:, a, :], mid(binr[:, :], a.stop - a.start), ALU.add)\
                    .then_inc(u_ok, 1)
            with v.If(nbig > 2):
                ranks_block(v, 2)
            for l in range(LAYERS):
                v.wait_ge(mix_ok, 1 + l)
                v.tensor_copy(yrow[:, :], bank5[:, 1:33])
                v.tensor_copy(yfar[64:128, :], bank5[0:64, 33:65])
                v.drain()
                v.tensor_tensor(yrow[64:128, :], yrow[64:128, :], yfar[64:128, :], ALU.add)
                v.drain()
                v.wait_ge(y_mm, 2 + l)
                v.tensor_tensor(xc[:, 0:16, :], wtok[:, 0:16, :], bc(yrow[:, 0:16], H), ALU.add).then_inc(y_ok, 1)
                v.tensor_tensor(xc[:, 16:32, :], wtok[:, 16:32, :], bc(yrow[:, 16:32], H), ALU.add)
                v.tensor_copy(xc[:, 32, :], wtok[:, 32, :])
                v.drain().then_inc(y_ok, 1)
                for k, a in enumerate(HALVES):
                    v.wait_ge(g_ok, 2 * l + k + 1)
                    v.tensor_tensor(u[:, a, :], u[:, a, :], sq[:, a, :], ALU.add)
                v.drain()
                layer_norm(v, 2 + l, u[:, :, :], u[:, :, :], signal=l < LAYERS - 1)
                if l == LAYERS - 1:
                    layer_norm(v, 3 + l, u[:, :, :], u[:, :, :])
                if l == 0:
                    with v.If(nbig > 3):
                        ranks_block(v, 3)
                elif l == 1:
                    with v.If(nbig > 4):
                        with v.Fori(4, nbig) as i:
                            ranks_block(v, i)
                        v.drain()
                else:
                    count_last_dve(v, 0, l - 2)
            v.tensor_tensor(h0[:, :, :], h0[:, :, :], mid(boutr[:, :], SLOTS), ALU.add)
            v.drain()
            v.wait_ge(y_mm, LAYERS + 2)
            v.tensor_tensor(h0[:, :, :], h0[:, :, :], wtok, ALU.add)
            v.drain()
            layer_norm(v, LAYERS + 3, h0[:, :, :], u[:, :, :])
            chunk_sort(v, 0)
            v.wait_ge(y_mm, LAYERS + 3)
            v.tensor_copy(nt[:, 0:20, :], wide[:, 0:20 * NF].rearrange("p (s f) -> p s f", f=NF))
            v.tensor_copy(nt[:, 20:SLOTS, :], wide[:, 512:512 + 13 * NF].rearrange("p (s f) -> p s f", f=NF))
            v.drain().then_inc(nt_ok, 1)
            sources(v, 0, CW // 2)
            chunk_sources(v, first=True)
            for g in range(EARLY, H_GROUPS):
                count_last_dve(v, g, 0, 1)
                k = g - EARLY
                if k == 0:
                    chunk_places(v, first=True)
                    v.wait_ge(nn_in, 32)
                    nodes_dst(v)
                elif k <= 4:
                    if k == 1:
                        upper_dve(v)
                    chunk_dst(v, SLOTS * (k - 1) // 4, SLOTS * k // 4)
                elif k == 5:
                    v.wait_ge(first_in, 16 * LEAST_COLS)
                    scan_scores(v, 0, LEAST_COLS)
                    scan_sums(v, 0, LEAST_COLS, 1)
            v.wait_ge(gath_in, 1)
            scan_scores(v, LEAST_COLS, CW)
            v.wait_ge(h_used, H_GROUPS)
            v.tensor_copy(hsum[:, :], bank7[0:DHI, 0:DLO])
            v.drain().then_inc(hsum_ok, 1)
            scan_sums(v, LEAST_COLS, CW, 2)
            graph_start(v)
            v.wait_ge(ye_in[0], 16)
            for e in range(EXPERTS - 1):
                add_bias(v, e)
            chunk_merge(v, 0)
            n = nc.vector.value_load(ctl[0:1, 1:2], min_val=1, max_val=MAX_CHUNKS)
            with v.If(n > 1):
                with v.Fori(1, n) as t:
                    chunk_rows(v, t)
                    chunk_sort(v, t)
                    chunk_sources(v)
                    chunk_places(v)
                    chunk_dst(v, 0, SLOTS)
                    v.wait_ge(gath_in, t + 1)
                    scan_scores(v, 0, CW)
                    scan_sums(v, 0, CW, 3 + 2 * t)
                    chunk_merge(v, t)
                v.drain()
            graph_end(v, n)
            v.wait_ge(ye_in[1], 16)
            add_bias(v, EXPERTS - 1)
            v.drain().then_inc(bias_ok, 1)
            for k in range(2):
                combine(v, slice(k * V_SLOTS // 2, (k + 1) * V_SLOTS // 2), OWN, k)
                v.drain().then_inc(done_dve, 1)


_INS = {'x': 'x', 'cls_tok': 'cls_tok', 'L0_tok_W': 'tok_W', 'L0_tok_b': 'tok_b', 'L0_attn_Win': 'Win',
        'L0_attn_bin_': 'bin_', 'L0_attn_Wout': 'Wout', 'L0_attn_bout': 'bout', 'L0_attn_A': 'A',
        'L0_attn_Bm': 'Bm', 'L0_attn_Cm': 'Cm', 'L0_attn_Dm': 'Dm', 'L0_ffn_W_gat': 'W_gat',
        'L0_ffn_att_src': 'att_src', 'L0_ffn_att_dst': 'att_dst', 'L0_ffn_b_gat': 'b_gat',
        'L0_ffn_ln_gamma': 'ln_gamma', 'L0_ffn_ln_beta': 'ln_beta', 'L0_ffn_W1': 'W1', 'L0_ffn_b1': 'b1',
        'L0_ffn_W2': 'W2', 'L0_ffn_b2': 'b2', 'L0_ffn_edge_index': 'edge_index'}


def kernel(**inputs):
    import concourse.bacc as bacc
    from concourse.bass_utils import run_bass_kernel_spmd

    nc = bacc.Bacc("TRN2", target_bir_lowering=False, num_devices=1)
    arrays, args = {}, {}
    for name, short in _INS.items():
        arrays[f"in_{short}"] = np.ascontiguousarray(inputs[name])
        args[short] = f"in_{short}"
    for name, a in constants().items():
        arrays[name] = a
        args[name] = name
    args = {k: nc.dram_tensor(n, arrays[n].shape, mybir.dt.from_np(arrays[n].dtype), kind="ExternalInput").ap()
            for k, n in args.items()}
    out = nc.dram_tensor("out_h", (IMAGES, TOK, H), F32, kind="ExternalOutput").ap()
    tower(nc, **args, out=out)
    r = run_bass_kernel_spmd(nc, [arrays], core_ids=[0])
    return r.results[0]["out_h"]
```
